# Optimizing a Trainium2 kernel written in Bass

```python
import numpy as np
import jax
import jax.numpy as jnp

def _softmax(x, axis=-1):
    return jax.nn.softmax(x, axis=axis)

def _gelu(x):
    return jax.nn.gelu(x, approximate=True)

def _silu(x):
    return jax.nn.silu(x)

def _sigmoid(x):
    return jax.nn.sigmoid(x)

def _layernorm(x, axis=-1, eps=1e-05):
    m = jnp.mean(x, axis=axis, keepdims=True)
    v = jnp.var(x, axis=axis, keepdims=True)
    return (x - m) / jnp.sqrt(v + eps)

def _scatter_add(tgt, idx, src, axis=0):
    return tgt.at[idx].add(src)

def _segment_sum(src, seg, n):
    return jax.ops.segment_sum(src, seg, n)
kernel_name = 'mk_sandwich_d4_jaxref_r8_e9b624'

def setup_inputs(seed: int=0):
    np.random.seed(seed)
    _w = jnp.asarray

    def _L0_attn_setup():
        import jax, jax.numpy as jnp
        import numpy as np
        import math
        B, S, DM = (1, 256, 512)
        H, HKV, HD = (32, 8, 128)
        EPS = 1e-06
        NEG_INF = -1e+30

        def _alibi_slopes(n_heads: int) -> np.ndarray:
            start = 2 ** (-2 ** (-(math.log2(n_heads) - 3)))
            return np.array([start * start ** i for i in range(n_heads)], dtype=np.float32)

        def _rmsnorm(t, w):
            tf = t.astype(jnp.float32)
            inv = jax.lax.rsqrt(jnp.mean(tf * tf, axis=-1, keepdims=True) + EPS)
            return (tf * inv * w).astype(t.dtype)
        key = jax.random.key(seed)
        ks = jax.random.split(key, 5)
        std = 0.02
        return {'x': jax.random.normal(ks[0], (B, S, DM), dtype=jnp.float32), 'Wq': jax.random.normal(ks[1], (H * HD, DM), dtype=jnp.float32) * std, 'Wk': jax.random.normal(ks[2], (HKV * HD, DM), dtype=jnp.float32) * std, 'Wv': jax.random.normal(ks[3], (HKV * HD, DM), dtype=jnp.float32) * std, 'Wo': jax.random.normal(ks[4], (H * HD, DM), dtype=jnp.float32).T * (std / math.sqrt(2 * 32)), 'q_norm_w': jnp.ones((HD,), dtype=jnp.float32), 'k_norm_w': jnp.ones((HD,), dtype=jnp.float32)}
    _L0_attn_in = _L0_attn_setup()

    def _L0_ffn_setup():
        import jax, jax.numpy as jnp
        import numpy as np
        H = 512
        I = 1376
        B, S = (4, 256)

        def _dequant(wq, scale):
            return wq.astype(jnp.float32) * scale[:, None]
        key = jax.random.key(seed)
        ks = jax.random.split(key, 7)
        x = jax.random.normal(ks[0], (B, S, H), dtype=jnp.float32)
        gate_wq = jax.random.randint(ks[1], (I, H), -127, 128, dtype=jnp.int32)
        up_wq = jax.random.randint(ks[2], (I, H), -127, 128, dtype=jnp.int32)
        down_wq = jax.random.randint(ks[3], (H, I), -127, 128, dtype=jnp.int32)
        gate_scale = jax.random.uniform(ks[4], (I,), dtype=jnp.float32) * 0.01 + 0.0001
        up_scale = jax.random.uniform(ks[5], (I,), dtype=jnp.float32) * 0.01 + 0.0001
        down_scale = jax.random.uniform(ks[6], (H,), dtype=jnp.float32) * 0.01 + 0.0001
        return {'x': x, 'gate_wq': gate_wq, 'gate_scale': gate_scale, 'up_wq': up_wq, 'up_scale': up_scale, 'down_wq': down_wq, 'down_scale': down_scale}
    _L0_ffn_in = _L0_ffn_setup()

    def _L1_attn_setup():
        import jax, jax.numpy as jnp
        import numpy as np
        import math
        D_MODEL = 256
        D_STATE = 16
        EXPAND = 2
        D_INNER = D_MODEL * EXPAND
        DT_RANK = math.ceil(D_MODEL / 16)
        BATCH, SEQ_LEN = (2, 64)
        key = jax.random.key(seed)
        ks = jax.random.split(key, 6)
        x = jax.random.normal(ks[0], (BATCH, SEQ_LEN, D_INNER), dtype=jnp.float32)
        A_log = jnp.log(jax.random.uniform(ks[1], (D_INNER, D_STATE), minval=0.5, maxval=16.0, dtype=jnp.float32))
        D = jnp.ones((D_INNER,), dtype=jnp.float32)
        x_proj_w = 0.02 * jax.random.normal(ks[2], (DT_RANK + 2 * D_STATE, D_INNER), dtype=jnp.float32)
        dt_init_std = DT_RANK ** (-0.5)
        dt_proj_w = jax.random.uniform(ks[3], (D_INNER, DT_RANK), minval=-dt_init_std, maxval=dt_init_std, dtype=jnp.float32)
        dt = jnp.exp(jax.random.uniform(ks[4], (D_INNER,), dtype=jnp.float32) * (math.log(0.1) - math.log(0.001)) + math.log(0.001))
        dt = jnp.clip(dt, 0.0001, None)
        dt_proj_b = dt + jnp.log(-jnp.expm1(-dt))
        return {'x': x, 'A_log': A_log, 'D': D, 'x_proj_w': x_proj_w, 'dt_proj_w': dt_proj_w, 'dt_proj_b': dt_proj_b}
    _L1_attn_in = _L1_attn_setup()

    def _L1_ffn_setup():
        import jax, jax.numpy as jnp
        import numpy as np
        B_L, B_H = (4, 8)
        LIN_SLOPE, LIN_INTER, EST_T = (1.0, 0.0, 64.0)
        BATCH, SEQ, IN_F, OUT_F = (4, 256, 512, 512)
        MAX_BITS = 8

        def dequant_kbit(qweight, lut, bit):
            O, I32 = (qweight.shape[1], qweight.shape[2])
            shifts = jnp.arange(32, dtype=jnp.int32)
            idx = jnp.zeros((O, I32 * 32), dtype=jnp.int32)
            for p in range(bit):
                bits = (qweight[p][:, :, None] >> shifts & 1).reshape(O, I32 * 32)
                idx = idx | bits << p
            return jnp.take_along_axis(lut, idx, axis=1)
        key = jax.random.key(seed)
        k = jax.random.split(key, 5)
        x = jax.random.normal(k[0], (BATCH, SEQ, IN_F), dtype=jnp.float32)
        qweight = jax.random.randint(k[1], (MAX_BITS, OUT_F, IN_F // 32), 0, 2147483647, dtype=jnp.int32)
        lut4 = jax.random.normal(k[2], (OUT_F, 2 ** B_L), dtype=jnp.float32) * 0.02
        lut8 = jax.random.normal(k[3], (OUT_F, 2 ** B_H), dtype=jnp.float32) * 0.02
        bias = jax.random.normal(k[4], (OUT_F,), dtype=jnp.float32) * 0.01
        return {'x': x, 'qweight': qweight, 'lut4': lut4, 'lut8': lut8, 'bias': bias}
    _L1_ffn_in = _L1_ffn_setup()

    def _L2_attn_setup():
        import jax, jax.numpy as jnp
        import numpy as np
        HIDDEN = 512
        NUM_HEADS = 32
        HEAD_DIM = HIDDEN // NUM_HEADS
        THRESH = 0.001
        key = jax.random.key(seed)
        ks = jax.random.split(key, 9)
        w_std = 0.02
        x = jax.random.normal(ks[0], (4, 512, HIDDEN), dtype=jnp.float32)
        Wq = jax.random.normal(ks[1], (HIDDEN, HIDDEN), dtype=jnp.float32) * w_std
        bq = jax.random.normal(ks[2], (HIDDEN,), dtype=jnp.float32) * w_std
        Wk = jax.random.normal(ks[3], (HIDDEN, HIDDEN), dtype=jnp.float32) * w_std
        bk = jax.random.normal(ks[4], (HIDDEN,), dtype=jnp.float32) * w_std
        Wv = jax.random.normal(ks[5], (HIDDEN, HIDDEN), dtype=jnp.float32) * w_std
        bv = jax.random.normal(ks[6], (HIDDEN,), dtype=jnp.float32) * w_std
        Wo = jax.random.normal(ks[7], (HIDDEN, HIDDEN), dtype=jnp.float32) * w_std
        bo = jax.random.normal(ks[8], (HIDDEN,), dtype=jnp.float32) * w_std
        return {'x': x, 'Wq': Wq, 'bq': bq, 'Wk': Wk, 'bk': bk, 'Wv': Wv, 'bv': bv, 'Wo': Wo, 'bo': bo}
    _L2_attn_in = _L2_attn_setup()

    def _L2_ffn_setup():
        import jax, jax.numpy as jnp
        import numpy as np
        SCALE = 16.0 / 8.0
        key = jax.random.key(seed)
        ks = jax.random.split(key, 6)
        B, S, IN, OUT, E, R = (4, 256, 512, 512, 4, 8)
        x = jax.random.normal(ks[0], (B, S, IN), dtype=jnp.float32)
        W = jax.random.normal(ks[1], (OUT, IN), dtype=jnp.float32) * 0.02
        b = jax.random.normal(ks[2], (OUT,), dtype=jnp.float32) * 0.02
        A = jax.random.normal(ks[3], (E, R, IN), dtype=jnp.float32) * 0.02
        Bm = jax.random.normal(ks[4], (E, OUT, R), dtype=jnp.float32) * 0.02
        Wr = jax.random.normal(ks[5], (E, IN), dtype=jnp.float32) * 0.02
        return {'x': x, 'W': W, 'b': b, 'A': A, 'Bm': Bm, 'Wr': Wr}
    _L2_ffn_in = _L2_ffn_setup()

    def _L3_attn_setup():
        import jax, jax.numpy as jnp
        import numpy as np
        B, S, D = (1, 256, 512)
        H = 32
        QL = 192
        KVL = 64
        DN = 128
        DR = 64
        DV = 128
        BASE = 10000.0
        FACTOR = 40.0
        BFAST, BSLOW = (32.0, 1.0)
        OLD_CTX = 4096.0
        MSCALE = 1.0

        def _yarn_inv_freq():
            freqs = 1.0 / BASE ** (jnp.arange(0, DR, 2, dtype=jnp.float32) / DR)
            wavelengths = 2.0 * jnp.pi / freqs
            ramp = jnp.clip((wavelengths / OLD_CTX - BSLOW) / (BFAST - BSLOW), 0.0, 1.0)
            scale = 1.0 - ramp + ramp * FACTOR
            return (freqs / scale, MSCALE)

        def _apply_rope(x, inv_freq, mscale):
            seq = x.shape[-2]
            pos = jnp.arange(seq, dtype=jnp.float32)
            f = jnp.concatenate([pos[:, None] * inv_freq[None, :]] * 2, axis=-1)
            cos = jnp.cos(f) * mscale
            sin = jnp.sin(f) * mscale
            half = DR // 2
            x1, x2 = (x[..., :half], x[..., half:])
            c1, c2 = (cos[:, :half], cos[:, half:])
            s2 = sin[:, half:]
            return jnp.concatenate([x1 * c1 - x2 * s2, x1 * s2 + x2 * c2], axis=-1)
        key = jax.random.key(seed)
        ks = jax.random.split(key, 10)

        def glorot(k, shape):
            lim = np.sqrt(6.0 / (shape[0] + shape[1])).astype(np.float32)
            return jax.random.uniform(k, shape, jnp.float32, -lim, lim)
        return {'hidden_states': jax.random.normal(ks[0], (B, S, D), jnp.float32), 'w_q_down': glorot(ks[1], (D, QL)), 'w_q_up_nope': glorot(ks[2], (QL, H * DN)), 'w_q_up_rope': glorot(ks[3], (QL, H * DR)), 'w_kv_down': glorot(ks[4], (D, KVL)), 'w_k_rope': glorot(ks[5], (D, DR)), 'w_uk': glorot(ks[6], (H * DN, KVL)), 'w_uv': glorot(ks[7], (H * DV, KVL)), 'w_out': glorot(ks[8], (H * DV, D))}
    _L3_attn_in = _L3_attn_setup()

    def _L3_ffn_setup():
        import jax, jax.numpy as jnp
        import numpy as np
        HIDDEN = 512
        MOE_INTER = 128
        SHARED_INTER = 512
        NUM_EXPERTS = 16
        TOP_K = 2

        def _moe_forward(x, gate_w, w_gate_up, w_down, shared_w_gate_up, shared_w_down):
            orig_shape = x.shape
            x2 = x.reshape(-1, orig_shape[-1])
            gu_s = x2 @ shared_w_gate_up.T
            g_s, u_s = jnp.split(gu_s, 2, axis=-1)
            shared_out = jax.nn.silu(g_s) * u_s @ shared_w_down.T
            logits = x2 @ gate_w.T
            probs = jax.nn.softmax(logits, axis=-1)
            topk_vals, topk_idx = jax.lax.top_k(probs, TOP_K)
            topk_vals = topk_vals / jnp.sum(topk_vals, axis=-1, keepdims=True)
            combine = jnp.sum(jax.nn.one_hot(topk_idx, NUM_EXPERTS, dtype=x2.dtype) * topk_vals[..., None], axis=1)
            gu = jnp.einsum('th,eih->eti', x2, w_gate_up)
            g, u = jnp.split(gu, 2, axis=-1)
            act = jax.nn.silu(g) * u
            out_e = jnp.einsum('eti,ehi->eth', act, w_down)
            moe_out = jnp.einsum('eth,te->th', out_e, combine)
            return (moe_out + shared_out).reshape(orig_shape)
        key = jax.random.key(seed)
        ks = jax.random.split(key, 6)
        s = 0.02
        hidden_states = jax.random.normal(ks[0], (2, 256, HIDDEN), dtype=jnp.float32)
        gate_w = jax.random.normal(ks[1], (NUM_EXPERTS, HIDDEN), dtype=jnp.float32) * s
        w_gate_up = jax.random.normal(ks[2], (NUM_EXPERTS, 2 * MOE_INTER, HIDDEN), dtype=jnp.float32) * s
        w_down = jax.random.normal(ks[3], (NUM_EXPERTS, HIDDEN, MOE_INTER), dtype=jnp.float32) * s
        shared_w_gate_up = jax.random.normal(ks[4], (2 * SHARED_INTER, HIDDEN), dtype=jnp.float32) * s
        shared_w_down = jax.random.normal(ks[5], (HIDDEN, SHARED_INTER), dtype=jnp.float32) * s
        return {'hidden_states': hidden_states, 'gate_w': gate_w, 'w_gate_up': w_gate_up, 'w_down': w_down, 'shared_w_gate_up': shared_w_gate_up, 'shared_w_down': shared_w_down}
    _L3_ffn_in = _L3_ffn_setup()
    _d = {'L0_attn_x': _L0_attn_in['x'], 'L0_attn_Wq': _L0_attn_in['Wq'], 'L0_attn_Wk': _L0_attn_in['Wk'], 'L0_attn_Wv': _L0_attn_in['Wv'], 'L0_attn_Wo': _L0_attn_in['Wo'], 'L0_attn_q_norm_w': _L0_attn_in['q_norm_w'], 'L0_attn_k_norm_w': _L0_attn_in['k_norm_w'], 'L0_ffn_gate_wq': _L0_ffn_in['gate_wq'], 'L0_ffn_gate_scale': _L0_ffn_in['gate_scale'], 'L0_ffn_up_wq': _L0_ffn_in['up_wq'], 'L0_ffn_up_scale': _L0_ffn_in['up_scale'], 'L0_ffn_down_wq': _L0_ffn_in['down_wq'], 'L0_ffn_down_scale': _L0_ffn_in['down_scale'], 'L1_attn_A_log': _L1_attn_in['A_log'], 'L1_attn_D': _L1_attn_in['D'], 'L1_attn_x_proj_w': _L1_attn_in['x_proj_w'], 'L1_attn_dt_proj_w': _L1_attn_in['dt_proj_w'], 'L1_attn_dt_proj_b': _L1_attn_in['dt_proj_b'], 'L1_ffn_qweight': _L1_ffn_in['qweight'], 'L1_ffn_lut4': _L1_ffn_in['lut4'], 'L1_ffn_lut8': _L1_ffn_in['lut8'], 'L1_ffn_bias': _L1_ffn_in['bias'], 'L2_attn_Wq': _L2_attn_in['Wq'], 'L2_attn_bq': _L2_attn_in['bq'], 'L2_attn_Wk': _L2_attn_in['Wk'], 'L2_attn_bk': _L2_attn_in['bk'], 'L2_attn_Wv': _L2_attn_in['Wv'], 'L2_attn_bv': _L2_attn_in['bv'], 'L2_attn_Wo': _L2_attn_in['Wo'], 'L2_attn_bo': _L2_attn_in['bo'], 'L2_ffn_W': _L2_ffn_in['W'], 'L2_ffn_b': _L2_ffn_in['b'], 'L2_ffn_A': _L2_ffn_in['A'], 'L2_ffn_Bm': _L2_ffn_in['Bm'], 'L2_ffn_Wr': _L2_ffn_in['Wr'], 'L3_attn_w_q_down': _L3_attn_in['w_q_down'], 'L3_attn_w_q_up_nope': _L3_attn_in['w_q_up_nope'], 'L3_attn_w_q_up_rope': _L3_attn_in['w_q_up_rope'], 'L3_attn_w_kv_down': _L3_attn_in['w_kv_down'], 'L3_attn_w_k_rope': _L3_attn_in['w_k_rope'], 'L3_attn_w_uk': _L3_attn_in['w_uk'], 'L3_attn_w_uv': _L3_attn_in['w_uv'], 'L3_attn_w_out': _L3_attn_in['w_out'], 'L3_ffn_gate_w': _L3_ffn_in['gate_w'], 'L3_ffn_w_gate_up': _L3_ffn_in['w_gate_up'], 'L3_ffn_w_down': _L3_ffn_in['w_down'], 'L3_ffn_shared_w_gate_up': _L3_ffn_in['shared_w_gate_up'], 'L3_ffn_shared_w_down': _L3_ffn_in['shared_w_down']}
    _x0 = _d['L0_attn_x']
    _d['L0_attn_x'] = jax.random.normal(jax.random.fold_in(jax.random.key(seed), 1), (4, 256, 512), dtype=_x0.dtype)
    del _x0
    return _d

def reference(L0_attn_x, L0_attn_Wq, L0_attn_Wk, L0_attn_Wv, L0_attn_Wo, L0_attn_q_norm_w, L0_attn_k_norm_w, L0_ffn_gate_wq, L0_ffn_gate_scale, L0_ffn_up_wq, L0_ffn_up_scale, L0_ffn_down_wq, L0_ffn_down_scale, L1_attn_A_log, L1_attn_D, L1_attn_x_proj_w, L1_attn_dt_proj_w, L1_attn_dt_proj_b, L1_ffn_qweight, L1_ffn_lut4, L1_ffn_lut8, L1_ffn_bias, L2_attn_Wq, L2_attn_bq, L2_attn_Wk, L2_attn_bk, L2_attn_Wv, L2_attn_bv, L2_attn_Wo, L2_attn_bo, L2_ffn_W, L2_ffn_b, L2_ffn_A, L2_ffn_Bm, L2_ffn_Wr, L3_attn_w_q_down, L3_attn_w_q_up_nope, L3_attn_w_q_up_rope, L3_attn_w_kv_down, L3_attn_w_k_rope, L3_attn_w_uk, L3_attn_w_uv, L3_attn_w_out, L3_ffn_gate_w, L3_ffn_w_gate_up, L3_ffn_w_down, L3_ffn_shared_w_gate_up, L3_ffn_shared_w_down):

    def _L0_attn_ref(x, Wq, Wk, Wv, Wo, q_norm_w, k_norm_w):
        import jax, jax.numpy as jnp
        import numpy as np
        import math
        B, S, DM = (1, 256, 512)
        H, HKV, HD = (32, 8, 128)
        EPS = 1e-06
        NEG_INF = -1e+30

        def _alibi_slopes(n_heads: int) -> np.ndarray:
            start = 2 ** (-2 ** (-(math.log2(n_heads) - 3)))
            return np.array([start * start ** i for i in range(n_heads)], dtype=np.float32)

        def _rmsnorm(t, w):
            tf = t.astype(jnp.float32)
            inv = jax.lax.rsqrt(jnp.mean(tf * tf, axis=-1, keepdims=True) + EPS)
            return (tf * inv * w).astype(t.dtype)
        b, s, _ = x.shape
        G = H // HKV
        q = (x @ Wq.T).reshape(b, s, H, HD).transpose(0, 2, 1, 3)
        k = (x @ Wk.T).reshape(b, s, HKV, HD).transpose(0, 2, 1, 3)
        v = (x @ Wv.T).reshape(b, s, HKV, HD).transpose(0, 2, 1, 3)
        q = _rmsnorm(q, q_norm_w)
        k = _rmsnorm(k, k_norm_w)
        qg = q.reshape(b, HKV, G, s, HD)
        scores = jnp.einsum('bkgqd,bksd->bkgqs', qg, k) / math.sqrt(HD)
        slopes = jnp.asarray(_alibi_slopes(H)).reshape(HKV, G)
        pos = jnp.arange(s, dtype=jnp.float32)
        rel = pos[None, :] - pos[:, None]
        bias = jnp.where(rel > 0, NEG_INF, slopes[:, :, None, None] * rel)
        attn = jax.nn.softmax(scores + bias[None], axis=-1)
        out = jnp.einsum('bkgqs,bksd->bkgqd', attn, v)
        out = out.reshape(b, H, s, HD).transpose(0, 2, 1, 3).reshape(b, s, H * HD)
        return out @ Wo.T

    def _L0_ffn_ref(x, gate_wq, gate_scale, up_wq, up_scale, down_wq, down_scale):
        import jax, jax.numpy as jnp
        import numpy as np
        H = 512
        I = 1376
        B, S = (4, 256)

        def _dequant(wq, scale):
            return wq.astype(jnp.float32) * scale[:, None]
        gate_w = _dequant(gate_wq, gate_scale)
        up_w = _dequant(up_wq, up_scale)
        down_w = _dequant(down_wq, down_scale)
        g = jnp.einsum('bsh,ih->bsi', x, gate_w)
        u = jnp.einsum('bsh,ih->bsi', x, up_w)
        return jnp.einsum('bsi,hi->bsh', g * u, down_w)

    def _L1_attn_ref(x, A_log, D, x_proj_w, dt_proj_w, dt_proj_b):
        import jax, jax.numpy as jnp
        import numpy as np
        import math
        D_MODEL = 256
        D_STATE = 16
        EXPAND = 2
        D_INNER = D_MODEL * EXPAND
        DT_RANK = math.ceil(D_MODEL / 16)
        BATCH, SEQ_LEN = (2, 64)
        A = -jnp.exp(A_log)
        xp = jnp.einsum('bld,rd->blr', x, x_proj_w)
        dt_in = xp[..., :DT_RANK]
        B = xp[..., DT_RANK:DT_RANK + D_STATE]
        C = xp[..., DT_RANK + D_STATE:]
        dt = jax.nn.softplus(jnp.einsum('blr,dr->bld', dt_in, dt_proj_w) + dt_proj_b)
        dA = jnp.exp(dt[..., None] * A)
        dBx = dt[..., None] * B[:, :, None, :] * x[..., None]

        def step(h, inp):
            dA_t, dBx_t, C_t = inp
            h = dA_t * h + dBx_t
            y = jnp.einsum('bdn,bn->bd', h, C_t)
            return (h, y)
        h0 = jnp.zeros((x.shape[0], D_INNER, D_STATE), dtype=x.dtype)
        _, ys = jax.lax.scan(step, h0, (jnp.moveaxis(dA, 1, 0), jnp.moveaxis(dBx, 1, 0), jnp.moveaxis(C, 1, 0)))
        y = jnp.moveaxis(ys, 0, 1) + D * x
        return y

    def _L1_ffn_ref(x, qweight, lut4, lut8, bias):
        import jax, jax.numpy as jnp
        import numpy as np
        B_L, B_H = (4, 8)
        LIN_SLOPE, LIN_INTER, EST_T = (1.0, 0.0, 64.0)
        BATCH, SEQ, IN_F, OUT_F = (4, 256, 512, 512)
        MAX_BITS = 8

        def dequant_kbit(qweight, lut, bit):
            O, I32 = (qweight.shape[1], qweight.shape[2])
            shifts = jnp.arange(32, dtype=jnp.int32)
            idx = jnp.zeros((O, I32 * 32), dtype=jnp.int32)
            for p in range(bit):
                bits = (qweight[p][:, :, None] >> shifts & 1).reshape(O, I32 * 32)
                idx = idx | bits << p
            return jnp.take_along_axis(lut, idx, axis=1)
        e = jnp.linalg.norm(x, axis=-1) * LIN_SLOPE + LIN_INTER
        mask = e > EST_T
        w_l = dequant_kbit(qweight, lut4, B_L)
        w_h = dequant_kbit(qweight, lut8, B_H)
        y_l = jnp.einsum('bsi,oi->bso', x, w_l)
        y_h = jnp.einsum('bsi,oi->bso', x, w_h)
        y = jnp.where(mask[..., None], y_h, y_l) + bias
        return y

    def _L2_attn_ref(x, Wq, bq, Wk, bk, Wv, bv, Wo, bo):
        import jax, jax.numpy as jnp
        import numpy as np
        HIDDEN = 512
        NUM_HEADS = 32
        HEAD_DIM = HIDDEN // NUM_HEADS
        THRESH = 0.001
        B, S, Hd = x.shape
        H, D = (NUM_HEADS, HEAD_DIM)
        q = (x @ Wq.T + bq).reshape(B, S, H, D)
        k = (x @ Wk.T + bk).reshape(B, S, H, D)
        v = (x @ Wv.T + bv).reshape(B, S, H, D)
        inv_sqrt_d = np.float32(1.0 / np.sqrt(D))
        scores = jnp.einsum('bshd,bsgd->bshg', q, k) * inv_sqrt_d
        scores = jnp.where(scores > THRESH, scores, -jnp.inf)
        attn = jax.nn.softmax(scores, axis=-1)
        out = jnp.einsum('bshg,bsgd->bshd', attn, v).reshape(B, S, Hd)
        return out @ Wo.T + bo

    def _L2_ffn_ref(x, W, b, A, Bm, Wr):
        import jax, jax.numpy as jnp
        import numpy as np
        SCALE = 16.0 / 8.0
        base_out = jnp.einsum('bsi,oi->bso', x, W) + b
        gates = jax.nn.softmax(jnp.einsum('bsi,ei->bse', x, Wr), axis=-1)
        proj_r = jnp.einsum('bsi,eri->bser', x, A)
        lora_out = jnp.einsum('bser,eor->bseo', proj_r, Bm)
        lora_mix = jnp.einsum('bse,bseo->bso', gates * SCALE, lora_out)
        return base_out + lora_mix

    def _L3_attn_ref(hidden_states, w_q_down, w_q_up_nope, w_q_up_rope, w_kv_down, w_k_rope, w_uk, w_uv, w_out):
        import jax, jax.numpy as jnp
        import numpy as np
        B, S, D = (1, 256, 512)
        H = 32
        QL = 192
        KVL = 64
        DN = 128
        DR = 64
        DV = 128
        BASE = 10000.0
        FACTOR = 40.0
        BFAST, BSLOW = (32.0, 1.0)
        OLD_CTX = 4096.0
        MSCALE = 1.0

        def _yarn_inv_freq():
            freqs = 1.0 / BASE ** (jnp.arange(0, DR, 2, dtype=jnp.float32) / DR)
            wavelengths = 2.0 * jnp.pi / freqs
            ramp = jnp.clip((wavelengths / OLD_CTX - BSLOW) / (BFAST - BSLOW), 0.0, 1.0)
            scale = 1.0 - ramp + ramp * FACTOR
            return (freqs / scale, MSCALE)

        def _apply_rope(x, inv_freq, mscale):
            seq = x.shape[-2]
            pos = jnp.arange(seq, dtype=jnp.float32)
            f = jnp.concatenate([pos[:, None] * inv_freq[None, :]] * 2, axis=-1)
            cos = jnp.cos(f) * mscale
            sin = jnp.sin(f) * mscale
            half = DR // 2
            x1, x2 = (x[..., :half], x[..., half:])
            c1, c2 = (cos[:, :half], cos[:, half:])
            s2 = sin[:, half:]
            return jnp.concatenate([x1 * c1 - x2 * s2, x1 * s2 + x2 * c2], axis=-1)
        b, s, _ = hidden_states.shape
        c_q = hidden_states @ w_q_down
        q_nope = (c_q @ w_q_up_nope).reshape(b, s, H, DN).transpose(0, 2, 1, 3)
        q_rope = (c_q @ w_q_up_rope).reshape(b, s, H, DR).transpose(0, 2, 1, 3)
        c_kv = hidden_states @ w_kv_down
        k_rope = (hidden_states @ w_k_rope)[:, None]
        inv_freq, mscale = _yarn_inv_freq()
        q_rope = _apply_rope(q_rope, inv_freq, mscale)
        k_rope = _apply_rope(k_rope, inv_freq, mscale)
        wuk = w_uk.reshape(H, DN, KVL)
        q_lat = jnp.einsum('bhsd,hdr->bhsr', q_nope, wuk)
        scores = jnp.einsum('bhsr,btr->bhst', q_lat, c_kv) + jnp.einsum('bhsd,btd->bhst', q_rope, k_rope[:, 0])
        scores = scores / jnp.sqrt(jnp.float32(DN + DR))
        causal = jnp.tril(jnp.ones((s, s), dtype=bool))
        scores = jnp.where(causal, scores, jnp.finfo(scores.dtype).min)
        probs = jax.nn.softmax(scores, axis=-1)
        out_lat = jnp.einsum('bhst,btr->bhsr', probs, c_kv)
        wuv = w_uv.reshape(H, DV, KVL)
        out = jnp.einsum('bhsr,hdr->bhsd', out_lat, wuv)
        out = out.transpose(0, 2, 1, 3).reshape(b, s, H * DV)
        return out @ w_out

    def _L3_ffn_ref(hidden_states, gate_w, w_gate_up, w_down, shared_w_gate_up, shared_w_down):
        import jax, jax.numpy as jnp
        import numpy as np
        HIDDEN = 512
        MOE_INTER = 128
        SHARED_INTER = 512
        NUM_EXPERTS = 16
        TOP_K = 2

        def _moe_forward(x, gate_w, w_gate_up, w_down, shared_w_gate_up, shared_w_down):
            orig_shape = x.shape
            x2 = x.reshape(-1, orig_shape[-1])
            gu_s = x2 @ shared_w_gate_up.T
            g_s, u_s = jnp.split(gu_s, 2, axis=-1)
            shared_out = jax.nn.silu(g_s) * u_s @ shared_w_down.T
            logits = x2 @ gate_w.T
            probs = jax.nn.softmax(logits, axis=-1)
            topk_vals, topk_idx = jax.lax.top_k(probs, TOP_K)
            topk_vals = topk_vals / jnp.sum(topk_vals, axis=-1, keepdims=True)
            combine = jnp.sum(jax.nn.one_hot(topk_idx, NUM_EXPERTS, dtype=x2.dtype) * topk_vals[..., None], axis=1)
            gu = jnp.einsum('th,eih->eti', x2, w_gate_up)
            g, u = jnp.split(gu, 2, axis=-1)
            act = jax.nn.silu(g) * u
            out_e = jnp.einsum('eti,ehi->eth', act, w_down)
            moe_out = jnp.einsum('eth,te->th', out_e, combine)
            return (moe_out + shared_out).reshape(orig_shape)
        return _moe_forward(hidden_states, gate_w, w_gate_up, w_down, shared_w_gate_up, shared_w_down)
    x = L0_attn_x
    x = x + _layernorm(_L0_attn_ref(_layernorm(x, axis=-1), L0_attn_Wq, L0_attn_Wk, L0_attn_Wv, L0_attn_Wo, L0_attn_q_norm_w, L0_attn_k_norm_w), axis=-1)
    x = x + _layernorm(_L0_ffn_ref(_layernorm(x, axis=-1), L0_ffn_gate_wq, L0_ffn_gate_scale, L0_ffn_up_wq, L0_ffn_up_scale, L0_ffn_down_wq, L0_ffn_down_scale), axis=-1)
    x = x + _layernorm(_L1_attn_ref(_layernorm(x, axis=-1), L1_attn_A_log, L1_attn_D, L1_attn_x_proj_w, L1_attn_dt_proj_w, L1_attn_dt_proj_b), axis=-1)
    x = x + _layernorm(_L1_ffn_ref(_layernorm(x, axis=-1), L1_ffn_qweight, L1_ffn_lut4, L1_ffn_lut8, L1_ffn_bias), axis=-1)
    x = x + _layernorm(_L2_attn_ref(_layernorm(x, axis=-1), L2_attn_Wq, L2_attn_bq, L2_attn_Wk, L2_attn_bk, L2_attn_Wv, L2_attn_bv, L2_attn_Wo, L2_attn_bo), axis=-1)
    x = x + _layernorm(_L2_ffn_ref(_layernorm(x, axis=-1), L2_ffn_W, L2_ffn_b, L2_ffn_A, L2_ffn_Bm, L2_ffn_Wr), axis=-1)
    x = x + _layernorm(_L3_attn_ref(_layernorm(x, axis=-1), L3_attn_w_q_down, L3_attn_w_q_up_nope, L3_attn_w_q_up_rope, L3_attn_w_kv_down, L3_attn_w_k_rope, L3_attn_w_uk, L3_attn_w_uv, L3_attn_w_out), axis=-1)
    x = x + _layernorm(_L3_ffn_ref(_layernorm(x, axis=-1), L3_ffn_gate_w, L3_ffn_w_gate_up, L3_ffn_w_down, L3_ffn_shared_w_gate_up, L3_ffn_shared_w_down), axis=-1)
    return x

_drawn_inputs = setup_inputs


def setup_inputs(seed=0):
    import zlib

    import numpy as np

    out = dict(_drawn_inputs(seed))
    spreads = {'L0_attn_q_norm_w': (1.0, 0.2), 'L0_attn_k_norm_w': (1.0, 0.2), 'L1_attn_D': (1.0, 0.2)}
    factors = {'L1_attn_dt_proj_w': 3.334,
     'L2_ffn_Wr': 5.759,
     'L3_attn_w_q_up_nope': 2.771,
     'L3_attn_w_uk': 2.822,
     'L2_attn_bv': 2.668}
    for name, (base, spread) in spreads.items():
        noise = np.random.default_rng([zlib.crc32(name.encode()), seed]).standard_normal(out[name].shape)
        drawn = base * np.exp(spread * noise) if base else spread * noise
        out[name] = jnp.asarray(drawn.astype(out[name].dtype))
    for name, factor in factors.items():
        out[name] = (out[name] * factor).astype(out[name].dtype)
    return out
```

```python
import math
from contextlib import ExitStack

import numpy as np

import concourse.bass as bass
from concourse import mybir

FP32 = mybir.dt.float32
FP32R = mybir.dt.float32r
I32 = mybir.dt.int32
ALU = mybir.AluOpType
ACT = mybir.ActivationFunctionType
AX = mybir.AxisListType.X

P = 128
TOKENS, C = 1024, 512
BATCHES, SEQ = 4, 256
NT = TOKENS // P
KC = C // P
HALF = 512
NH2 = TOKENS // HALF
LN_EPS = 1e-5
LAYERS = 8


class Chip:

    def __init__(self, nc, ctx, dram):
        self.nc, self.ctx, self.dram = nc, ctx, dram
        self.bank = [ctx.enter_context(nc.psum_tensor(f"bank{i}", [P, 512], FP32)) for i in range(8)]
        self.branch = ctx.enter_context(nc.sbuf_tensor("branch", [P, NT, C], FP32))
        self.x_hi = ctx.enter_context(nc.sbuf_tensor("x_hi", [P, KC, TOKENS], FP32R))
        self.x_lo = ctx.enter_context(nc.sbuf_tensor("x_lo", [P, KC, TOKENS], FP32R))
        self.ident = ctx.enter_context(nc.sbuf_tensor("ident", [P, P], FP32))
        self.norms = 0
        self.norm_ticks = 0
        self.x_loaded = [self.sem(f"x_loaded{t}") for t in range(NT)]
        self.spent = []
        self.norm_sems = {n: self.sem("norm_" + n) for n in (
            "loaded", "branch_stats", "branch_dev", "stream_stats", "stream_dev", "tile_ready",
            "transposed", "stored", "dve", "copied", "bias")}

    def place_stream(self):
        self.stream = self.ctx.enter_context(self.nc.sbuf_tensor("stream", [P, NT, C], FP32))

    def sem(self, name):
        return self.ctx.enter_context(self.nc.semaphore(name))

    def layer_sem(self, scope, name):
        self.spent.append(scope.enter_context(self.nc.semaphore(name)))
        return self.spent[-1]


def split_matmul(nc, out, lhs, rhs, start, stop):
    passes = [(0, 0)] + [(0, 1)] * (len(rhs) > 1) + [(1, 0)] * (len(lhs) > 1)
    for n, (i, j) in enumerate(passes):
        last = n == len(passes) - 1
        ins = nc.tensor.matmul(out, lhs[i], rhs[j], start=start and n == 0, stop=stop and last)
    return ins


def add_and_norm(chip):
    nc, s, n = chip.nc, chip.norm_sems, chip.norms
    first, last = n == 0, n == LAST_LAYERS
    chip.norms += 1
    branch, ident, bank = chip.branch, chip.ident, chip.bank
    posts = NT * (n - 1)
    pres = NT * n
    with ExitStack() as ctx:
        def sb(name, shape, dt=FP32):
            return ctx.enter_context(nc.sbuf_tensor(f"norm{n}_{name}", shape, dt))

        stats = sb("stats", [P, NT, 6])
        bmv = sb("branch_mean_var", [P, NT, 2])
        smv = sb("stream_mean_var", [P, NT, 2])
        bdev = sb("branch_dev", [P, NT])
        sdev = sb("stream_dev", [P, NT])
        tmp = sb("normed", [P, NT, C])
        stream = sb("x", [P, NT, C]) if first else chip.stream
        eps = sb("eps", [P, 1])
        block = ctx.enter_context(nc.Block())

        @block.gpsimd
        def _(pool):
            for spent in chip.spent:
                pool.sem_clear(spent)
            chip.spent = []

        @block.sync
        def _(sp):
            if n <= 1:
                for t in range(NT):
                    sp.dma_start(stream[:, t, :], chip.dram["x"][t]).then_inc(chip.x_loaded[t], 16)
            if first:
                sp.dma_start(ident[:], chip.dram["ident"]).then_inc(s["loaded"], 16)
            if last:
                for t in range(NT):
                    sp.wait_ge(s["tile_ready"], pres + t + 1)
                    sp.dma_start(chip.dram["out"][t], stream[:, t, :]).then_inc(s["stored"], 16)
                sp.wait_ge(s["stored"], 16 * NT)

        @block.vector
        def _(dve):
            ticks = [chip.norm_ticks]

            def tick(ins):
                ticks[0] += 1
                ins.then_inc(s["dve"], 1)
                return ticks[0]

            nc.vector.memset(eps[:], LN_EPS).then_inc(s["bias"], 1)
            if not first:
                seen = [tick(nc.vector.bn_stats(stats[:, t, :], branch[:, t, :])) for t in range(NT)]
                for t in range(NT):
                    dve.wait_ge(s["dve"], seen[t])
                    nc.vector.bn_aggr(bmv[:, t, :], stats[:, t, :]).then_inc(s["branch_stats"], 1)
                for t in range(NT):
                    dve.wait_ge(s["branch_dev"], posts + t + 1)
                    seen[t] = tick(nc.vector.reciprocal(bdev[:, t:t + 1], bdev[:, t:t + 1]))
                for t in range(NT):
                    dve.wait_ge(s["dve"], seen[t])
                    seen[t] = tick(nc.vector.tensor_scalar(tmp[:, t, :], branch[:, t, :], bmv[:, t, 0:1],
                                                           bdev[:, t:t + 1], ALU.subtract, ALU.mult))
                for t in range(NT):
                    dve.wait_ge(s["dve"], seen[t])
                    if n == 1:
                        dve.wait_ge(chip.x_loaded[t], 32)
                    ins = nc.vector.tensor_tensor(stream[:, t, :], stream[:, t, :], tmp[:, t, :], ALU.add)
                    if last:
                        ins.then_inc(s["tile_ready"], 1)
                    else:
                        seen[t] = tick(ins)
            if not last:
                for t in range(NT):
                    if first:
                        dve.wait_ge(chip.x_loaded[t], 16)
                    else:
                        dve.wait_ge(s["dve"], seen[t])
                    v = tick(nc.vector.bn_stats(stats[:, t, :], stream[:, t, :]))
                    dve.wait_ge(s["dve"], v)
                    nc.vector.bn_aggr(smv[:, t, :], stats[:, t, :]).then_inc(s["stream_stats"], 1)
                seen = [0] * NT
                for t in range(NT):
                    dve.wait_ge(s["stream_dev"], pres + t + 1)
                    seen[t] = tick(nc.vector.reciprocal(sdev[:, t:t + 1], sdev[:, t:t + 1]))
                for t in range(NT):
                    dve.wait_ge(s["dve"], seen[t])
                    nc.vector.tensor_scalar(tmp[:, t, :], stream[:, t, :], smv[:, t, 0:1], sdev[:, t:t + 1],
                                            ALU.subtract, ALU.mult).then_inc(s["tile_ready"], 1)
                for t in range(NT):
                    dve.wait_ge(s["copied"], pres + t + 1)
                    nc.vector.tensor_tensor(chip.x_lo[:, :, t * P:(t + 1) * P],
                                            bank[t % 8][:].rearrange("p (k m) -> p k m", k=KC),
                                            chip.x_hi[:, :, t * P:(t + 1) * P].bitcast(FP32), ALU.subtract)
            chip.norm_ticks = ticks[0]

        @block.scalar
        def _(act):
            act.wait_ge(s["bias"], n + 1)
            if not first:
                for t in range(NT):
                    act.wait_ge(s["branch_stats"], posts + t + 1)
                    nc.scalar.activation(bdev[:, t:t + 1], bmv[:, t, 1:2], ACT.Sqrt,
                                         bias=eps[:]).then_inc(s["branch_dev"], 1)
            if not last:
                for t in range(NT):
                    act.wait_ge(s["stream_stats"], pres + t + 1)
                    nc.scalar.activation(sdev[:, t:t + 1], smv[:, t, 1:2], ACT.Sqrt,
                                         bias=eps[:]).then_inc(s["stream_dev"], 1)
                for t in range(NT):
                    act.wait_ge(s["transposed"], pres + t + 1)
                    nc.scalar.activation(chip.x_hi[:, :, t * P:(t + 1) * P],
                                         bank[t % 8][:].rearrange("p (k m) -> p k m", k=KC),
                                         ACT.Copy).then_inc(s["copied"], 1)

        @block.tensor
        def _(pe):
            if not last:
                if first:
                    pe.wait_ge(s["loaded"], 16)
                for t in range(NT):
                    pe.wait_ge(s["tile_ready"], pres + t + 1)
                    for k in range(KC):
                        ins = nc.tensor.transpose(bank[t % 8][:, k * P:(k + 1) * P],
                                                  tmp[:, t, k * P:(k + 1) * P], ident[:])
                    ins.then_inc(s["transposed"], 1)


def gqa_attention(chip):
    nc, d, bank = chip.nc, chip.dram, chip.bank
    x_hi, x_lo, branch, ident = chip.x_hi, chip.x_lo, chip.branch, chip.ident
    GROUPS, G, HD = 8, 4, 128
    UNITS = BATCHES * G
    W = P + SEQ
    EPS = 1e-6
    start = 2 ** (-2 ** (-(math.log2(GROUPS * G) - 3)))
    slopes = [start * start ** i for i in range(GROUPS * G)]
    VALS = 3
    AHEAD = 2
    with ExitStack() as ctx:
        def sb(name, shape, dt=FP32):
            return ctx.enter_context(nc.sbuf_tensor(f"gqa_{name}", shape, dt))

        QKV = KC * (G * HD + 2 * HD)
        WO = G * C
        stage = sb("weights", [P, QKV])
        w_hi = sb("w_qkv_hi", [P, QKV], FP32R)
        w_lo = sb("w_qkv_lo", [P, QKV], FP32R)
        wo_hi = sb("wo_hi", [P, WO], FP32R)
        wo_lo = sb("wo_lo", [P, WO], FP32R)
        q_t = sb("q_t", [P, 2, G, TOKENS])
        q_sq = sb("q_sq", [P, HALF])
        q_sq_hi = sb("q_sq_hi", [P, 2, HALF], FP32R)
        q_sq_lo = sb("q_sq_lo", [P, 2, HALF], FP32R)
        pick = sb("one_hot", [P, G * NH2, G * NH2], FP32R)
        ssq_t = sb("ssq_t", [G * NH2, HALF])
        keys = sb("keys", [P, NT, HD])
        vals = sb("vals", [P, VALS, NT, HD])
        k_sq = sb("k_sq", [P, HD])
        k_t = sb("k_t", [P, 2, TOKENS])
        kss = sb("kss", [P, 2, NT])
        kinv = sb("kinv", [P, 2, NT])
        qinv = sb("qinv", [P, 2, NT * G])
        nw = sb("norm_weights", [P, 2])
        kw = sb("key_scale", [P, 1])
        eps = sb("eps", [P, 1])
        rel = sb("relative", [P, W])
        alibi = sb("alibi", [P, 2, G, W])
        sc = sb("scores", [P, 3, W])
        nmax = sb("neg_max", [P, 3, 2])
        den = sb("denominators", [P, 3, 2])
        pt = sb("probs_t", [P, 2, W])
        o_hi = sb("out_t_hi", [P, 2, G, SEQ], FP32R)
        o_lo = sb("out_t_lo", [P, 2, G, SEQ], FP32R)
        S = {n: chip.layer_sem(ctx, "gqa_" + n) for n in (
            "w", "w_hi", "w_lo", "wo_hi", "wo_lo", "small", "kw", "kw0", "ready", "alibi", "sq", "sq_hi",
            "ssq_t", "ssq_tr", "o_hi", "kv_mm", "k_copied", "kv_copied", "kss",
            "q_mm", "q_copied", "q_sq", "ssq", "root", "inv", "k_scaled", "k_tr", "k_t", "s_mm",
            "biased", "maxed", "exped", "rden", "scaled", "p_tr", "p_copied", "pv", "o_copied", "y_mm",
            "y_added")}
        block = ctx.enter_context(nc.Block())


        @block.sync
        def _(sp):
            sp.dma_start(nw[:], d["qk_norm_w"]).then_inc(S["small"], 16)
            sp.dma_start(rel[:], d["alibi_rel"]).then_inc(S["small"], 16)
            sp.dma_start(stage[:], d["Wqkv0"][0]).then_inc(S["w"], 16)
            for g in range(GROUPS):
                if g + 1 < GROUPS:
                    sp.wait_ge(S["w_lo"], g + 1)
                    if g:
                        sp.wait_ge(S["wo_lo"], g)
                    sp.dma_start(stage[:], d["Wqkv0"][g + 1]).then_inc(S["w"], 16)
                    sp.wait_ge(S["w_lo"], g + 2)
                else:
                    sp.wait_ge(S["wo_lo"], g)
                sp.dma_start(stage[:, 0:WO], d["Wo0"][g]).then_inc(S["w"], 16)

        @block.gpsimd
        def _(pool):
            pool.wait_ge(S["small"], 32)

            def qkv_low(g):
                pool.wait_ge(S["w_hi"], g + 1)
                nc.gpsimd.tensor_tensor(w_lo[:], stage[:], w_hi[:].bitcast(FP32), ALU.subtract).then_inc(
                    S["w_lo"], 1)

            def out_low(g):
                pool.wait_ge(S["wo_hi"], g + 1)
                nc.gpsimd.tensor_tensor(wo_lo[:], stage[:, 0:WO], wo_hi[:].bitcast(FP32),
                                        ALU.subtract).then_inc(S["wo_lo"], 1)

            def biases(g):
                for h in range(G):
                    if g >= 2:
                        pool.wait_ge(S["biased"], UNITS * (g - 1))
                    nc.gpsimd.tensor_scalar(alibi[:, g % 2, h, :], rel[:], slopes[g * G + h], None,
                                            ALU.mult).then_inc(S["alibi"], 1)

            def squares(g):
                for i in range(G * NH2):
                    n = G * NH2 * g + i
                    pool.wait_ge(S["q_copied"], n + 1)
                    if n:
                        pool.wait_ge(S["q_sq"], n)
                    q = q_t[:, g % 2, i // NH2, (i % NH2) * HALF:(i % NH2 + 1) * HALF]
                    nc.gpsimd.tensor_tensor(q_sq[:], q, q, ALU.mult).then_inc(S["sq"], 1)
                    pool.wait_ge(S["sq_hi"], n + 1)
                    if n >= 2:
                        pool.wait_ge(S["ssq"], n - 1)
                    nc.gpsimd.tensor_tensor(q_sq_lo[:, n % 2, :], q_sq[:], q_sq_hi[:, n % 2, :].bitcast(FP32),
                                            ALU.subtract).then_inc(S["q_sq"], 1)

            qkv_low(0)
            biases(0)
            squares(0)
            qkv_low(1)
            for g in range(GROUPS):
                if g + 1 < GROUPS:
                    biases(g + 1)
                out_low(g)
                if g + 1 < GROUPS:
                    squares(g + 1)
                if g + 2 < GROUPS:
                    qkv_low(g + 2)

        def unit(u):
            g, r = divmod(u, UNITS)
            return g, r // G, r % G

        ALL = GROUPS * UNITS
        KV, Q, SSQ, KTR, TAIL = 0, NT // 2, NT // 2 + 2, NT // 2 + G * NH2, NT // 2 + G * NH2 + 2
        SPLIT_OUT, SPLIT_QKV = AHEAD + 3, TAIL - 1

        def output_of(v):
            if v < G or v % G > 1:
                return None
            return (*divmod(v // G - 1, BATCHES), v % G)

        def query_weights(w, k, h):
            return w[:, k * G * HD + h * HD:k * G * HD + (h + 1) * HD]

        def key_value_weights(w, k):
            at = KC * G * HD + k * 2 * HD
            return w[:, at:at + 2 * HD]

        def wait_projection_bank(pe, g, i):
            if i >= 2:
                if i - 2 < NT:
                    pe.wait_ge(S["kv_copied"], NT * g + i - 1)
                else:
                    pe.wait_ge(S["q_copied"], G * NH2 * g + i - 2 - NT + 1)
            elif g >= 1:
                pe.wait_ge(S["k_t"], 2 * (g - 1) + i + 1)

        @block.tensor
        def _(pe):
            def project(g, step):
                if step < Q:
                    if step == 0:
                        pe.wait_ge(S["w_lo"], g + 1)
                    for t in (2 * step, 2 * step + 1):
                        tok = slice(t * P, (t + 1) * P)
                        wait_projection_bank(pe, g, t)
                        for c in range(KC):
                            ins = split_matmul(nc, bank[t % 2][:, 0:2 * HD], (x_hi[:, c, tok], x_lo[:, c, tok]),
                                               (key_value_weights(w_hi, c), key_value_weights(w_lo, c)),
                                               c == 0, c == KC - 1)
                        ins.then_inc(S["kv_mm"], 1)
                elif step < KTR:
                    i = step - Q
                    h, half = divmod(i, NH2)
                    tok = slice(half * HALF, (half + 1) * HALF)
                    wait_projection_bank(pe, g, NT + i)
                    for c in range(KC):
                        ins = split_matmul(nc, bank[i % 2][:], (query_weights(w_hi, c, h),
                                                                query_weights(w_lo, c, h)),
                                           (x_hi[:, c, tok], x_lo[:, c, tok]), c == 0, c == KC - 1)
                    ins.then_inc(S["q_mm"], 1)
                elif step < TAIL:
                    j = step - KTR
                    pe.wait_ge(S["k_scaled"], NT * g + 4 * (j + 1))
                    pe.wait_ge(S["q_copied"], G * NH2 * (g + 1) - 1 + j)
                    for t in range(4):
                        ins = nc.tensor.transpose(bank[j][:, t * P:(t + 1) * P], keys[:, 4 * j + t, :],
                                                  ident[:])
                    ins.then_inc(S["k_tr"], 1)
                if SSQ <= step < SSQ + G * NH2:
                    sum_squares(g, step - SSQ)
                if step == TAIL:
                    pe.wait_ge(S["ssq_t"], g + 1)
                    for t in range(HALF // P):
                        n = G * NH2
                        ins = nc.tensor.transpose(bank[2][:, t * n:(t + 1) * n], ssq_t[:, t * P:(t + 1) * P],
                                                  ident[0:n, 0:n])
                    ins.then_inc(S["ssq_tr"], 1)

            def sum_squares(g, i):
                n = G * NH2 * g + i
                pe.wait_ge(S["q_sq"], n + 1)
                if g >= 1 and i == 0:
                    pe.wait_ge(S["root"], 2 * g)
                split_matmul(nc, bank[2][0:G * NH2, :], (pick[:, i, :],),
                             (q_sq_hi[:, n % 2, :], q_sq_lo[:, n % 2, :]), i == 0,
                             i == G * NH2 - 1).then_inc(S["ssq"], 1)

            def scores(u):
                g, b, h = unit(u)
                if u % UNITS == 0:
                    pe.wait_ge(S["k_t"], 2 * (g + 1))
                    pe.wait_ge(S["q_copied"], G * NH2 * (g + 1))
                if u >= 2:
                    pe.wait_ge(S["biased"], u - 1)
                qs = q_t[:, g % 2, h, b * SEQ:(b + 1) * SEQ]
                ks = k_t[:, g % 2, b * SEQ:(b + 1) * SEQ]
                nc.tensor.matmul(bank[3 + u % 2][:, 0:P], qs[:, 0:P], ks[:, 0:P], start=True, stop=True)
                nc.tensor.matmul(bank[3 + u % 2][:, P:W], qs[:, P:SEQ], ks, start=True,
                                 stop=True).then_inc(S["s_mm"], 1)

            def transposes(u):
                pe.wait_ge(S["scaled"], u + 1)
                if u >= 1:
                    pe.wait_ge(S["p_copied"], u)
                p = sc[:, u % 3, :]
                nc.tensor.transpose(bank[5][:, 0:P], p[:, 0:P], ident[:])
                nc.tensor.transpose(bank[5][:, P:2 * P], p[:, P:2 * P], ident[:])
                nc.tensor.transpose(bank[5][:, 2 * P:W], p[:, 2 * P:W], ident[:]).then_inc(S["p_tr"], 1)

            def values(u):
                g, b, h = unit(u)
                pe.wait_ge(S["p_copied"], u + 1)
                if u >= 1:
                    pe.wait_ge(S["o_copied"], u)
                nc.tensor.matmul(bank[6][:, 0:SEQ], vals[:, g % VALS, 2 * b, :], pt[:, u % 2, 0:SEQ],
                                 start=True, stop=False)
                nc.tensor.matmul(bank[6][:, P:SEQ], vals[:, g % VALS, 2 * b + 1, :], pt[:, u % 2, SEQ:W],
                                 start=False, stop=True).then_inc(S["pv"], 1)

            def output(g, b, t):
                if b == 0 and t == 0:
                    pe.wait_ge(S["wo_lo"], g + 1)
                nb = BATCHES * g + b
                if t == 0:
                    pe.wait_ge(S["o_copied"], G * (nb + 1))
                if 2 * nb + t >= 1:
                    pe.wait_ge(S["y_added"], 2 * nb + t)
                for h in range(G):
                    tok, cols = slice(t * P, (t + 1) * P), slice(h * C, (h + 1) * C)
                    ins = split_matmul(nc, bank[7][:], (o_hi[:, nb % 2, h, tok], o_lo[:, nb % 2, h, tok]),
                                       (wo_hi[:, cols], wo_lo[:, cols]), h == 0, h == G - 1)
                ins.then_inc(S["y_mm"], 1)

            pe.wait_ge(S["ready"], 2)
            for step in range(UNITS):
                project(0, step)
            for u in range(ALL + AHEAD + 3):
                if u < ALL:
                    scores(u)
                    if u // UNITS + 1 < GROUPS:
                        project(u // UNITS + 1, u % UNITS)
                if 0 <= u - AHEAD < ALL:
                    transposes(u - AHEAD)
                v = u - AHEAD - 1
                if 0 <= v < ALL:
                    values(v)
                if output_of(v):
                    output(*output_of(v))

        @block.scalar
        def _(act):
            def project(g, step):
                b = g % 2
                if step < Q:
                    for t in (2 * step, 2 * step + 1):
                        act.wait_ge(S["kv_mm"], NT * g + t + 1)
                        if t == 0 and g:
                            act.wait_ge(S["k_tr"], 2 * g)
                        if t == 0 and g >= VALS:
                            act.wait_ge(S["pv"], UNITS * (g - VALS + 1))
                        nc.scalar.activation(keys[:, t, :], bank[t % 2][:, 0:HD], ACT.Copy).then_inc(
                            S["k_copied"], 1)
                        nc.scalar.activation(vals[:, g % VALS, t, :], bank[t % 2][:, HD:2 * HD],
                                             ACT.Copy).then_inc(S["kv_copied"], 1)
                        act.wait_ge(S["k_copied"], NT * g + t + 1)
                        if t or g:
                            act.wait_ge(S["kss"], NT * g + t)
                        nc.scalar.activation(k_sq[:], keys[:, t, :], ACT.Square,
                                             accum_out=kss[:, b, t:t + 1]).then_inc(S["kss"], 1)
                elif step < KTR:
                    i = step - Q
                    h, half = divmod(i, NH2)
                    act.wait_ge(S["q_mm"], G * NH2 * g + i + 1)
                    if g >= 2 and i == 0:
                        act.wait_ge(S["s_mm"], UNITS * (g - 1))
                    nc.scalar.activation(q_t[:, b, h, half * HALF:(half + 1) * HALF], bank[i % 2][:],
                                         ACT.Copy).then_inc(S["q_copied"], 1)
                    if i == 0:
                        act.wait_ge(S["kss"], NT * (g + 1))
                        nc.scalar.activation(kinv[:, b, :], kss[:, b, :], ACT.Sqrt, bias=eps[:],
                                             scale=1.0 / HD).then_inc(S["root"], 1)
                elif step < TAIL:
                    j = step - KTR
                    act.wait_ge(S["k_tr"], 2 * g + j + 1)
                    nc.scalar.activation(k_t[:, b, j * 512:(j + 1) * 512], bank[j][:], ACT.Copy,
                                         scale=kw[:]).then_inc(S["k_t"], 1)
                    if j == 1:
                        act.wait_ge(S["ssq"], G * NH2 * (g + 1))
                        nc.scalar.activation(ssq_t[:], bank[2][0:G * NH2, :], ACT.Copy).then_inc(S["ssq_t"], 1)
                elif step == TAIL:
                    act.wait_ge(S["ssq_tr"], g + 1)
                    nc.scalar.activation(qinv[:, b, :], bank[2][:, 0:NT * G], ACT.Sqrt, bias=eps[:],
                                         scale=1.0 / HD).then_inc(S["root"], 1)

            def exp(u):
                act.wait_ge(S["maxed"], u + 1)
                for i, (lo, hi) in enumerate(((0, P), (P, W))):
                    ins = nc.scalar.activation(sc[:, u % 3, lo:hi], sc[:, u % 3, lo:hi], ACT.Exp,
                                               bias=nmax[:, u % 3, i:i + 1],
                                               accum_out=den[:, u % 3, i:i + 1])
                ins.then_inc(S["exped"], 1)

            def copy_probs(u):
                act.wait_ge(S["p_tr"], u + 1)
                if u >= 2:
                    act.wait_ge(S["pv"], u - 1)
                nc.scalar.activation(pt[:, u % 2, :], bank[5][:, 0:W], ACT.Copy).then_inc(S["p_copied"], 1)

            def copy_out(u):
                nb = u // G
                act.wait_ge(S["pv"], u + 1)
                if nb >= 2:
                    act.wait_ge(S["y_mm"], 2 * (nb - 1))
                nc.scalar.activation(o_hi[:, nb % 2, u % G, :], bank[6][:, 0:SEQ], ACT.Copy).then_inc(S["o_hi"], 1)

            act.wait_ge(S["kw"], 1)
            for step in range(UNITS):
                project(0, step)
            for u in range(ALL + AHEAD + 2):
                if u < ALL:
                    exp(u)
                    if u // UNITS + 1 < GROUPS:
                        project(u // UNITS + 1, u % UNITS)
                if AHEAD <= u < ALL + AHEAD:
                    copy_probs(u - AHEAD)
                if 0 <= u - AHEAD - 1 < ALL:
                    copy_out(u - AHEAD - 1)

        @block.vector
        def _(dve):
            nc.vector.memset(pick[:].bitcast(FP32), 0.0).then_inc(S["ready"], 1)
            dve.wait_ge(S["ready"], 1)
            nc.vector.memset(pick[:].rearrange("p a b -> p (a b)")[:, 0:(G * NH2) ** 2:G * NH2 + 1].bitcast(FP32),
                             1.0).then_inc(S["ready"], 1)
            nc.vector.memset(eps[:], EPS).then_inc(S["kw0"], 1)
            dve.wait_ge(S["small"], 32)
            nc.vector.tensor_scalar(nw[:, 0:1], nw[:, 0:1], 1.0 / math.sqrt(HD), None, ALU.mult).then_inc(
                S["kw0"], 1)
            dve.wait_ge(S["kw0"], 2)
            nc.vector.tensor_tensor(kw[:], nw[:, 0:1], nw[:, 1:2], ALU.mult).then_inc(S["kw"], 1)

            def split_qkv(g):
                dve.wait_ge(S["w"], 16 * max(2 * g, 1))
                if g:
                    dve.wait_ge(S["q_mm"], G * NH2 * g)
                    dve.wait_ge(S["kv_mm"], NT * g)
                nc.vector.tensor_copy(w_hi[:], stage[:]).then_inc(S["w_hi"], 1)

            def split_out(g):
                dve.wait_ge(S["w"], 16 * min(2 * g + 3, 2 * GROUPS))
                if g:
                    dve.wait_ge(S["y_mm"], NT * g)
                nc.vector.tensor_copy(wo_hi[:], stage[:, 0:WO]).then_inc(S["wo_hi"], 1)

            def project(g, step):
                b = g % 2
                if step == Q + 1:
                    dve.wait_ge(S["root"], 2 * g + 1)
                    nc.vector.reciprocal(kinv[:, b, :], kinv[:, b, :]).then_inc(S["inv"], 1)
                if step in (Q + 3, Q + 4):
                    dve.wait_ge(S["inv"], 2 * g + 1)
                    for t in range(4 * (step - Q - 3), 4 * (step - Q - 2)):
                        nc.vector.tensor_scalar(keys[:, t, :], keys[:, t, :], kinv[:, b, t:t + 1], None,
                                                ALU.mult).then_inc(S["k_scaled"], 1)
                if Q < step <= KTR:
                    n = G * NH2 * g + step - Q - 1
                    dve.wait_ge(S["sq"], n + 1)
                    if n >= 2:
                        dve.wait_ge(S["ssq"], n - 1)
                    nc.vector.tensor_copy(q_sq_hi[:, n % 2, :], q_sq[:]).then_inc(S["sq_hi"], 1)
                if step == SPLIT_QKV and g + 1 < GROUPS:
                    split_qkv(g + 1)
                if step == TAIL + 1:
                    dve.wait_ge(S["root"], 2 * g + 2)
                    nc.vector.reciprocal(qinv[:, b, :], qinv[:, b, :]).then_inc(S["inv"], 1)

            def bias_and_max(u):
                g, b, h = unit(u)
                s = sc[:, u % 3, :]
                dve.wait_ge(S["s_mm"], u + 1)
                if u % UNITS == 0:
                    dve.wait_ge(S["inv"], 2 * g + 2)
                dve.wait_ge(S["alibi"], G * g + h + 1)
                if u >= 3:
                    dve.wait_ge(S["p_tr"], u - 2)
                for i, (lo, hi) in enumerate(((0, P), (P, W))):
                    half, t4 = divmod(2 * b + i, HALF // P)
                    at = t4 * G * NH2 + h * NH2 + half
                    ins = nc.vector.scalar_tensor_tensor(
                        out=s[:, lo:hi], in0=bank[3 + u % 2][:, lo:hi], scalar=qinv[:, g % 2, at:at + 1],
                        in1=alibi[:, g % 2, h, lo:hi], op0=ALU.mult, op1=ALU.add)
                ins.then_inc(S["biased"], 1)
                dve.wait_ge(S["biased"], u + 1)
                for i, (lo, hi) in enumerate(((0, P), (P, W))):
                    ins = nc.vector.tensor_reduce(nmax[:, u % 3, i:i + 1], s[:, lo:hi], AX, ALU.max,
                                                  negate=True)
                ins.then_inc(S["maxed"], 1)

            def normalise(u):
                dve.wait_ge(S["exped"], u + 1)
                nc.vector.reciprocal(den[:, u % 3, :], den[:, u % 3, :]).then_inc(S["rden"], 1)
                dve.wait_ge(S["rden"], u + 1)
                for i, (lo, hi) in enumerate(((0, P), (P, W))):
                    p = sc[:, u % 3, lo:hi]
                    ins = nc.vector.tensor_scalar(p, p, den[:, u % 3, i:i + 1], None, ALU.mult)
                ins.then_inc(S["scaled"], 1)

            def copy_out(u):
                g, b, h = unit(u)
                nb = u // G
                dve.wait_ge(S["o_hi"], u + 1)
                if nb >= 2:
                    dve.wait_ge(S["y_mm"], 2 * (nb - 1))
                nc.vector.tensor_tensor(o_lo[:, nb % 2, h, :], bank[6][:, 0:SEQ],
                                        o_hi[:, nb % 2, h, :].bitcast(FP32), ALU.subtract).then_inc(
                    S["o_copied"], 1)

            def add_output(g, b, tile):
                t = 2 * b + tile
                dve.wait_ge(S["y_mm"], NT * g + t + 1)
                if g == 0:
                    nc.vector.tensor_copy(branch[:, t, :], bank[7][:]).then_inc(S["y_added"], 1)
                else:
                    dve.wait_ge(S["y_added"], NT * (g - 1) + t + 1)
                    nc.vector.tensor_tensor(branch[:, t, :], branch[:, t, :], bank[7][:],
                                            ALU.add).then_inc(S["y_added"], 1)

            split_qkv(0)
            for step in range(UNITS):
                project(0, step)
            for u in range(ALL + AHEAD + 4):
                if output_of(u - AHEAD - 2):
                    add_output(*output_of(u - AHEAD - 2))
                if u < ALL:
                    g = u // UNITS
                    bias_and_max(u)
                    if u == 0 or (g and u % UNITS == SPLIT_OUT):
                        split_out(g)
                    if g + 1 < GROUPS:
                        project(g + 1, u % UNITS)
                if 1 <= u <= ALL:
                    normalise(u - 1)
                if 0 <= u - AHEAD - 1 < ALL:
                    copy_out(u - AHEAD - 1)


def int8_ffn(chip):
    nc, d, bank = chip.nc, chip.dram, chip.bank
    x_hi, x_lo, branch = chip.x_hi, chip.x_lo, chip.branch
    INNER = 1376
    IC = -(-INNER // P)
    rows = [min(P, INNER - i * P) for i in range(IC)]
    with ExitStack() as ctx:
        def sb(name, shape, dt=FP32):
            return ctx.enter_context(nc.sbuf_tensor(f"ffn_{name}", shape, dt))

        gate_i = sb("gate_int", [P, 2, INNER], I32)
        up_i = sb("up_int", [P, INNER], I32)
        down_i = sb("down_int", [P, 2, C], I32)
        gate_w = sb("gate_w", [P, KC, INNER], FP32R)
        up_w = sb("up_w", [P, KC, INNER], FP32R)
        down_w = sb("down_w", [P, IC, C], FP32R)
        scales = sb("scales", [P, 2, IC])
        down_s = sb("down_scale", [P, C])
        gate = sb("gate", [P, 2, HALF])
        h = sb("hidden", [P, 2, HALF])
        h_hi = sb("hidden_hi", [P, IC, HALF], FP32R)
        h_lo = sb("hidden_lo", [P, IC, HALF], FP32R)
        S = {n: chip.layer_sem(ctx, "ffn_" + n) for n in (
            "g0", "g1", "u", "d0", "d1", "small", "g_cast", "u_cast", "d_cast",
            "g_mm", "u_mm", "gated", "hidden", "h_hi", "h_lo", "y_mm", "y_copied")}
        block = ctx.enter_context(nc.Block())


        @block.sync
        def _(sp):
            for k in range(KC):
                if k >= 2:
                    sp.wait_ge(S["g_cast"], k - 1)
                sp.dma_start(gate_i[:, k % 2], d["gate1"][:, k, :]).then_inc(S[f"g{k % 2}"], 16)
                if k >= 1:
                    sp.wait_ge(S["u_cast"], k)
                sp.dma_start(up_i[:], d["up1"][:, k, :]).then_inc(S["u"], 16)
            sp.dma_start(scales[:], d["scales1"]).then_inc(S["small"], 16)
            sp.dma_start(down_s[:], d["down_scale1"]).then_inc(S["small"], 16)
            for i in range(IC):
                if i >= 2:
                    sp.wait_ge(S["d_cast"], i - 1)
                sp.dma_start(down_i[:, i % 2], d["down1"][:, i, :]).then_inc(S[f"d{i % 2}"], 16)

        @block.gpsimd
        def _(pool):
            for k in range(KC):
                pool.wait_ge(S["u"], 16 * (k + 1))
                nc.gpsimd.tensor_copy(up_w[:, k, :], up_i[:]).then_inc(S["u_cast"], 1)
            for n in range(NH2 * IC):
                i = n % IC
                if n < IC:
                    pool.wait_ge(S[f"d{i % 2}"], 16 * (i // 2 + 1))
                    nc.gpsimd.tensor_copy(down_w[:, i, :], down_i[:, i % 2]).then_inc(S["d_cast"], 1)
                r = rows[i]
                pool.wait_ge(S["h_hi"], n + 1)
                if n >= IC:
                    pool.wait_ge(S["y_mm"], NT // 2)
                nc.gpsimd.tensor_tensor(h_lo[0:r, i, :], h[0:r, n % 2, :], h_hi[0:r, i, :].bitcast(FP32),
                                        ALU.subtract).then_inc(S["h_lo"], 1)

        @block.tensor
        def _(pe):
            for half in range(NH2):
                tok = slice(half * HALF, (half + 1) * HALF)
                for i in range(IC):
                    n = half * IC + i
                    cols = slice(i * P, i * P + rows[i])
                    for w, out, cast, done, freed in ((gate_w, bank[n % 2], "g_cast", "g_mm", "gated"),
                                                      (up_w, bank[2 + n % 2], "u_cast", "u_mm", "hidden")):
                        if n >= 2:
                            pe.wait_ge(S[freed], n - 1)
                        for k in range(KC):
                            if n == 0:
                                pe.wait_ge(S[cast], k + 1)
                            ins = split_matmul(nc, out[0:rows[i], :], (w[:, k, cols],),
                                               (x_hi[:, k, tok], x_lo[:, k, tok]), k == 0, k == KC - 1)
                        ins.then_inc(S[done], 1)
                pe.wait_ge(S["d_cast"], IC)
                for j in range(4):
                    t = 4 * half + j
                    if t >= 4:
                        pe.wait_ge(S["y_copied"], t - 3)
                    for i in range(IC):
                        if j == 0:
                            pe.wait_ge(S["h_lo"], half * IC + i + 1)
                        a = (slice(0, rows[i]), i, slice(j * P, (j + 1) * P))
                        ins = split_matmul(nc, bank[4 + j][:], (h_hi[a], h_lo[a]),
                                           (down_w[0:rows[i], i, :],), i == 0, i == IC - 1)
                    ins.then_inc(S["y_mm"], 1)

        @block.scalar
        def _(act):
            act.wait_ge(S["small"], 32)
            for n in range(NH2 * IC):
                i = n % IC
                r = rows[i]
                act.wait_ge(S["g_mm"], n + 1)
                if n >= 2:
                    act.wait_ge(S["hidden"], n - 1)
                nc.scalar.activation(gate[0:r, n % 2, :], bank[n % 2][0:r, :], ACT.Copy,
                                     scale=scales[0:r, 0, i:i + 1]).then_inc(S["gated"], 1)
                act.wait_ge(S["hidden"], n + 1)
                if n >= IC:
                    act.wait_ge(S["y_mm"], NT // 2)
                nc.scalar.activation(h_hi[0:r, i, :], h[0:r, n % 2, :], ACT.Copy).then_inc(S["h_hi"], 1)

        @block.vector
        def _(dve):
            for k in range(KC):
                dve.wait_ge(S[f"g{k % 2}"], 16 * (k // 2 + 1))
                nc.vector.tensor_copy(gate_w[:, k, :], gate_i[:, k % 2]).then_inc(S["g_cast"], 1)
            dve.wait_ge(S["small"], 32)
            for n in range(NH2 * IC):
                half, i = divmod(n, IC)
                r = rows[i]
                dve.wait_ge(S["u_mm"], n + 1)
                dve.wait_ge(S["gated"], n + 1)
                if n >= 2:
                    dve.wait_ge(S["h_lo"], n - 1)
                nc.vector.scalar_tensor_tensor(
                    out=h[0:r, n % 2, :], in0=bank[2 + n % 2][0:r, :], scalar=scales[0:r, 1, i:i + 1],
                    in1=gate[0:r, n % 2, :], op0=ALU.mult, op1=ALU.mult).then_inc(S["hidden"], 1)
                if i == IC - 1:
                    for j in range(4):
                        t = 4 * half + j
                        dve.wait_ge(S["y_mm"], t + 1)
                        nc.vector.tensor_tensor(branch[:, t, :], bank[4 + j][:], down_s[:], ALU.mult).then_inc(
                            S["y_copied"], 1)


def selective_scan(chip):
    nc, d, bank = chip.nc, chip.dram, chip.bank
    x_hi, x_lo, branch, ident = chip.x_hi, chip.x_lo, chip.branch, chip.ident
    STATES, RANK = 16, 16
    R = RANK + 2 * STATES
    UNITS = NH2 * STATES * KC
    RING = 3
    with ExitStack() as ctx:
        def sb(name, shape, dt=FP32):
            return ctx.enter_context(nc.sbuf_tensor(f"ssm_{name}", shape, dt))

        x_t = sb("x_t", [P, KC, TOKENS])
        xpw = sb("x_proj", [P, KC, R])
        xpw_hi = sb("x_proj_hi", [P, KC, R], FP32R)
        xpw_lo = sb("x_proj_lo", [P, KC, R], FP32R)
        dtw = sb("dt_proj", [RANK, C])
        dtb = sb("dt_bias", [P, KC])
        a_neg = sb("a", [P, KC, STATES])
        dskip = sb("d", [P, KC])
        sel = sb("row_select", [R, 2 * STATES, P])
        one = sb("one", [P, 1])
        xp = sb("xp", [R, TOKENS])
        dt = sb("dt", [P, KC, TOKENS])
        dtx = sb("dt_x", [P, KC, TOKENS])
        tmp = sb("softplus", [P, 2, 3, HALF])
        bc = sb("b_and_c", [P, RING, 2, HALF])
        da = sb("decay", [P, RING, HALF])
        dbx = sb("drive", [P, RING, HALF])
        hs = sb("state", [P, RING, HALF])
        hc = sb("read_out", [P, RING, HALF])
        S = {n: chip.layer_sem(ctx, "ssm_" + n) for n in (
            "w", "w2", "a", "xp_mm", "xp", "dt_mm", "pre", "e", "ln", "dt", "dtx", "bc_mm", "bc", "decay", "zero",
            "drive", "scan", "read", "y_mm", "y", "y_tr", "y_copied", "v", "one", "w_split", "x_whole")}
        block = ctx.enter_context(nc.Block())
        W1 = 16 * 5


        def unit(u):
            half, r = divmod(u, STATES * KC)
            return half, r // KC, r % KC

        def tok(half):
            return slice(half * HALF, (half + 1) * HALF)

        @block.sync
        def _(sp):
            sp.dma_start(xpw[:], d["x_proj2"]).then_inc(S["w"], 16)
            sp.dma_start(dtw[:], d["dt_proj2"]).then_inc(S["w2"], 16)
            sp.dma_start(dtb[:], d["dt_bias2"]).then_inc(S["w2"], 16)
            sp.dma_start(a_neg[:], d["a_log2"]).then_inc(S["w2"], 16)
            sp.dma_start(dskip[:], d["d2"]).then_inc(S["w2"], 16)
            sp.dma_start(sel[:], d["row_select2"]).then_inc(S["w2"], 16)

        @block.tensor
        def _(pe):
            pe.wait_ge(S["w_split"], 2)
            for half in range(NH2):
                for k in range(KC):
                    ins = split_matmul(nc, bank[half][0:R, :], (xpw_hi[:, k, :], xpw_lo[:, k, :]),
                                       (x_hi[:, k, tok(half)], x_lo[:, k, tok(half)]), k == 0, k == KC - 1)
                ins.then_inc(S["xp_mm"], 1)
            pe.wait_ge(S["w2"], W1)
            for i in range(NH2 * KC):
                half, c = divmod(i, KC)
                pe.wait_ge(S["xp"], half + 1)
                if i >= 4:
                    pe.wait_ge(S["pre"], 3 * (i - 3))
                nc.tensor.matmul(bank[4 + i % 4][:], dtw[:, c * P:(c + 1) * P], xp[0:RANK, tok(half)],
                                 start=True, stop=True).then_inc(S["dt_mm"], 1)

            def broadcast(j):
                half, n = divmod(j, STATES)
                if j < 2:
                    pe.wait_ge(S["pre"], 3 * NH2 * KC)
                else:
                    pe.wait_ge(S["bc"], j - 1)
                for i in range(2):
                    ins = nc.tensor.matmul(bank[4 + 2 * (j % 2) + i][:], sel[:, i * STATES + n, :],
                                           xp[:, tok(half)], start=True, stop=True)
                ins.then_inc(S["bc_mm"], 1)

            broadcast(0)
            broadcast(1)
            for u in range(UNITS):
                half, n, c = unit(u)
                if c == 0 and u // KC + 2 < NH2 * STATES:
                    broadcast(u // KC + 2)
                if half and n == 0:
                    pe.wait_ge(S["y"], c + 1)
                pe.wait_ge(S["read"], u + 1)
                nc.tensor.matmul(bank[c][:], ident[:], hc[:, u % RING, :], start=(n == 0),
                                 stop=(n == STATES - 1)).then_inc(S["y_mm"], 1)
            for t in range(NT):
                pe.wait_ge(S["y"], KC * (t // 4 + 1))
                if t >= 4:
                    pe.wait_ge(S["y_copied"], t - 3)
                for c in range(KC):
                    ins = nc.tensor.transpose(bank[4 + t % 4][:, c * P:(c + 1) * P], dt[:, c, t * P:(t + 1) * P],
                                              ident[:])
                ins.then_inc(S["y_tr"], 1)

        @block.scalar
        def _(act):
            for half in range(NH2):
                act.wait_ge(S["xp_mm"], half + 1)
                nc.scalar.activation(xp[:, tok(half)], bank[half][0:R, :], ACT.Copy).then_inc(S["xp"], 1)
            act.wait_ge(S["w2"], W1)
            act.wait_ge(S["one"], 1)
            nc.scalar.activation(a_neg[:], a_neg[:], ACT.Exp).then_inc(S["a"], 1)
            for i in range(NH2 * KC):
                act.wait_ge(S["pre"], 3 * i + 3)
                nc.scalar.activation(tmp[:, i % 2, 0, :], tmp[:, i % 2, 0, :], ACT.Exp).then_inc(S["e"], 1)
                act.wait_ge(S["e"], i + 1)
                half, c = divmod(i, KC)
                nc.scalar.activation(dt[:, c, tok(half)], tmp[:, i % 2, 0, :], ACT.Ln,
                                     bias=one[:]).then_inc(S["ln"], 1)
            act.wait_ge(S["dt"], NH2 * KC)
            act.wait_ge(S["a"], 2)
            for u in range(UNITS):
                half, n, c = unit(u)
                if c == 0:
                    j = u // KC
                    act.wait_ge(S["bc_mm"], j + 1)
                    if j >= RING:
                        act.wait_ge(S["drive"], KC * (j - RING + 1))
                        act.wait_ge(S["read"], KC * (j - RING + 1))
                    for i in range(2):
                        ins = nc.scalar.activation(bc[:, j % RING, i, :], bank[4 + 2 * (j % 2) + i][:], ACT.Copy)
                    ins.then_inc(S["bc"], 1)
                if u >= RING:
                    act.wait_ge(S["scan"], u - RING + 1)
                nc.scalar.activation(da[:, u % RING, :], dt[:, c, tok(half)], ACT.Exp,
                                     scale=a_neg[:, c, n:n + 1]).then_inc(S["decay"], 1)
            for t in range(NT):
                act.wait_ge(S["y_tr"], t + 1)
                nc.scalar.activation(branch[:, t, :], bank[4 + t % 4][:], ACT.Copy).then_inc(S["y_copied"], 1)

        @block.gpsimd
        def _(pool):
            for half in range(NH2):
                for c in range(KC):
                    nc.gpsimd.tensor_tensor(x_t[:, c, tok(half)], x_hi[:, c, tok(half)].bitcast(FP32),
                                            x_lo[:, c, tok(half)].bitcast(FP32), ALU.add).then_inc(
                        S["x_whole"], 1)
            for u in range(UNITS):
                half, n, c = unit(u)
                pool.wait_ge(S["scan"], u + 1)
                pool.wait_ge(S["bc"], u // KC + 1)
                if u >= RING:
                    pool.wait_ge(S["y_mm"], u - RING + 1)
                nc.gpsimd.tensor_tensor(hc[:, u % RING, :], hs[:, u % RING, :], bc[:, (u // KC) % RING, 1, :],
                                        ALU.mult).then_inc(S["read"], 1)

        @block.vector
        def _(dve):
            nc.vector.memset(one[:], 1.0).then_inc(S["one"], 1)
            dve.wait_ge(S["w"], 16)
            nc.vector.tensor_copy(xpw_hi[:], xpw[:]).then_inc(S["w_split"], 1)
            dve.wait_ge(S["w_split"], 1)
            nc.vector.tensor_tensor(xpw_lo[:], xpw[:], xpw_hi[:].bitcast(FP32), ALU.subtract).then_inc(
                S["w_split"], 1)
            dve.wait_ge(S["w2"], W1)

            def before_log(i):
                half, c = divmod(i, KC)
                dve.wait_ge(S["dt_mm"], i + 1)
                nc.vector.tensor_scalar(tmp[:, i % 2, 0, :], bank[4 + i % 4][:], dtb[:, c:c + 1], None,
                                        ALU.add).then_inc(S["pre"], 1)
                nc.vector.tensor_scalar(tmp[:, i % 2, 1, :], bank[4 + i % 4][:], dtb[:, c:c + 1], 0.0,
                                        ALU.add, ALU.max).then_inc(S["pre"], 1)
                dve.wait_ge(S["pre"], 3 * i + 2)
                nc.vector.scalar_tensor_tensor(out=tmp[:, i % 2, 0, :], in0=tmp[:, i % 2, 1, :], scalar=-2.0,
                                               in1=tmp[:, i % 2, 0, :], op0=ALU.mult,
                                               op1=ALU.add).then_inc(S["pre"], 1)

            def after_log(i):
                half, c = divmod(i, KC)
                e, m, w = (tmp[:, i % 2, j, :] for j in range(3))
                out = dt[:, c, tok(half)]
                dve.wait_ge(S["e"], i + 1)
                nc.vector.tensor_scalar(w, e, 1.0, -1.0, ALU.add, ALU.add).then_inc(S["v"], 1)
                dve.wait_ge(S["v"], 4 * i + 1)
                nc.vector.tensor_tensor(w, e, w, ALU.subtract).then_inc(S["v"], 1)
                dve.wait_ge(S["v"], 4 * i + 2)
                nc.vector.tensor_tensor(w, w, m, ALU.add).then_inc(S["v"], 1)
                dve.wait_ge(S["v"], 4 * i + 3)
                dve.wait_ge(S["ln"], i + 1)
                nc.vector.tensor_tensor(out, out, w, ALU.add).then_inc(S["dt"], 1)
                dve.wait_ge(S["dt"], i + 1)
                dve.wait_ge(S["x_whole"], i + 1)
                nc.vector.tensor_tensor(dtx[:, c, tok(half)], out, x_t[:, c, tok(half)], ALU.mult).then_inc(
                    S["v"], 1)

            for i in range(NH2 * KC + 1):
                if i < NH2 * KC:
                    before_log(i)
                if i >= 1:
                    after_log(i - 1)
            dve.wait_ge(S["a"], 1)
            nc.vector.tensor_scalar(a_neg[:], a_neg[:], -1.0, None, ALU.mult).then_inc(S["a"], 1)
            dve.wait_ge(S["v"], 4 * NH2 * KC)
            for u in range(UNITS + 1):
                if u < UNITS:
                    half, n, c = unit(u)
                    dve.wait_ge(S["bc"], u // KC + 1)
                    if u >= RING:
                        dve.wait_ge(S["scan"], u - RING + 1)
                    nc.vector.tensor_tensor(dbx[:, u % RING, :], dtx[:, c, tok(half)],
                                            bc[:, (u // KC) % RING, 0, :], ALU.mult).then_inc(S["drive"], 1)
                    dve.wait_ge(S["decay"], u + 1)
                    nc.vector.memset(da[:, u % RING, 0:HALF:SEQ], 0.0).then_inc(S["zero"], 1)
                if u >= 1:
                    v = u - 1
                    dve.wait_ge(S["zero"], v + 1)
                    dve.wait_ge(S["drive"], v + 1)
                    if v >= RING:
                        dve.wait_ge(S["read"], v - RING + 1)
                    nc.vector.tensor_tensor_scan(hs[:, v % RING, :], da[:, v % RING, :], dbx[:, v % RING, :],
                                                 0.0, ALU.mult, ALU.add).then_inc(S["scan"], 1)
                if u and u % (STATES * KC) == 0:
                    half = u // (STATES * KC) - 1
                    for c in range(KC):
                        dve.wait_ge(S["y_mm"], u - KC + c + 1)
                        nc.vector.scalar_tensor_tensor(
                            out=dt[:, c, tok(half)], in0=x_t[:, c, tok(half)], scalar=dskip[:, c:c + 1],
                            in1=bank[c][:], op0=ALU.mult, op1=ALU.add).then_inc(S["y"], 1)


def table_linear(chip):
    nc, d, bank = chip.nc, chip.dram, chip.bank
    x_hi, x_lo, branch, ident = chip.x_hi, chip.x_lo, chip.branch, chip.ident
    BITS, WORD = 4, 32
    WORDS = C // WORD
    CODES = 1 << BITS
    with ExitStack() as ctx:
        def sb(name, shape, dt=FP32):
            return ctx.enter_context(nc.sbuf_tensor(f"lut_{name}", shape, dt))

        planes = sb("planes", [P, BITS, KC * WORDS], I32)
        bits = sb("bits", [P, BITS, KC * WORDS, WORD], I32)
        code = sb("code", [P, KC, C])
        lut = sb("table", [P, KC, CODES])
        w = sb("weights", [P, KC, C])
        pick = sb("pick", [P, 2, 2, C])
        w_hi = sb("weights_t_hi", [P, KC, C], FP32R)
        w_lo = sb("weights_t_lo", [P, KC, C], FP32R)
        bias = sb("bias", [P, C])
        S = {n: chip.layer_sem(ctx, "lut_" + n) for n in (
            "in", "bits", "code", "dve_pick", "dve_w", "pool_pick", "pool_w", "w_tr", "w_hi", "w_lo", "y_mm", "y")}
        block = ctx.enter_context(nc.Block())

        @block.sync
        def _(sp):
            sp.dma_start(planes[:], d["planes3"]).then_inc(S["in"], 16)
            sp.dma_start(lut[:], d["lut3"]).then_inc(S["in"], 16)
            sp.dma_start(bias[:], d["bias3"]).then_inc(S["in"], 16)

        def look_up(eng, e, chunks, picked, written, slot):
            n = 0
            for o in chunks:
                for l in range(CODES):
                    if l == 0:
                        e.tensor_scalar(w[:, o, :], code[:, o, :], float(l), lut[:, o, l:l + 1], ALU.is_equal,
                                        ALU.mult).then_inc(written, 1)
                    else:
                        if n >= 2:
                            eng.wait_ge(written, written_before(n - 2))
                        e.tensor_scalar(pick[:, slot, n % 2, :], code[:, o, :], float(l), lut[:, o, l:l + 1],
                                        ALU.is_equal, ALU.mult).then_inc(picked, 1)
                        eng.wait_ge(picked, n + 1)
                        eng.wait_ge(written, written_before(n))
                        e.tensor_tensor(w[:, o, :], w[:, o, :], pick[:, slot, n % 2, :], ALU.add).then_inc(
                            written, 1)
                        n += 1

        def written_before(n):
            return n + n // (CODES - 1) + 1

        @block.gpsimd
        def _(pool):
            pool.wait_ge(S["code"], BITS - 1)
            look_up(pool, nc.gpsimd, (3,), S["pool_pick"], S["pool_w"], 1)

        @block.vector
        def _(dve):
            dve.wait_ge(S["in"], 48)
            for b in range(WORD):
                ins = nc.vector.tensor_scalar(bits[:, :, :, b], planes[:], b, 1, ALU.logical_shift_right,
                                              ALU.bitwise_and)
            ins.then_inc(S["bits"], 1)
            dve.wait_ge(S["bits"], 1)
            c2 = code[:].rearrange("p k c -> p (k c)")
            b2 = [bits[:, p].rearrange("p a b -> p (a b)") for p in range(BITS)]
            for p in range(BITS - 2, -1, -1):
                src = b2[BITS - 1] if p == BITS - 2 else c2
                if p < BITS - 2:
                    dve.wait_ge(S["code"], BITS - 2 - p)
                nc.vector.scalar_tensor_tensor(out=c2, in0=src, scalar=2.0, in1=b2[p], op0=ALU.mult,
                                               op1=ALU.add).then_inc(S["code"], 1)
            dve.wait_ge(S["code"], BITS - 1)
            look_up(dve, nc.vector, (0, 1, 2), S["dve_pick"], S["dve_w"], 0)
            for o in range(KC):
                dve.wait_ge(S["w_hi"], o + 1)
                nc.vector.tensor_tensor(w_lo[:, :, o * P:(o + 1) * P],
                                        bank[o][:].rearrange("p (k m) -> p k m", k=KC),
                                        w_hi[:, :, o * P:(o + 1) * P].bitcast(FP32), ALU.subtract).then_inc(
                    S["w_lo"], 1)
            for t in range(NT):
                dve.wait_ge(S["y_mm"], t + 1)
                nc.vector.tensor_tensor(branch[:, t, :], bank[4 + t % 4][:], bias[:], ALU.add).then_inc(
                    S["y"], 1)

        @block.tensor
        def _(pe):
            for o in range(KC):
                if o == 3:
                    pe.wait_ge(S["pool_w"], CODES)
                else:
                    pe.wait_ge(S["dve_w"], CODES * (o + 1))
                for i in range(KC):
                    ins = nc.tensor.transpose(bank[o][:, i * P:(i + 1) * P], w[:, o, i * P:(i + 1) * P],
                                              ident[:])
                ins.then_inc(S["w_tr"], 1)
            pe.wait_ge(S["w_lo"], KC)
            for t in range(NT):
                if t >= 4:
                    pe.wait_ge(S["y"], t - 3)
                for k in range(KC):
                    tok = slice(t * P, (t + 1) * P)
                    ins = split_matmul(nc, bank[4 + t % 4][:], (x_hi[:, k, tok], x_lo[:, k, tok]),
                                       (w_hi[:, k, :], w_lo[:, k, :]), k == 0, k == KC - 1)
                ins.then_inc(S["y_mm"], 1)

        @block.scalar
        def _(act):
            for o in range(KC):
                act.wait_ge(S["w_tr"], o + 1)
                nc.scalar.activation(w_hi[:, :, o * P:(o + 1) * P], bank[o][:].rearrange("p (k m) -> p k m", k=KC),
                                     ACT.Copy).then_inc(S["w_hi"], 1)


def head_mixer(chip):
    nc, d, bank = chip.nc, chip.dram, chip.bank
    x_hi, x_lo, branch, ident = chip.x_hi, chip.x_lo, chip.branch, chip.ident
    H, D = 32, 16
    Q = 32
    PAIRS = Q // 2
    THRESHOLD = 4.0 * float(np.float32(0.001))
    with ExitStack() as ctx:
        def sb(name, shape, dt=FP32):
            return ctx.enter_context(nc.sbuf_tensor(f"mix_{name}", shape, dt))

        w = sb("w_qkv", [P, KC, C])
        w_hi = sb("w_qkv_hi", [P, 3, KC, C], FP32R)
        w_lo = sb("w_qkv_lo", [P, 3, KC, C], FP32R)
        wo = sb("w_out", [P, KC, C])
        bias = sb("bias", [1, 4, C])
        one = sb("ones_row", [1, P])
        q_h = sb("q_heads", [P, 2, Q, D])
        k_h = sb("k_heads", [P, 2, PAIRS, 2, 2, D])
        v_h = sb("v_heads", [P, 2, Q, D])
        q_d = sb("q_channels", [P, 2, PAIRS, H])
        k_d = sb("k_channels", [P, 2, PAIRS, 2, H])
        top = sb("top", [P, 2, Q])
        ex = sb("exps", [P, 2, Q, H])
        den = sb("denominators", [P, 2, Q])
        pr = sb("probs_t", [P, 2, Q, H])
        o_h = sb("out_heads", [P, 2, Q, D])
        o = sb("out", [P, 2, H, D])
        o_t = sb("out_t", [P, 2, KC, P])
        S = {n: chip.layer_sem(ctx, "mix_" + n) for n in (
            "w", "w_hi", "w_lo", "bias", "wo", "ready", "q_mm", "k_mm", "v_mm", "heads", "channels", "s_mm",
            "top", "shifted", "exped", "masked", "sum", "probs_t", "o_mm", "scaled", "o", "o_tr", "o_t", "y_mm", "y")}
        block = ctx.enter_context(nc.Block())


        @block.sync
        def _(sp):
            sp.dma_start(bias[:], d["bias4"]).then_inc(S["bias"], 16)
            for i in range(3):
                if i:
                    sp.wait_ge(S["w_lo"], i)
                sp.dma_start(w[:], d["Wqkv4"][:, i]).then_inc(S["w"], 16)
            sp.dma_start(wo[:], d["Wo4"]).then_inc(S["wo"], 16)

        @block.gpsimd
        def _(pool):
            nc.gpsimd.memset(one[:], 1.0).then_inc(S["ready"], 1)
            nc.gpsimd.memset(k_h[:], 0.0).then_inc(S["ready"], 1)

        @block.tensor
        def _(pe):
            def project(t):
                for i, name in enumerate(("q_mm", "k_mm", "v_mm")):
                    if t == 0:
                        pe.wait_ge(S["w_lo"], i + 1)
                    else:
                        pe.wait_ge(S["heads"], 3 * (t - 1) + i + 1)
                    for k in range(KC):
                        tok = slice(t * P, (t + 1) * P)
                        split_matmul(nc, bank[i][:], (x_hi[:, k, tok], x_lo[:, k, tok]),
                                     (w_hi[:, i, k, :], w_lo[:, i, k, :]), k == 0, False)
                    nc.tensor.matmul(bank[i][:], one[:], bias[:, i, :], start=False, stop=True).then_inc(
                        S[name], 1)

            def scores(t):
                pe.wait_ge(S["channels"], 2 * (t + 1))
                if t:
                    pe.wait_ge(S["masked"], t)
                for pair in range(PAIRS):
                    for j in range(4):
                        r = slice(Q * j, Q * (j + 1))
                        ins = nc.tensor.matmul(
                            bank[3 + pair // 8][r, (pair % 8) * 64:(pair % 8 + 1) * 64], q_d[r, t % 2, pair, :],
                            k_d[r, t % 2, pair].rearrange("p e h -> p (e h)"), start=True, stop=True)
                ins.then_inc(S["s_mm"], 1)

            def mix(t):
                pe.wait_ge(S["probs_t"], t + 1)
                if t:
                    pe.wait_ge(S["scaled"], t)
                for n in range(Q):
                    for j in range(4):
                        r = slice(Q * j, Q * (j + 1))
                        ins = nc.tensor.matmul(bank[5][r, n * D:(n + 1) * D], pr[r, t % 2, n, :],
                                               v_h[r, t % 2, n, :], start=True, stop=True)
                ins.then_inc(S["o_mm"], 1)

            def output(t):
                pe.wait_ge(S["o"], t + 1)
                if t:
                    pe.wait_ge(S["o_t"], t)
                for k in range(KC):
                    ins = nc.tensor.transpose(bank[6][:, k * P:(k + 1) * P],
                                              o[:, t % 2].rearrange("p h d -> p (h d)")[:, k * P:(k + 1) * P],
                                              ident[:])
                ins.then_inc(S["o_tr"], 1)

            def result(t):
                pe.wait_ge(S["o_t"], t + 1)
                if t:
                    pe.wait_ge(S["y"], t)
                for k in range(KC):
                    nc.tensor.matmul(bank[7][:], o_t[:, t % 2, k, :], wo[:, k, :], start=(k == 0), stop=False)
                nc.tensor.matmul(bank[7][:], one[:], bias[:, 3, :], start=False, stop=True).then_inc(
                    S["y_mm"], 1)

            pe.wait_ge(S["bias"], 16)
            pe.wait_ge(S["ready"], 2)
            project(0)
            pe.wait_ge(S["wo"], 16)
            for t in range(NT + 3):
                if t + 1 < NT:
                    project(t + 1)
                if t < NT:
                    scores(t)
                if 1 <= t <= NT:
                    mix(t - 1)
                if 2 <= t <= NT + 1:
                    output(t - 2)
                if t >= 3:
                    result(t - 3)

        @block.scalar
        def _(act):
            for i in range(3):
                act.wait_ge(S["w"], 16 * (i + 1))
                nc.scalar.activation(w_hi[:, i], w[:], ACT.Copy).then_inc(S["w_hi"], 1)
            for t in range(NT + 3):
                if t < NT:
                    act.wait_ge(S["shifted"], t + 1)
                    e = ex[:, t % 2].rearrange("p n h -> p (n h)")
                    nc.scalar.activation(e, e, ACT.Exp, scale=0.25).then_inc(S["exped"], 1)
                if 2 <= t <= NT + 1:
                    act.wait_ge(S["o_tr"], t - 1)
                    if t >= 4:
                        act.wait_ge(S["y_mm"], t - 3)
                    nc.scalar.activation(o_t[:, t % 2], bank[6][:].rearrange("p (k m) -> p k m", k=KC),
                                         ACT.Copy).then_inc(S["o_t"], 1)
                if t >= 3:
                    act.wait_ge(S["y_mm"], t - 2)
                    nc.scalar.activation(branch[:, t - 3, :], bank[7][:], ACT.Copy).then_inc(S["y"], 1)

        @block.vector
        def _(dve):
            def heads(t):
                if t >= 2:
                    dve.wait_ge(S["channels"], 2 * (t - 1))
                dve.wait_ge(S["q_mm"], t + 1)
                nc.vector.transpose(q_h[:, t % 2].rearrange("p n d -> p d n"),
                                    bank[0][:].rearrange("p (h d) -> p d h", d=D)).then_inc(S["heads"], 1)
                dve.wait_ge(S["k_mm"], t + 1)
                dve.wait_ge(S["ready"], 2)
                k_out = k_h[:, t % 2].rearrange("p n a b d -> p n (a b) d")[:, :, 0:4:3, :]
                nc.vector.transpose(k_out.rearrange("p n e d -> p d n e"),
                                    bank[1][:].rearrange("p (h d) -> p d h", d=D)).then_inc(S["heads"], 1)
                dve.wait_ge(S["v_mm"], t + 1)
                if t >= 2:
                    dve.wait_ge(S["o_mm"], t - 1)
                nc.vector.transpose(v_h[:, t % 2].rearrange("p n d -> p d n"),
                                    bank[2][:].rearrange("p (h d) -> p d h", d=D)).then_inc(S["heads"], 1)
                dve.wait_ge(S["heads"], 3 * t + 2)
                if t >= 2:
                    dve.wait_ge(S["s_mm"], t - 1)
                nc.vector.transpose(q_d[:, t % 2].rearrange("p n h -> p (n h)"),
                                    q_h[:, t % 2].rearrange("p n d -> p (n d)")).then_inc(S["channels"], 1)
                nc.vector.transpose(k_d[:, t % 2].rearrange("p n e h -> p (n e h)"),
                                    k_h[:, t % 2].rearrange("p n a b d -> p (n a b d)")).then_inc(
                    S["channels"], 1)

            def shift(t):
                dve.wait_ge(S["s_mm"], t + 1)
                if t >= 2:
                    dve.wait_ge(S["probs_t"], t - 1)
                for i in range(2):
                    s = bank[3 + i][:].rearrange("p (n h) -> p n h", h=H)
                    m = top[:, t % 2, i * PAIRS:(i + 1) * PAIRS]
                    nc.vector.tensor_reduce(m, s, AX, ALU.max).then_inc(S["top"], 1)
                for i in range(2):
                    s = bank[3 + i][:].rearrange("p (n h) -> p n h", h=H)
                    m = top[:, t % 2, i * PAIRS:(i + 1) * PAIRS]
                    dve.wait_ge(S["top"], 2 * t + i + 1)
                    ins = nc.vector.tensor_tensor(ex[:, t % 2, i * PAIRS:(i + 1) * PAIRS, :], s,
                                                  m.unsqueeze(2).to_broadcast([P, PAIRS, H]), ALU.subtract)
                ins.then_inc(S["shifted"], 1)

            def mask(t):
                dve.wait_ge(S["exped"], t + 1)
                for i in range(2):
                    e = ex[:, t % 2, i * PAIRS:(i + 1) * PAIRS, :].rearrange("p n h -> p (n h)")
                    ins = nc.vector.scalar_tensor_tensor(out=e, in0=bank[3 + i][:], scalar=THRESHOLD, in1=e,
                                                         op0=ALU.is_gt, op1=ALU.mult)
                ins.then_inc(S["masked"], 1)
                dve.wait_ge(S["masked"], t + 1)
                nc.vector.tensor_reduce(den[:, t % 2, :], ex[:, t % 2], AX, ALU.add).then_inc(S["sum"], 1)
                dve.wait_ge(S["sum"], 2 * t + 1)
                nc.vector.reciprocal(den[:, t % 2, :], den[:, t % 2, :]).then_inc(S["sum"], 1)
                if t >= 2:
                    dve.wait_ge(S["o_mm"], t - 1)
                nc.vector.transpose(pr[:, t % 2].rearrange("p n h -> p (n h)"),
                                    ex[:, t % 2].rearrange("p n h -> p (n h)")).then_inc(S["probs_t"], 1)

            def normalise(t):
                dve.wait_ge(S["o_mm"], t + 1)
                dve.wait_ge(S["sum"], 2 * t + 2)
                if t >= 2:
                    dve.wait_ge(S["o"], t - 1)
                nc.vector.tensor_tensor(o_h[:, t % 2], bank[5][:].rearrange("p (n d) -> p n d", d=D),
                                        den[:, t % 2, :].unsqueeze(2).to_broadcast([P, Q, D]),
                                        ALU.mult).then_inc(S["scaled"], 1)
                dve.wait_ge(S["scaled"], t + 1)
                if t >= 2:
                    dve.wait_ge(S["o_tr"], t - 1)
                nc.vector.transpose(o[:, t % 2].rearrange("p h d -> p d h"),
                                    o_h[:, t % 2].rearrange("p n d -> p d n")).then_inc(S["o"], 1)

            for i in range(3):
                dve.wait_ge(S["w_hi"], i + 1)
                nc.vector.tensor_tensor(w_lo[:, i], w[:], w_hi[:, i].bitcast(FP32), ALU.subtract).then_inc(
                    S["w_lo"], 1)
            heads(0)
            for t in range(NT + 1):
                if t + 1 < NT:
                    heads(t + 1)
                if t < NT:
                    shift(t)
                if t >= 1:
                    normalise(t - 1)
                if t < NT:
                    mask(t)


def routed_lora(chip):
    nc, d, bank = chip.nc, chip.dram, chip.bank
    x_hi, x_lo, branch, ident = chip.x_hi, chip.x_lo, chip.branch, chip.ident
    E, R = 4, 8
    ER = E * R
    SCALE = 16.0 / 8.0
    with ExitStack() as ctx:
        def sb(name, shape, dt=FP32):
            return ctx.enter_context(nc.sbuf_tensor(f"lora_{name}", shape, dt))

        small_w = sb("a_and_router", [P, KC, ER + E])
        small_hi = sb("a_and_router_hi", [P, KC, ER + E], FP32R)
        small_lo = sb("a_and_router_lo", [P, KC, ER + E], FP32R)
        ra_t = sb("ranks_and_logits_t", [ER + E, TOKENS])
        w = sb("w", [P, KC, C])
        w_hi = sb("w_hi", [P, KC, C], FP32R)
        w_lo = sb("w_lo", [P, KC, C], FP32R)
        bm = sb("b", [ER, C])
        bias = sb("bias", [P, C])
        ra = sb("ranks_and_logits", [P, NT, ER + E])
        top = sb("top", [P, NT])
        g = sb("gates", [P, NT, E])
        den = sb("den", [P, NT])
        mixed_t = sb("mixed_t", [ER, TOKENS])
        S = {n: chip.layer_sem(ctx, "lora_" + n) for n in ("in", "w", "bm", "split", "w_hi", "w_lo", "ra_mm", "ra_t", "ra_tr", "ra", "v", "exped", "mixed", "m_tr",
                                                "m_t", "y_mm", "y")}
        block = ctx.enter_context(nc.Block())

        @block.sync
        def _(sp):
            sp.dma_start(small_w[:], d["small5"]).then_inc(S["in"], 16)
            sp.dma_start(w[:], d["W5"]).then_inc(S["w"], 16)
            sp.dma_start(bm[:], d["Bm5"]).then_inc(S["bm"], 16)
            sp.dma_start(bias[:], d["bias5"]).then_inc(S["bm"], 16)

        @block.tensor
        def _(pe):
            pe.wait_ge(S["split"], 2)
            for half in range(NH2):
                tok = slice(half * HALF, (half + 1) * HALF)
                for k in range(KC):
                    ins = split_matmul(nc, bank[2 + half][0:ER + E, :], (small_hi[:, k, :], small_lo[:, k, :]),
                                       (x_hi[:, k, tok], x_lo[:, k, tok]), k == 0, k == KC - 1)
                ins.then_inc(S["ra_mm"], 1)
            pe.wait_ge(S["ra_t"], 2)
            for t in range(NT):
                ins = nc.tensor.transpose(bank[0][:, t * (ER + E):(t + 1) * (ER + E)],
                                          ra_t[:, t * P:(t + 1) * P], ident[0:ER + E, 0:ER + E])
            ins.then_inc(S["ra_tr"], 1)
            pe.wait_ge(S["w_lo"], 1)
            pe.wait_ge(S["bm"], 32)

            def base(t):
                if t >= 4:
                    pe.wait_ge(S["y"], t - 3)
                for k in range(KC):
                    tok = slice(t * P, (t + 1) * P)
                    split_matmul(nc, bank[4 + t % 4][:], (x_hi[:, k, tok], x_lo[:, k, tok]),
                                 (w_hi[:, k, :], w_lo[:, k, :]), k == 0, False)

            def update(t):
                nc.tensor.matmul(bank[4 + t % 4][:], mixed_t[:, t * P:(t + 1) * P], bm[:], start=False,
                                 stop=True).then_inc(S["y_mm"], 1)

            for t in range(4):
                base(t)
            pe.wait_ge(S["mixed"], 1)
            for t in range(NT):
                ins = nc.tensor.transpose(bank[1 + t // 4][0:ER, (t % 4) * P:(t % 4 + 1) * P], ra[:, t, 0:ER],
                                          ident[:])
            ins.then_inc(S["m_tr"], 1)
            pe.wait_ge(S["m_t"], 2)
            for t in range(4):
                update(t)
            for t in range(4, NT):
                base(t)
                update(t)

        @block.scalar
        def _(act):
            for half in range(NH2):
                act.wait_ge(S["ra_mm"], half + 1)
                nc.scalar.activation(ra_t[:, half * HALF:(half + 1) * HALF], bank[2 + half][0:ER + E, :],
                                     ACT.Copy).then_inc(S["ra_t"], 1)
            act.wait_ge(S["ra_tr"], 1)
            nc.scalar.activation(ra[:].rearrange("p t n -> p (t n)"), bank[0][:, 0:NT * (ER + E)],
                                 ACT.Copy).then_inc(S["ra"], 1)
            act.wait_ge(S["v"], 2)
            nc.scalar.activation(g[:], g[:], ACT.Exp).then_inc(S["exped"], 1)
            act.wait_ge(S["m_tr"], 1)
            for i in range(2):
                nc.scalar.activation(mixed_t[:, i * HALF:(i + 1) * HALF], bank[1 + i][0:ER, :],
                                     ACT.Copy).then_inc(S["m_t"], 1)

        @block.vector
        def _(dve):
            dve.wait_ge(S["in"], 16)
            nc.vector.tensor_copy(small_hi[:], small_w[:]).then_inc(S["split"], 1)
            dve.wait_ge(S["split"], 1)
            nc.vector.tensor_tensor(small_lo[:], small_w[:], small_hi[:].bitcast(FP32),
                                    ALU.subtract).then_inc(S["split"], 1)
            dve.wait_ge(S["w"], 16)
            nc.vector.tensor_copy(w_hi[:], w[:]).then_inc(S["w_hi"], 1)
            dve.wait_ge(S["w_hi"], 1)
            nc.vector.tensor_tensor(w_lo[:], w[:], w_hi[:].bitcast(FP32), ALU.subtract).then_inc(S["w_lo"], 1)
            logits = ra[:, :, ER:ER + E]
            dve.wait_ge(S["ra"], 1)
            nc.vector.tensor_reduce(top[:], logits, AX, ALU.max).then_inc(S["v"], 1)
            dve.wait_ge(S["v"], 1)
            nc.vector.tensor_tensor(g[:], logits, top[:].unsqueeze(2).to_broadcast([P, NT, E]),
                                    ALU.subtract).then_inc(S["v"], 1)
            dve.wait_ge(S["exped"], 1)
            nc.vector.tensor_reduce(den[:], g[:], AX, ALU.add).then_inc(S["v"], 1)
            dve.wait_ge(S["v"], 3)
            nc.vector.reciprocal(den[:], den[:]).then_inc(S["v"], 1)
            dve.wait_ge(S["v"], 4)
            nc.vector.tensor_tensor(g[:], g[:], den[:].unsqueeze(2).to_broadcast([P, NT, E]),
                                    ALU.mult).then_inc(S["v"], 1)
            dve.wait_ge(S["v"], 5)
            nc.vector.tensor_scalar(g[:], g[:], SCALE, None, ALU.mult).then_inc(S["v"], 1)
            dve.wait_ge(S["v"], 6)
            for e in range(E):
                r = ra[:, :, e * R:(e + 1) * R]
                ins = nc.vector.tensor_tensor(r, r, g[:, :, e:e + 1].to_broadcast([P, NT, R]), ALU.mult)
            ins.then_inc(S["mixed"], 1)
            dve.wait_ge(S["bm"], 32)
            for t in range(NT):
                dve.wait_ge(S["y_mm"], t + 1)
                nc.vector.tensor_tensor(branch[:, t, :], bank[4 + t % 4][:], bias[:], ALU.add).then_inc(
                    S["y"], 1)


def latent_attention(chip):
    nc, d, bank = chip.nc, chip.dram, chip.bank
    x_hi, x_lo, branch, ident = chip.x_hi, chip.x_lo, chip.branch, chip.ident
    H, QL, L, DN, DR, DV = 32, 192, 64, 128, 64, 128
    QL2 = QL - P
    SCALE = 1.0 / math.sqrt(DN + DR)
    W = P + SEQ
    PAIRS = H // 2
    with ExitStack() as keep:
        def kb(name, shape, dt=FP32):
            return keep.enter_context(nc.sbuf_tensor(f"mla_{name}", shape, dt))

        wq1 = kb("w_query_low", [P, H, 2 * L])
        wq2 = kb("w_query_high", [QL2, H, 2 * L])
        wvo = kb("w_value_out", [P, PAIRS, C])

        with ExitStack() as ctx:
            def sb(name, shape, dt=FP32):
                return ctx.enter_context(nc.sbuf_tensor(f"mla_{name}", shape, dt))

            up_t = sb("w_q_up_t", [P, H, QL])
            uk = sb("w_uk", [P, H, L])
            uv = sb("w_uv", [P, H, L])
            HS = 4
            wout = sb("w_out", [P, 2, HS, C])
            S = {n: chip.layer_sem(keep, "mlw_" + n) for n in ("up0", "up1", "uv", "rope", "out0", "out1", "a_mm", "b_mm", "a",
                                                   "b", "vo_mm", "vo")}
            block = ctx.enter_context(nc.Block())

            @block.sync
            def _(sp):
                for i in range(2):
                    h = slice(i * H // 2, (i + 1) * H // 2)
                    sp.dma_start(up_t[:, h], d["w_q_up_nope_t6"][:, h]).then_inc(S[f"up{i}"], 16)
                    sp.dma_start(uk[:, h], d["w_uk6"][:, h]).then_inc(S[f"up{i}"], 16)
                sp.dma_start(uv[:], d["w_uv6"]).then_inc(S["uv"], 16)
                for c in range(H // HS):
                    if c >= 2:
                        sp.wait_ge(S["vo_mm"], HS * (c - 1) // 2)
                    sp.dma_start(wout[:, c % 2], d["w_out6"][:, c * HS:(c + 1) * HS]).then_inc(
                        S[f"out{c % 2}"], 16)
                sp.dma_start(wq1[:, :, L:2 * L], d["w_q_up_rope_low6"]).then_inc(S["rope"], 16)
                sp.dma_start(wq2[:, :, L:2 * L], d["w_q_up_rope_high6"]).then_inc(S["rope"], 16)
                sp.wait_ge(S["rope"], 32)

            @block.tensor
            def _(pe):
                for i in range(H // 8):
                    if i % 2 == 0:
                        pe.wait_ge(S[f"up{i // 2}"], 32)
                    if i >= 2:
                        pe.wait_ge(S["a"], i - 1)
                    for h in range(8 * i, 8 * i + 8):
                        ins = nc.tensor.matmul(bank[i % 2][:, (h % 8) * L:(h % 8 + 1) * L], up_t[:, h, 0:P],
                                               uk[:, h, :], start=True, stop=True)
                    ins.then_inc(S["a_mm"], 1)
                    if i >= 2:
                        pe.wait_ge(S["b"], i - 1)
                    for h in range(8 * i, 8 * i + 8):
                        ins = nc.tensor.matmul(bank[2 + i % 2][0:QL2, (h % 8) * L:(h % 8 + 1) * L],
                                               up_t[:, h, P:QL], uk[:, h, :], start=True, stop=True)
                    ins.then_inc(S["b_mm"], 1)
                pe.wait_ge(S["uv"], 16)
                for j in range(PAIRS):
                    c = j // (HS // 2)
                    if j % (HS // 2) == 0:
                        pe.wait_ge(S[f"out{c % 2}"], 16 * (c // 2 + 1))
                    if j >= 2:
                        pe.wait_ge(S["vo"], j - 1)
                    for e in range(2):
                        h = 2 * j + e
                        ins = nc.tensor.matmul(bank[4 + j % 2][L * e:L * (e + 1), :], uv[:, h, :],
                                               wout[:, c % 2, h % HS, :], start=True, stop=True)
                    ins.then_inc(S["vo_mm"], 1)

            @block.scalar
            def _(act):
                for i in range(H // 8):
                    act.wait_ge(S["a_mm"], i + 1)
                    nc.scalar.activation(wq1[:, 8 * i:8 * i + 8, 0:L],
                                         bank[i % 2][:].rearrange("p (h l) -> p h l", l=L),
                                         ACT.Copy).then_inc(S["a"], 1)
                    act.wait_ge(S["b_mm"], i + 1)
                    nc.scalar.activation(wq2[:, 8 * i:8 * i + 8, 0:L],
                                         bank[2 + i % 2][0:QL2, :].rearrange("p (h l) -> p h l", l=L),
                                         ACT.Copy).then_inc(S["b"], 1)

            @block.vector
            def _(dve):
                for j in range(PAIRS):
                    dve.wait_ge(S["vo_mm"], j + 1)
                    nc.vector.tensor_copy(wvo[:, j, :], bank[4 + j % 2][:]).then_inc(S["vo"], 1)

        with ExitStack() as ctx:
            def sb(name, shape, dt=FP32):
                return ctx.enter_context(nc.sbuf_tensor(f"mla_{name}", shape, dt))

            wd = sb("w_down", [P, KC, QL + L + DR])
            wd_hi = sb("w_down_hi", [P, KC, QL + L + DR], FP32R)
            wd_lo = sb("w_down_lo", [P, KC, QL + L + DR], FP32R)
            cos = sb("cos", [P, SEQ])
            sin = sb("sin", [P, SEQ])
            mask = sb("causal", [P, W])
            cq1 = sb("query_latent_low", [P, TOKENS])
            cq2 = sb("query_latent_high", [QL2, TOKENS])
            ckv = sb("latent", [P, NT, L])
            k_t = sb("keys_t", [P, TOKENS])
            q_t = sb("queries_t", [P, 3, SEQ])
            rot = sb("rotated", [P, 2, SEQ])
            sc = sb("scores", [P, 3, W])
            nmax = sb("neg_max", [P, 3, 2])
            den = sb("denominators", [P, 3, 2])
            pt = sb("probs_t", [P, 2, W])
            o_t = sb("out_t", [P, 2, PAIRS, SEQ])
            UNITS = BATCHES * H
            S = {n: chip.layer_sem(keep, "mla_" + n) for n in (
                "wd", "wd_split", "tab", "c_mm", "c", "r_mm", "kv_mm", "kv", "q_mm", "q_lat", "rot", "q_rot", "q_add", "s_mm",
                "biased", "maxed", "exped", "rden", "scaled", "p_tr", "p_copied", "pv", "o_copied", "y_mm", "y")}
            block = ctx.enter_context(nc.Block())

            KU = BATCHES

            @block.sync
            def _(sp):
                sp.dma_start(wd[:], d["w_down6"]).then_inc(S["wd"], 16)
                sp.dma_start(cos[L:P, :], d["cos6"]).then_inc(S["tab"], 16)
                sp.dma_start(sin[L:P, :], d["sin6"]).then_inc(S["tab"], 16)
                sp.dma_start(mask[:], d["causal6"]).then_inc(S["tab"], 16)

            def rope_target(i):
                if i < KU:
                    return k_t[:, i * SEQ:(i + 1) * SEQ]
                return q_t[:, (i - KU) % 3, :]

            @block.tensor
            def _(pe):
                pe.wait_ge(S["wd_split"], 2)
                for i in range(2 * NH2):
                    half, part = divmod(i, 2)
                    m = P if part == 0 else QL2
                    if i >= 2:
                        pe.wait_ge(S["c"], i - 1)
                    for k in range(KC):
                        tok, cols = slice(half * HALF, (half + 1) * HALF), slice(part * P, part * P + m)
                        ins = split_matmul(nc, bank[5 + i % 2][0:m, :], (wd_hi[:, k, cols], wd_lo[:, k, cols]),
                                           (x_hi[:, k, tok], x_lo[:, k, tok]), k == 0, k == KC - 1)
                    ins.then_inc(S["c_mm"], 1)

                def project(i):
                    if i >= 2:
                        pe.wait_ge(S["q_rot"], i - 1)
                    b = bank[i % 2][:, 0:SEQ]
                    if i < KU:
                        for k in range(KC):
                            tok = slice(i * SEQ, (i + 1) * SEQ)
                            ins = split_matmul(nc, b, (wd_hi[:, k, QL:], wd_lo[:, k, QL:]),
                                               (x_hi[:, k, tok], x_lo[:, k, tok]), k == 0, k == KC - 1)
                    else:
                        bt, h = divmod(i - KU, H)
                        tok = slice(bt * SEQ, (bt + 1) * SEQ)
                        if i == KU:
                            pe.wait_ge(S["c"], 2 * NH2)
                        nc.tensor.matmul(b, wq1[:, h, :], cq1[:, tok], start=True, stop=False)
                        ins = nc.tensor.matmul(b, wq2[:, h, :], cq2[:, tok], start=False, stop=True)
                    ins.then_inc(S["q_mm"], 1)

                def scores(u):
                    bt = u // H
                    pe.wait_ge(S["q_add"], KU + u + 1)
                    pe.wait_ge(S["q_rot"], KU + u + 1)
                    if u >= 2:
                        pe.wait_ge(S["biased"], u - 1)
                    q, k = q_t[:, u % 3, :], k_t[:, bt * SEQ:(bt + 1) * SEQ]
                    nc.tensor.matmul(bank[2 + u % 2][:, 0:P], q[:, 0:P], k[:, 0:P], start=True, stop=True)
                    nc.tensor.matmul(bank[2 + u % 2][:, P:W], q[:, P:SEQ], k, start=True, stop=True).then_inc(
                        S["s_mm"], 1)

                def transposes(u):
                    pe.wait_ge(S["scaled"], u + 1)
                    if u >= 1:
                        pe.wait_ge(S["p_copied"], u)
                    p = sc[:, u % 3, :]
                    nc.tensor.transpose(bank[4][:, 0:P], p[:, 0:P], ident[:])
                    nc.tensor.transpose(bank[4][:, P:2 * P], p[:, P:2 * P], ident[:])
                    nc.tensor.transpose(bank[4][:, 2 * P:W], p[:, 2 * P:W], ident[:]).then_inc(S["p_tr"], 1)

                def values(u):
                    bt, h = divmod(u, H)
                    pe.wait_ge(S["p_copied"], u + 1)
                    if u >= 2:
                        pe.wait_ge(S["o_copied"], u - 1)
                    r = slice(L * (h % 2), L * (h % 2 + 1))
                    o = bank[5 + u % 2]
                    nc.tensor.matmul(o[r, 0:SEQ], ckv[:, 2 * bt, :], pt[:, u % 2, 0:SEQ], start=True, stop=False)
                    nc.tensor.matmul(o[r, P:SEQ], ckv[:, 2 * bt + 1, :], pt[:, u % 2, SEQ:W], start=False,
                                     stop=True).then_inc(S["pv"], 1)

                def result(bt, t):
                    pe.wait_ge(S["o_copied"], H * (bt + 1))
                    n = 2 * bt + t
                    if n >= 1:
                        pe.wait_ge(S["y"], n)
                    for j in range(PAIRS):
                        ins = nc.tensor.matmul(bank[7][:], o_t[:, bt % 2, j, t * P:(t + 1) * P], wvo[:, j, :],
                                               start=(j == 0), stop=(j == PAIRS - 1))
                    ins.then_inc(S["y_mm"], 1)

                for i in range(KU + 2):
                    project(i)
                pe.wait_ge(S["q_rot"], KU)
                for t in range(NT):
                    ins = nc.tensor.transpose(bank[7][:, t * L:(t + 1) * L], k_t[0:L, t * P:(t + 1) * P],
                                              ident[0:L, 0:L])
                ins.then_inc(S["kv_mm"], 1)
                pe.wait_ge(S["kv"], 1)
                for u in range(UNITS + 3):
                    if u < UNITS:
                        scores(u)
                        if u + 2 < UNITS:
                            project(KU + u + 2)
                    if 2 <= u < UNITS + 2:
                        transposes(u - 2)
                    if u >= 3:
                        values(u - 3)
                    if u >= H and u % H in (6, 12):
                        result(u // H - 1, u % H // 12)
                result(BATCHES - 1, 0)
                result(BATCHES - 1, 1)

            @block.scalar
            def _(act):
                for i in range(2 * NH2):
                    half, part = divmod(i, 2)
                    out = (cq1 if part == 0 else cq2)[:, half * HALF:(half + 1) * HALF]
                    act.wait_ge(S["c_mm"], i + 1)
                    nc.scalar.activation(out, bank[5 + i % 2][0:(P if part == 0 else QL2), :],
                                         ACT.Copy).then_inc(S["c"], 1)
                def latent(i):
                    act.wait_ge(S["rot"], i + 1)
                    if i >= KU + 3:
                        act.wait_ge(S["s_mm"], i - KU - 2)
                    nc.scalar.activation(rope_target(i)[0:L, :], bank[i % 2][0:L, 0:SEQ], ACT.Copy).then_inc(
                        S["q_rot"], 1)

                def exp(u):
                    act.wait_ge(S["maxed"], u + 1)
                    for i, (lo, hi) in enumerate(((0, P), (P, W))):
                        ins = nc.scalar.activation(sc[:, u % 3, lo:hi], sc[:, u % 3, lo:hi], ACT.Exp,
                                                   bias=nmax[:, u % 3, i:i + 1],
                                                   accum_out=den[:, u % 3, i:i + 1])
                    ins.then_inc(S["exped"], 1)

                def copy_probs(u):
                    act.wait_ge(S["p_tr"], u + 1)
                    if u >= 2:
                        act.wait_ge(S["pv"], u - 1)
                    nc.scalar.activation(pt[:, u % 2, :], bank[4][:, 0:W], ACT.Copy).then_inc(S["p_copied"], 1)

                def copy_out(u):
                    bt, h = divmod(u, H)
                    r = slice(L * (h % 2), L * (h % 2 + 1))
                    act.wait_ge(S["pv"], u + 1)
                    if bt >= 2:
                        act.wait_ge(S["y_mm"], 2 * (bt - 1))
                    nc.scalar.activation(o_t[r, bt % 2, h // 2, :], bank[5 + u % 2][r, 0:SEQ],
                                         ACT.Copy).then_inc(S["o_copied"], 1)

                for i in range(KU + 2):
                    latent(i)
                act.wait_ge(S["kv_mm"], 1)
                nc.scalar.activation(ckv[:].rearrange("p t l -> p (t l)"), bank[7][:], ACT.Copy).then_inc(
                    S["kv"], 1)
                for u in range(UNITS + 3):
                    if u < UNITS:
                        exp(u)
                        if u + 2 < UNITS:
                            latent(KU + u + 2)
                    if 2 <= u < UNITS + 2:
                        copy_probs(u - 2)
                    if u >= 3:
                        copy_out(u - 3)

            @block.gpsimd
            def _(pool):
                for i in range(KU + UNITS):
                    pool.wait_ge(S["rot"], i + 1)
                    out = rope_target(i)[L:P, :]
                    nc.gpsimd.tensor_tensor(out, out, rot[L:P, i % 2, :], ALU.add).then_inc(S["q_add"], 1)

            @block.vector
            def _(dve):
                dve.wait_ge(S["wd"], 16)
                nc.vector.tensor_copy(wd_hi[:], wd[:]).then_inc(S["wd_split"], 1)
                dve.wait_ge(S["wd_split"], 1)
                nc.vector.tensor_tensor(wd_lo[:], wd[:], wd_hi[:].bitcast(FP32), ALU.subtract).then_inc(
                    S["wd_split"], 1)
                dve.wait_ge(S["tab"], 48)

                def rotate(i):
                    b = bank[i % 2]
                    out = rope_target(i)
                    dve.wait_ge(S["q_mm"], i + 1)
                    if i >= KU + 3:
                        dve.wait_ge(S["s_mm"], i - KU - 2)
                    if i >= 2:
                        dve.wait_ge(S["q_add"], i - 1)
                    nc.vector.tensor_tensor(out[L:P, :], b[L:P, 0:SEQ], cos[L:P, :], ALU.mult)
                    nc.vector.tensor_tensor(rot[64:96, i % 2, :], b[96:128, 0:SEQ], sin[64:96, :], ALU.mult)
                    nc.vector.tensor_tensor(rot[96:128, i % 2, :], b[64:96, 0:SEQ], sin[96:128, :],
                                            ALU.mult).then_inc(S["rot"], 1)

                def bias_and_max(u):
                    s = sc[:, u % 3, :]
                    dve.wait_ge(S["s_mm"], u + 1)
                    if u >= 3:
                        dve.wait_ge(S["p_tr"], u - 2)
                    nc.vector.scalar_tensor_tensor(out=s, in0=bank[2 + u % 2][:, 0:W], scalar=SCALE, in1=mask[:],
                                                   op0=ALU.mult, op1=ALU.add).then_inc(S["biased"], 1)
                    dve.wait_ge(S["biased"], u + 1)
                    for i, (lo, hi) in enumerate(((0, P), (P, W))):
                        ins = nc.vector.tensor_reduce(nmax[:, u % 3, i:i + 1], s[:, lo:hi], AX, ALU.max,
                                                      negate=True)
                    ins.then_inc(S["maxed"], 1)

                def normalise(u):
                    dve.wait_ge(S["exped"], u + 1)
                    nc.vector.reciprocal(den[:, u % 3, :], den[:, u % 3, :]).then_inc(S["rden"], 1)
                    dve.wait_ge(S["rden"], u + 1)
                    for i, (lo, hi) in enumerate(((0, P), (P, W))):
                        p = sc[:, u % 3, lo:hi]
                        ins = nc.vector.tensor_scalar(p, p, den[:, u % 3, i:i + 1], None, ALU.mult)
                    ins.then_inc(S["scaled"], 1)

                def copy_result(n):
                    dve.wait_ge(S["y_mm"], n + 1)
                    nc.vector.tensor_copy(branch[:, n, :], bank[7][:]).then_inc(S["y"], 1)

                for i in range(KU + 2):
                    rotate(i)
                for u in range(UNITS + 1):
                    if u < UNITS:
                        bias_and_max(u)
                        if u + 2 < UNITS:
                            rotate(KU + u + 2)
                    if u >= 1:
                        normalise(u - 1)
                    if u >= H and u % H in (7, 13):
                        copy_result(2 * (u // H - 1) + u % H // 13)
                copy_result(NT - 2)
                copy_result(NT - 1)


def moe_ffn(chip):
    nc, d, bank = chip.nc, chip.dram, chip.bank
    x_hi, x_lo, branch, ident = chip.x_hi, chip.x_lo, chip.branch, chip.ident
    E, SC = 16, 4
    U = E + SC
    UNITS = NH2 * U
    GU = KC * 2 * P
    WN = GU + C
    STAGE, RING, HR = 2, 5, 4
    LAG = 3
    with ExitStack() as ctx:
        def sb(name, shape, dt=FP32):
            return ctx.enter_context(nc.sbuf_tensor(f"moe_{name}", shape, dt))

        gw = sb("gate_w", [P, KC, E])
        gw_hi = sb("gate_w_hi", [P, KC, E], FP32R)
        gw_lo = sb("gate_w_lo", [P, KC, E], FP32R)
        stage = sb("weights", [P, STAGE, WN])
        w_hi = sb("w_hi", [P, RING, WN], FP32R)
        w_lo = sb("w_lo", [P, RING, WN], FP32R)
        sel_in = sb("row_select_in", [E, E, P])
        sel = sb("row_select", [E, E, P], FP32R)
        iota = sb("iota", [P, NT, E])
        lg_t = sb("logits_t", [E, TOKENS])
        p = sb("probs", [P, NT, E])
        r1 = sb("rank1", [P, NT, E])
        r2 = sb("rank2", [P, NT, E])
        t1 = sb("top1", [P, NT])
        t2 = sb("top2", [P, NT])
        ix = sb("index", [P, NT])
        comb_hi = sb("combine_t_hi", [E, TOKENS], FP32R)
        comb_lo = sb("combine_t_lo", [E, TOKENS], FP32R)
        act_s = sb("silu", [P, 2, HALF])
        mul = sb("product", [P, 2, HALF])
        h = sb("hidden", [P, 2, HALF])
        h_hi = sb("hidden_hi", [P, HR, HALF], FP32R)
        h_lo = sb("hidden_lo", [P, HR, HALF], FP32R)
        S = {n: chip.layer_sem(ctx, "moe_" + n) for n in (
            "in", "in2", "gw", "sel", "w0", "w1", "w_hi", "w_lo", "l_mm", "lg_t", "l_tr", "v", "exped", "comb", "c_tr",
            "c_hi", "c_lo", "g_mm", "u_mm", "b_mm", "silu", "prod", "hidden", "h_hi", "h_lo", "down", "y_mm", "y")}
        block = ctx.enter_context(nc.Block())


        def tok(n):
            return slice(n // U * HALF, (n // U + 1) * HALF)

        @block.sync
        def _(sp):
            sp.dma_start(gw[:], d["gate_w7"]).then_inc(S["in"], 16)
            for n in range(UNITS):
                if n >= STAGE:
                    sp.wait_ge(S["w_lo"], n - STAGE + 1)
                sp.dma_start(stage[:, n % STAGE], d["w7"][n % U]).then_inc(S[f"w{n % STAGE}"], 16)
                if n == 1:
                    sp.dma_start(iota[:], d["iota7"]).then_inc(S["in2"], 16)
                    sp.dma_start(sel_in[:], d["expert_select7"]).then_inc(S["in2"], 16)

        @block.gpsimd
        def _(pool):
            def weights_low(n):
                pool.wait_ge(S["w_hi"], n + 1)
                nc.gpsimd.tensor_tensor(w_lo[:, n % RING], stage[:, n % STAGE], w_hi[:, n % RING].bitcast(FP32),
                                        ALU.subtract).then_inc(S["w_lo"], 1)

            weights_low(0)
            weights_low(1)
            for n in range(UNITS):
                if n + 2 < UNITS:
                    weights_low(n + 2)
                pool.wait_ge(S["h_hi"], n + 1)
                nc.gpsimd.tensor_tensor(h_lo[:, n % HR, :], h[:, n % 2, :], h_hi[:, n % HR, :].bitcast(FP32),
                                        ALU.subtract).then_inc(S["h_lo"], 1)

        @block.tensor
        def _(pe):
            pe.wait_ge(S["gw"], 2)
            for half in range(NH2):
                t = slice(half * HALF, (half + 1) * HALF)
                for k in range(KC):
                    ins = split_matmul(nc, bank[4 + half][0:E, :], (gw_hi[:, k, :], gw_lo[:, k, :]),
                                       (x_hi[:, k, t], x_lo[:, k, t]), k == 0, k == KC - 1)
                ins.then_inc(S["l_mm"], 1)
            pe.wait_ge(S["lg_t"], NH2)
            for t in range(NT):
                ins = nc.tensor.transpose(bank[6][:, t * E:(t + 1) * E], lg_t[:, t * P:(t + 1) * P],
                                          ident[0:E, 0:E])
            ins.then_inc(S["l_tr"], 1)

            def gate_up(n):
                pe.wait_ge(S["w_lo"], n + 1)
                if n >= 2:
                    pe.wait_ge(S["hidden"], n - 1)
                for j, name in enumerate(("g_mm", "u_mm")):
                    for k in range(KC):
                        at = k * 2 * P + j * P
                        ins = split_matmul(nc, bank[2 * (n % 2) + j][:],
                                           (w_hi[:, n % RING, at:at + P], w_lo[:, n % RING, at:at + P]),
                                           (x_hi[:, k, tok(n)], x_lo[:, k, tok(n)]), k == 0, k == KC - 1)
                    ins.then_inc(S[name], 1)

            def token_weights(n):
                pe.wait_ge(S["silu"], n + 1)
                pe.wait_ge(S["sel"], 1)
                pe.wait_ge(S["c_lo"], NH2)
                split_matmul(nc, bank[2 * (n % 2)][:], (sel[:, n % U - SC, :],),
                             (comb_hi[:, tok(n)], comb_lo[:, tok(n)]), True, True).then_inc(S["b_mm"], 1)

            def down(n):
                pe.wait_ge(S["h_lo"], n + 1)
                for j in range(4):
                    if n % U == 0 and n:
                        pe.wait_ge(S["y"], j + 1)
                    a = (slice(0, P), n % HR, slice(j * P, (j + 1) * P))
                    ins = split_matmul(nc, bank[4 + j][:], (h_hi[a], h_lo[a]),
                                       (w_hi[:, n % RING, GU:], w_lo[:, n % RING, GU:]), n % U == 0,
                                       n % U == U - 1)
                    if n % U == U - 1:
                        ins.then_inc(S["y_mm"], 1)
                if n % U < U - 1:
                    ins.then_inc(S["down"], 1)
                else:
                    pe.wait_ge(S["y_mm"], 4 * (n // U + 1))
                    pe.sem_inc(S["down"], 1)

            for n in range(UNITS + LAG):
                if n < UNITS:
                    gate_up(n)
                if n == LAG - 1:
                    pe.wait_ge(S["comb"], 1)
                    for t in range(NT):
                        ins = nc.tensor.transpose(bank[4 + t // 4][0:E, (t % 4) * P:(t % 4 + 1) * P],
                                                  p[:, t, :], ident[:])
                    ins.then_inc(S["c_tr"], 1)
                if 1 <= n <= UNITS and (n - 1) % U >= SC:
                    token_weights(n - 1)
                if n >= LAG:
                    if n == LAG:
                        pe.wait_ge(S["c_lo"], NH2)
                    down(n - LAG)

        @block.scalar
        def _(act):
            for half in range(NH2):
                act.wait_ge(S["l_mm"], half + 1)
                nc.scalar.activation(lg_t[:, half * HALF:(half + 1) * HALF], bank[4 + half][0:E, :],
                                     ACT.Copy).then_inc(S["lg_t"], 1)
            act.wait_ge(S["v"], 2)
            nc.scalar.activation(p[:], p[:], ACT.Exp).then_inc(S["exped"], 1)

            def silu(n):
                act.wait_ge(S["g_mm"], n + 1)
                if n >= 2:
                    act.wait_ge(S["prod"], n - 1)
                nc.scalar.activation(act_s[:, n % 2, :], bank[2 * (n % 2)][:], ACT.Silu).then_inc(S["silu"], 1)

            for n in range(UNITS + 1):
                if n < UNITS:
                    silu(n)
                if n == LAG - 1:
                    act.wait_ge(S["c_tr"], 1)
                    for i in range(NH2):
                        nc.scalar.activation(comb_hi[:, i * HALF:(i + 1) * HALF], bank[4 + i][0:E, :],
                                             ACT.Copy).then_inc(S["c_hi"], 1)
                if n >= 1:
                    m = n - 1
                    act.wait_ge(S["hidden"], m + 1)
                    if m >= HR:
                        act.wait_ge(S["down"], m - HR + 1)
                    nc.scalar.activation(h_hi[:, m % HR, :], h[:, m % 2, :], ACT.Copy).then_inc(S["h_hi"], 1)
                if n == U + LAG - 1 or n == UNITS:
                    half = n // U - 1
                    for j in range(4):
                        act.wait_ge(S["y_mm"], 4 * half + j + 1)
                        nc.scalar.activation(branch[:, 4 * half + j, :], bank[4 + j][:], ACT.Copy).then_inc(
                            S["y"], 1)

        @block.vector
        def _(dve):
            v = [0]

            def chain(ins):
                v[0] += 1
                ins.then_inc(S["v"], 1)
                dve.wait_ge(S["v"], v[0])

            def wide(x):
                return x[:].unsqueeze(2).to_broadcast([P, NT, E])

            def weights_high(n):
                dve.wait_ge(S[f"w{n % STAGE}"], 16 * (n // STAGE + 1))
                if n >= RING:
                    dve.wait_ge(S["down"], n - RING + 1)
                nc.vector.tensor_copy(w_hi[:, n % RING], stage[:, n % STAGE]).then_inc(S["w_hi"], 1)

            tt, red = nc.vector.tensor_tensor, nc.vector.tensor_reduce
            dve.wait_ge(S["in"], 16)
            nc.vector.tensor_copy(gw_hi[:], gw[:]).then_inc(S["gw"], 1)
            dve.wait_ge(S["gw"], 1)
            tt(gw_lo[:], gw[:], gw_hi[:].bitcast(FP32), ALU.subtract).then_inc(S["gw"], 1)
            weights_high(0)
            weights_high(1)
            logits = bank[6][:, 0:NT * E].rearrange("p (t e) -> p t e", e=E)
            dve.wait_ge(S["l_tr"], 1)
            chain(red(t1[:], logits, AX, ALU.max))
            chain(tt(p[:], logits, wide(t1), ALU.subtract))
            dve.wait_ge(S["exped"], 1)
            chain(red(t1[:], p[:], AX, ALU.add))
            chain(nc.vector.reciprocal(t1[:], t1[:]))
            chain(tt(p[:], p[:], wide(t1), ALU.mult))
            dve.wait_ge(S["in2"], 32)
            for top, rank in ((t1, r1), (t2, r2)):
                chain(red(top[:], p[:], AX, ALU.max))
                chain(tt(rank[:], p[:], wide(top), ALU.is_equal))
                chain(nc.vector.scalar_tensor_tensor(out=rank[:], in0=rank[:], scalar=-100.0, in1=iota[:],
                                                     op0=ALU.mult, op1=ALU.add))
                chain(red(ix[:], rank[:], AX, ALU.min))
                chain(tt(rank[:], rank[:], wide(ix), ALU.is_equal))
                if top is t1:
                    chain(nc.vector.scalar_tensor_tensor(out=p[:], in0=rank[:], scalar=-4.0, in1=p[:],
                                                         op0=ALU.mult, op1=ALU.add))
            chain(tt(ix[:], t1[:], t2[:], ALU.add))
            chain(nc.vector.reciprocal(ix[:], ix[:]))
            chain(tt(t1[:], t1[:], ix[:], ALU.mult))
            chain(tt(t2[:], t2[:], ix[:], ALU.mult))
            chain(tt(r1[:], r1[:], wide(t1), ALU.mult))
            chain(tt(r2[:], r2[:], wide(t2), ALU.mult))
            tt(p[:], r1[:], r2[:], ALU.add).then_inc(S["comb"], 1)
            nc.vector.tensor_copy(sel[:], sel_in[:]).then_inc(S["sel"], 1)
            routed = 0
            for n in range(UNITS):
                if n + 2 < UNITS:
                    weights_high(n + 2)
                if n == LAG - 1:
                    for i in range(NH2):
                        t = slice(i * HALF, (i + 1) * HALF)
                        dve.wait_ge(S["c_hi"], i + 1)
                        tt(comb_lo[:, t], bank[4 + i][0:E, :], comb_hi[:, t].bitcast(FP32),
                           ALU.subtract).then_inc(S["c_lo"], 1)
                dve.wait_ge(S["silu"], n + 1)
                dve.wait_ge(S["u_mm"], n + 1)
                if n >= 2:
                    dve.wait_ge(S["h_lo"], n - 1)
                if n % U < SC:
                    tt(h[:, n % 2, :], act_s[:, n % 2, :], bank[2 * (n % 2) + 1][:], ALU.mult).then_inc(
                        S["hidden"], 1)
                    dve.wait_ge(S["hidden"], n + 1)
                    dve.sem_inc(S["prod"], 1)
                else:
                    tt(mul[:, n % 2, :], act_s[:, n % 2, :], bank[2 * (n % 2) + 1][:], ALU.mult).then_inc(
                        S["prod"], 1)
                    dve.wait_ge(S["prod"], n + 1)
                    dve.wait_ge(S["b_mm"], routed + 1)
                    tt(h[:, n % 2, :], mul[:, n % 2, :], bank[2 * (n % 2)][:], ALU.mult).then_inc(
                        S["hidden"], 1)
                    routed += 1


LAYER_BUILDERS = [gqa_attention, int8_ffn, selective_scan, table_linear, head_mixer, routed_lora, latent_attention, moe_ffn]
LAST_LAYERS = 8


def sandwich(nc, dram):
    with ExitStack() as ctx:
        chip = Chip(nc, ctx, dram)
        add_and_norm(chip)
        for n, layer in enumerate(LAYER_BUILDERS[:LAST_LAYERS]):
            layer(chip)
            if n == 0:
                chip.place_stream()
            add_and_norm(chip)


def _chunks(w):
    k, n = w.shape
    return np.ascontiguousarray(w.reshape(k // P, P, n).transpose(1, 0, 2))


def _layout(a):
    out = {}
    out["x"] = a["L0_attn_x"].reshape(NT, P, C)
    out["ident"] = np.eye(P, dtype=np.float32)
    wq, wk, wv, wo = (_chunks(a["L0_attn_W" + n].T) for n in "qkvo")
    q0 = wq.reshape(P, KC, 8, 512).transpose(2, 0, 1, 3).reshape(8, P, -1)
    kv0 = np.concatenate([wk.reshape(P, KC, 8, P), wv.reshape(P, KC, 8, P)], -1)
    out["Wqkv0"] = np.concatenate([q0, kv0.transpose(2, 0, 1, 3).reshape(8, P, -1)], -1)
    out["Wo0"] = wo.reshape(P, 8, 4 * C).transpose(1, 0, 2)
    out["qk_norm_w"] = np.stack([a["L0_attn_q_norm_w"], a["L0_attn_k_norm_w"]], 1)
    i, j = np.arange(P)[:, None], np.arange(SEQ)[None]
    rel = np.concatenate([j[:, :P] - i, j - i - P], 1).astype(np.float32)
    out["alibi_rel"] = np.where(rel > 0, np.float32(-1e33), rel)
    def pad_rows(w, n):
        return np.concatenate([w, np.zeros((n - w.shape[0],) + w.shape[1:], w.dtype)])
    out["gate1"] = _chunks(a["L0_ffn_gate_wq"].T)
    out["up1"] = _chunks(a["L0_ffn_up_wq"].T)
    out["down1"] = _chunks(pad_rows(a["L0_ffn_down_wq"].T, 11 * P))
    out["scales1"] = np.stack([pad_rows(a[f"L0_ffn_{n}_scale"], 11 * P).reshape(11, P).T
                               for n in ("gate", "up")], 1)
    out["down_scale1"] = np.broadcast_to(a["L0_ffn_down_scale"], (P, C))
    out["x_proj2"] = _chunks(a["L1_attn_x_proj_w"].T)
    out["dt_proj2"] = a["L1_attn_dt_proj_w"].T
    out["dt_bias2"] = a["L1_attn_dt_proj_b"].reshape(KC, P).T
    out["a_log2"] = _chunks(a["L1_attn_A_log"])
    out["d2"] = a["L1_attn_D"].reshape(KC, P).T
    row = np.zeros((48, 32, P), np.float32)
    row[np.arange(16, 48), np.arange(32)] = 1
    out["row_select2"] = row
    q = a["L1_ffn_qweight"][:4]
    out["planes3"] = q.reshape(4, KC, P, 16).transpose(2, 0, 1, 3).reshape(P, 4, KC * 16)
    out["lut3"] = _chunks(a["L1_ffn_lut4"])
    out["bias3"] = np.broadcast_to(a["L1_ffn_bias"], (P, C))
    out["Wqkv4"] = np.stack([_chunks(a[f"L2_attn_W{n}"].T) for n in "qkv"], 1)
    out["Wo4"] = _chunks(a["L2_attn_Wo"].T)
    out["bias4"] = np.stack([a[f"L2_attn_b{n}"] for n in "qkvo"])[None]
    lora_a = a["L2_ffn_A"].reshape(32, C)
    out["small5"] = _chunks(np.concatenate([lora_a, a["L2_ffn_Wr"]]).T)
    out["W5"] = _chunks(a["L2_ffn_W"].T)
    out["Bm5"] = a["L2_ffn_Bm"].transpose(0, 2, 1).reshape(32, C)
    out["bias5"] = np.broadcast_to(a["L2_ffn_b"], (P, C))
    out["w_q_up_nope_t6"] = a["L3_attn_w_q_up_nope"].reshape(192, 32, P).transpose(2, 1, 0)
    out["w_uk6"] = a["L3_attn_w_uk"].reshape(32, P, 64).transpose(1, 0, 2)
    out["w_uv6"] = a["L3_attn_w_uv"].reshape(32, P, 64).transpose(1, 0, 2)
    out["w_out6"] = a["L3_attn_w_out"].reshape(32, P, C).transpose(1, 0, 2)
    rope = a["L3_attn_w_q_up_rope"].reshape(192, 32, 64)
    out["w_q_up_rope_low6"], out["w_q_up_rope_high6"] = rope[:P], rope[P:]
    out["w_down6"] = _chunks(np.concatenate(
        [a["L3_attn_w_q_down"], a["L3_attn_w_kv_down"], a["L3_attn_w_k_rope"]], 1))
    f32 = np.float32
    freqs = f32(1) / np.power(f32(10000.0), np.arange(0, 64, 2, dtype=f32) / f32(64))
    ramp = np.clip((f32(2 * np.pi) / freqs / f32(4096.0) - f32(1)) / f32(31.0), f32(0), f32(1))
    inv = (freqs / (f32(1) - ramp + ramp * f32(40.0))).astype(f32)
    ang = inv[:, None] * np.arange(SEQ, dtype=f32)[None]
    out["cos6"] = np.concatenate([np.cos(ang)] * 2).astype(f32)
    out["sin6"] = np.concatenate([-np.sin(ang), np.sin(ang)]).astype(f32)
    out["causal6"] = np.where(rel > 0, f32(-1e30), f32(0))
    out["gate_w7"] = _chunks(a["L3_ffn_gate_w"].T)
    gu = a["L3_ffn_w_gate_up"].transpose(0, 2, 1).reshape(16, KC, P, 256)
    sg = a["L3_ffn_shared_w_gate_up"].T.reshape(KC, P, 2, 4, P).transpose(3, 0, 1, 2, 4).reshape(4, KC, P, 256)
    gu = np.concatenate([sg, gu]).transpose(0, 2, 1, 3).reshape(20, P, -1)
    down = np.concatenate([a["L3_ffn_shared_w_down"].T.reshape(4, P, C), a["L3_ffn_w_down"].transpose(0, 2, 1)])
    out["w7"] = np.concatenate([gu, down], 2)
    row = np.zeros((16, 16, P), np.float32)
    row[np.arange(16), np.arange(16)] = 1
    out["expert_select7"] = row
    out["iota7"] = np.broadcast_to(np.arange(16, dtype=np.float32), (P, NT, 16))
    return {k: np.ascontiguousarray(v) for k, v in out.items()}


def kernel(**inputs):
    import concourse.bacc as bacc
    from concourse.bass_utils import run_bass_kernel_spmd

    nc = bacc.Bacc("TRN2", target_bir_lowering=False, num_devices=1)
    arrays = _layout({k: np.asarray(v) for k, v in inputs.items()})
    dram = {k: nc.dram_tensor("in_" + k, v.shape, mybir.dt.from_np(v.dtype), kind="ExternalInput").ap()
            for k, v in arrays.items()}
    dram["out"] = nc.dram_tensor("out_x", (NT, P, C), FP32, kind="ExternalOutput").ap()
    sandwich(nc, dram)
    r = run_bass_kernel_spmd(nc, [{"in_" + k: v for k, v in arrays.items()}], core_ids=[0])
    return r.results[0]["out_x"].reshape(BATCHES, SEQ, C)
```

```python
import math
from contextlib import ExitStack

import numpy as np

import concourse.bass as bass
from concourse import mybir

FP32 = mybir.dt.float32
FP32R = mybir.dt.float32r
I32 = mybir.dt.int32
ALU = mybir.AluOpType
ACT = mybir.ActivationFunctionType
AX = mybir.AxisListType.X

P = 128
TOKENS, C = 1024, 512
BATCHES, SEQ = 4, 256
NT = TOKENS // P
KC = C // P
HALF = 512
NH2 = TOKENS // HALF
LN_EPS = 1e-5
LAYERS = 8


class Chip:

    def __init__(self, nc, ctx, dram):
        self.nc, self.ctx, self.dram = nc, ctx, dram
        self.bank = [ctx.enter_context(nc.psum_tensor(f"bank{i}", [P, 512], FP32)) for i in range(8)]
        self.branch = ctx.enter_context(nc.sbuf_tensor("branch", [P, NT, C], FP32))
        self.x_hi = ctx.enter_context(nc.sbuf_tensor("x_hi", [P, KC, TOKENS], FP32R))
        self.x_lo = ctx.enter_context(nc.sbuf_tensor("x_lo", [P, KC, TOKENS], FP32R))
        self.ident = ctx.enter_context(nc.sbuf_tensor("ident", [P, P], FP32))
        self.stats = ctx.enter_context(nc.sbuf_tensor("branch_sums", [P, NT, 6], FP32))
        self.mean_var = ctx.enter_context(nc.sbuf_tensor("branch_mean_var", [P, NT, 2], FP32))
        self.norms = 0
        self.seen = 0
        self.norm_ticks = 0
        self.x_loaded = [self.sem(f"x_loaded{t}") for t in range(NT)]
        self.spent = []
        self.norm_sems = {n: self.sem("norm_" + n) for n in (
            "loaded", "seen", "branch_stats", "branch_dev", "shift", "applied", "stream_stats", "stream_dev",
            "inverse", "tile_ready", "transposed", "stored", "dve", "copied", "bias")}

    def place_stream(self):
        self.stream = self.ctx.enter_context(self.nc.sbuf_tensor("stream", [P, NT, C], FP32))

    def sem(self, name):
        return self.ctx.enter_context(self.nc.semaphore(name))

    def layer_sem(self, scope, name):
        self.spent.append(scope.enter_context(self.nc.semaphore(name)))
        return self.spent[-1]


class Early:

    def __init__(self, sync, gpsimd, scalar, sems, tensors):
        self.sync, self.gpsimd, self.scalar, self.sems, self.tensors = sync, gpsimd, scalar, sems, tensors


def no_part(engine, part=0):
    pass


def branch_stats(chip, dve, t, written, count):
    s = chip.norm_sems
    dve.wait_ge(written, count)
    chip.nc.vector.bn_stats(chip.stats[:, t, :], chip.branch[:, t, :]).then_inc(s["seen"], 1)
    chip.seen += 1
    dve.wait_ge(s["seen"], chip.seen)
    chip.nc.vector.bn_aggr(chip.mean_var[:, t, :], chip.stats[:, t, :]).then_inc(s["branch_stats"], 1)


def split_matmul(nc, out, lhs, rhs, start, stop):
    passes = [(0, 0)] + [(0, 1)] * (len(rhs) > 1) + [(1, 0)] * (len(lhs) > 1)
    for n, (i, j) in enumerate(passes):
        last = n == len(passes) - 1
        ins = nc.tensor.matmul(out, lhs[i], rhs[j], start=start and n == 0, stop=stop and last)
    return ins


def add_and_norm(chip, early=None):
    nc, s, n = chip.nc, chip.norm_sems, chip.norms
    first, last = n == 0, n == LAST_LAYERS
    chip.norms += 1
    branch, ident, bank = chip.branch, chip.ident, chip.bank
    posts = NT * (n - 1)
    pres = NT * n
    with ExitStack() as ctx:
        def sb(name, shape, dt=FP32):
            return ctx.enter_context(nc.sbuf_tensor(f"norm{n}_{name}", shape, dt))

        stats = sb("stats", [P, NT, 6])
        bmv = chip.mean_var
        smv = sb("stream_mean_var", [P, NT, 2])
        bdev = sb("branch_dev", [P, NT])
        bshift = sb("branch_shift", [P, NT])
        sdev = sb("stream_dev", [P, NT])
        sshift = sb("stream_shift", [P, NT])
        tmp = sb("normed", [P, NT, C])
        stream = sb("x", [P, NT, C]) if first else chip.stream
        eps = sb("eps", [P, 1])
        PART = NT // 2
        block = ctx.enter_context(nc.Block())

        @block.gpsimd
        def _(pool):
            for spent in chip.spent:
                pool.sem_clear(spent)
            chip.spent = []
            if early:
                early.gpsimd(pool)

        @block.sync
        def _(sp):
            if n <= 1:
                for t in range(NT):
                    sp.dma_start(stream[:, t, :], chip.dram["x"][t]).then_inc(chip.x_loaded[t], 16)
            if first:
                sp.dma_start(ident[:], chip.dram["ident"]).then_inc(s["loaded"], 16)
            if early:
                early.sync(sp)
            if last:
                for t in range(NT):
                    sp.wait_ge(s["tile_ready"], pres + t + 1)
                    sp.dma_start(chip.dram["out"][t], stream[:, t, :]).then_inc(s["stored"], 16)
                sp.wait_ge(s["stored"], 16 * NT)

        @block.vector
        def _(dve):
            ticks = [chip.norm_ticks]

            def tick(ins):
                ticks[0] += 1
                ins.then_inc(s["dve"], 1)
                return ticks[0]

            nc.vector.memset(eps[:], LN_EPS).then_inc(s["bias"], 1)

            def invert(dev, mv, shift, tiles):
                t = tick(nc.vector.reciprocal(dev[:, tiles], dev[:, tiles]))
                dve.wait_ge(s["dve"], t)
                return nc.vector.scalar_tensor_tensor(out=shift[:, tiles], in0=mv[:, tiles, 0], scalar=-1.0,
                                                      in1=dev[:, tiles], op0=ALU.mult, op1=ALU.mult)

            def stream_stats(t, written):
                if first:
                    dve.wait_ge(chip.x_loaded[t], 16)
                else:
                    dve.wait_ge(s["dve"], written)
                return tick(nc.vector.bn_stats(stats[:, t, :], stream[:, t, :]))

            if not first:
                dve.wait_ge(s["branch_dev"], n)
                invert(bdev, bmv, bshift, slice(0, NT)).then_inc(s["shift"], 1)
            for part in range(2):
                tiles = range(part * PART, (part + 1) * PART)
                written, seen = {}, {}
                for t in (*tiles, None):
                    if t is not None and not first:
                        dve.wait_ge(s["applied"], posts + t + 1)
                        if n == 1:
                            dve.wait_ge(chip.x_loaded[t], 32)
                        ins = nc.vector.tensor_tensor(stream[:, t, :], stream[:, t, :], tmp[:, t, :], ALU.add)
                        if last:
                            ins.then_inc(s["tile_ready"], 1)
                        else:
                            written[t] = tick(ins)
                    if not last:
                        b = tiles[-1] if t is None else t - 1
                        if b >= tiles[0]:
                            seen[b] = stream_stats(b, written.get(b))
                if not last:
                    for t in tiles:
                        dve.wait_ge(s["dve"], seen[t])
                        nc.vector.bn_aggr(smv[:, t, :], stats[:, t, :]).then_inc(s["stream_stats"], 1)
                    dve.wait_ge(s["stream_dev"], 2 * n + part + 1)
                    invert(sdev, smv, sshift, slice(part * PART, (part + 1) * PART)).then_inc(s["inverse"], 1)
            if not last:
                for t in range(NT):
                    dve.wait_ge(s["copied"], pres + t + 1)
                    nc.vector.tensor_tensor(chip.x_lo[:, :, t * P:(t + 1) * P],
                                            bank[t % 8][:].rearrange("p (k m) -> p k m", k=KC),
                                            chip.x_hi[:, :, t * P:(t + 1) * P].bitcast(FP32), ALU.subtract)
            chip.norm_ticks = ticks[0]

        @block.scalar
        def _(act):
            act.wait_ge(s["bias"], n + 1)
            if not first:
                act.wait_ge(s["branch_stats"], posts + NT)
                nc.scalar.activation(bdev[:], bmv[:, :, 1], ACT.Sqrt, bias=eps[:]).then_inc(s["branch_dev"], 1)
                act.wait_ge(s["shift"], n)
                for t in range(NT):
                    nc.scalar.activation(tmp[:, t, :], branch[:, t, :], ACT.Identity, bias=bshift[:, t:t + 1],
                                         scale=bdev[:, t:t + 1]).then_inc(s["applied"], 1)

            def normalise(part):
                tiles = slice(part * PART, (part + 1) * PART)
                act.wait_ge(s["stream_stats"], pres + (part + 1) * PART)
                nc.scalar.activation(sdev[:, tiles], smv[:, tiles, 1], ACT.Sqrt, bias=eps[:]).then_inc(
                    s["stream_dev"], 1)
                act.wait_ge(s["inverse"], 2 * n + part + 1)
                for t in range(part * PART, (part + 1) * PART):
                    nc.scalar.activation(tmp[:, t, :], stream[:, t, :], ACT.Identity, bias=sshift[:, t:t + 1],
                                         scale=sdev[:, t:t + 1]).then_inc(s["tile_ready"], 1)

            def copy_high(part):
                for t in range(part * PART, (part + 1) * PART):
                    act.wait_ge(s["transposed"], pres + t + 1)
                    nc.scalar.activation(chip.x_hi[:, :, t * P:(t + 1) * P],
                                         bank[t % 8][:].rearrange("p (k m) -> p k m", k=KC),
                                         ACT.Copy).then_inc(s["copied"], 1)

            if not last:
                for part in range(2):
                    normalise(part)
                    if early:
                        early.scalar(act, part)
                    copy_high(part)

        @block.tensor
        def _(pe):
            if not last:
                if first:
                    pe.wait_ge(s["loaded"], 16)
                for t in range(NT):
                    pe.wait_ge(s["tile_ready"], pres + t + 1)
                    for k in range(KC):
                        ins = nc.tensor.transpose(bank[t % 8][:, k * P:(k + 1) * P],
                                                  tmp[:, t, k * P:(k + 1) * P], ident[:])
                    ins.then_inc(s["transposed"], 1)


def gqa_attention(chip):
    nc, d, bank = chip.nc, chip.dram, chip.bank
    x_hi, x_lo, branch, ident = chip.x_hi, chip.x_lo, chip.branch, chip.ident
    GROUPS, G, HD = 8, 4, 128
    UNITS = BATCHES * G
    W = P + SEQ
    EPS = 1e-6
    start = 2 ** (-2 ** (-(math.log2(GROUPS * G) - 3)))
    slopes = [start * start ** i for i in range(GROUPS * G)]
    VALS = 3
    AHEAD = 2
    with ExitStack() as ctx:
        def sb(name, shape, dt=FP32):
            return ctx.enter_context(nc.sbuf_tensor(f"gqa_{name}", shape, dt))

        QKV = KC * (G * HD + 2 * HD)
        WO = G * C
        stage = sb("weights", [P, QKV])
        w_hi = sb("w_qkv_hi", [P, QKV], FP32R)
        w_lo = sb("w_qkv_lo", [P, QKV], FP32R)
        wo_hi = sb("wo_hi", [P, WO], FP32R)
        wo_lo = sb("wo_lo", [P, WO], FP32R)
        q_t = sb("q_t", [P, 2, G, TOKENS])
        q_sq = sb("q_sq", [P, HALF])
        q_sq_hi = sb("q_sq_hi", [P, 2, HALF], FP32R)
        q_sq_lo = sb("q_sq_lo", [P, 2, HALF], FP32R)
        pick = sb("one_hot", [P, G * NH2, G * NH2], FP32R)
        ssq_t = sb("ssq_t", [G * NH2, HALF])
        keys = sb("keys", [P, NT, HD])
        vals = sb("vals", [P, VALS, NT, HD])
        k_sq = sb("k_sq", [P, HD])
        k_t = sb("k_t", [P, 2, TOKENS])
        kss = sb("kss", [P, 2, NT])
        kinv = sb("kinv", [P, 2, NT])
        qinv = sb("qinv", [P, 2, NT * G])
        nw = sb("norm_weights", [P, 2])
        kw = sb("key_scale", [P, 1])
        eps = sb("eps", [P, 1])
        rel = sb("relative", [P, W])
        alibi = sb("alibi", [P, 2, G, W])
        sc = sb("scores", [P, 3, W])
        nmax = sb("neg_max", [P, 3, 2])
        den = sb("denominators", [P, 3, 2])
        pt = sb("probs_t", [P, 2, W])
        o_hi = sb("out_t_hi", [P, 2, G, SEQ], FP32R)
        o_lo = sb("out_t_lo", [P, 2, G, SEQ], FP32R)
        S = {n: chip.layer_sem(ctx, "gqa_" + n) for n in (
            "w", "w_hi", "w_lo", "wo_hi", "wo_lo", "small", "kw", "kw0", "ready", "alibi", "sq", "sq_hi",
            "ssq_t", "ssq_tr", "o_hi", "kv_mm", "k_copied", "kv_copied", "kss",
            "q_mm", "q_copied", "q_sq", "ssq", "root", "inv", "k_scaled", "k_tr", "k_t", "s_mm",
            "biased", "maxed", "exped", "rden", "scaled", "p_tr", "p_copied", "pv", "o_copied", "y_mm",
            "y_added")}
        block = ctx.enter_context(nc.Block())


        @block.sync
        def _(sp):
            sp.dma_start(nw[:], d["qk_norm_w"]).then_inc(S["small"], 16)
            sp.dma_start(rel[:], d["alibi_rel"]).then_inc(S["small"], 16)
            sp.dma_start(stage[:], d["Wqkv0"][0]).then_inc(S["w"], 16)
            for g in range(GROUPS):
                if g + 1 < GROUPS:
                    sp.wait_ge(S["w_lo"], g + 1)
                    if g:
                        sp.wait_ge(S["wo_lo"], g)
                    sp.dma_start(stage[:], d["Wqkv0"][g + 1]).then_inc(S["w"], 16)
                    sp.wait_ge(S["w_lo"], g + 2)
                else:
                    sp.wait_ge(S["wo_lo"], g)
                sp.dma_start(stage[:, 0:WO], d["Wo0"][g]).then_inc(S["w"], 16)

        @block.gpsimd
        def _(pool):
            pool.wait_ge(S["small"], 32)

            def qkv_low(g):
                pool.wait_ge(S["w_hi"], g + 1)
                nc.gpsimd.tensor_tensor(w_lo[:], stage[:], w_hi[:].bitcast(FP32), ALU.subtract).then_inc(
                    S["w_lo"], 1)

            def out_low(g):
                pool.wait_ge(S["wo_hi"], g + 1)
                nc.gpsimd.tensor_tensor(wo_lo[:], stage[:, 0:WO], wo_hi[:].bitcast(FP32),
                                        ALU.subtract).then_inc(S["wo_lo"], 1)

            def biases(g):
                for h in range(G):
                    if g >= 2:
                        pool.wait_ge(S["biased"], UNITS * (g - 1))
                    nc.gpsimd.tensor_scalar(alibi[:, g % 2, h, :], rel[:], slopes[g * G + h], None,
                                            ALU.mult).then_inc(S["alibi"], 1)

            def squares(g):
                for i in range(G * NH2):
                    n = G * NH2 * g + i
                    pool.wait_ge(S["q_copied"], n + 1)
                    if n:
                        pool.wait_ge(S["q_sq"], n)
                    q = q_t[:, g % 2, i // NH2, (i % NH2) * HALF:(i % NH2 + 1) * HALF]
                    nc.gpsimd.tensor_tensor(q_sq[:], q, q, ALU.mult).then_inc(S["sq"], 1)
                    pool.wait_ge(S["sq_hi"], n + 1)
                    if n >= 2:
                        pool.wait_ge(S["ssq"], n - 1)
                    nc.gpsimd.tensor_tensor(q_sq_lo[:, n % 2, :], q_sq[:], q_sq_hi[:, n % 2, :].bitcast(FP32),
                                            ALU.subtract).then_inc(S["q_sq"], 1)

            qkv_low(0)
            biases(0)
            squares(0)
            qkv_low(1)
            for g in range(GROUPS):
                if g + 1 < GROUPS:
                    biases(g + 1)
                out_low(g)
                if g + 1 < GROUPS:
                    squares(g + 1)
                if g + 2 < GROUPS:
                    qkv_low(g + 2)

        def unit(u):
            g, r = divmod(u, UNITS)
            return g, r // G, r % G

        ALL = GROUPS * UNITS
        Q, SSQ, KTR, TAIL = NT // 2, NT // 2 + 2, NT // 2 + G * NH2, NT // 2 + G * NH2 + 2
        SPLIT_OUT, SPLIT_QKV = AHEAD + 3, TAIL - 1

        def output_of(v):
            if v < G or v % G > 1:
                return None
            return (*divmod(v // G - 1, BATCHES), v % G)

        def query_weights(w, k, h):
            return w[:, k * G * HD + h * HD:k * G * HD + (h + 1) * HD]

        def key_value_weights(w, k):
            at = KC * G * HD + k * 2 * HD
            return w[:, at:at + 2 * HD]

        def wait_projection_bank(pe, g, i):
            if i >= 2:
                if i - 2 < NT:
                    pe.wait_ge(S["kv_copied"], NT * g + i - 1)
                else:
                    pe.wait_ge(S["q_copied"], G * NH2 * g + i - 2 - NT + 1)
            elif g >= 1:
                pe.wait_ge(S["k_t"], 2 * (g - 1) + i + 1)

        @block.tensor
        def _(pe):
            def project(g, step):
                if step < Q:
                    if step == 0:
                        pe.wait_ge(S["w_lo"], g + 1)
                    for t in (2 * step, 2 * step + 1):
                        tok = slice(t * P, (t + 1) * P)
                        wait_projection_bank(pe, g, t)
                        for c in range(KC):
                            ins = split_matmul(nc, bank[t % 2][:, 0:2 * HD], (x_hi[:, c, tok], x_lo[:, c, tok]),
                                               (key_value_weights(w_hi, c), key_value_weights(w_lo, c)),
                                               c == 0, c == KC - 1)
                        ins.then_inc(S["kv_mm"], 1)
                elif step < KTR:
                    i = step - Q
                    h, half = divmod(i, NH2)
                    tok = slice(half * HALF, (half + 1) * HALF)
                    wait_projection_bank(pe, g, NT + i)
                    for c in range(KC):
                        ins = split_matmul(nc, bank[i % 2][:], (query_weights(w_hi, c, h),
                                                                query_weights(w_lo, c, h)),
                                           (x_hi[:, c, tok], x_lo[:, c, tok]), c == 0, c == KC - 1)
                    ins.then_inc(S["q_mm"], 1)
                elif step < TAIL:
                    j = step - KTR
                    pe.wait_ge(S["k_scaled"], NT * g + 4 * (j + 1))
                    pe.wait_ge(S["q_copied"], G * NH2 * (g + 1) - 1 + j)
                    for t in range(4):
                        ins = nc.tensor.transpose(bank[j][:, t * P:(t + 1) * P], keys[:, 4 * j + t, :],
                                                  ident[:])
                    ins.then_inc(S["k_tr"], 1)
                if SSQ <= step < SSQ + G * NH2:
                    sum_squares(g, step - SSQ)
                if step == TAIL:
                    pe.wait_ge(S["ssq_t"], g + 1)
                    for t in range(HALF // P):
                        n = G * NH2
                        ins = nc.tensor.transpose(bank[2][:, t * n:(t + 1) * n], ssq_t[:, t * P:(t + 1) * P],
                                                  ident[0:n, 0:n])
                    ins.then_inc(S["ssq_tr"], 1)

            def sum_squares(g, i):
                n = G * NH2 * g + i
                pe.wait_ge(S["q_sq"], n + 1)
                if g >= 1 and i == 0:
                    pe.wait_ge(S["root"], 2 * g)
                split_matmul(nc, bank[2][0:G * NH2, :], (pick[:, i, :],),
                             (q_sq_hi[:, n % 2, :], q_sq_lo[:, n % 2, :]), i == 0,
                             i == G * NH2 - 1).then_inc(S["ssq"], 1)

            def scores(u):
                g, b, h = unit(u)
                if u % UNITS == 0:
                    pe.wait_ge(S["k_t"], 2 * (g + 1))
                    pe.wait_ge(S["q_copied"], G * NH2 * (g + 1))
                if u >= 2:
                    pe.wait_ge(S["biased"], u - 1)
                qs = q_t[:, g % 2, h, b * SEQ:(b + 1) * SEQ]
                ks = k_t[:, g % 2, b * SEQ:(b + 1) * SEQ]
                nc.tensor.matmul(bank[3 + u % 2][:, 0:P], qs[:, 0:P], ks[:, 0:P], start=True, stop=True)
                nc.tensor.matmul(bank[3 + u % 2][:, P:W], qs[:, P:SEQ], ks, start=True,
                                 stop=True).then_inc(S["s_mm"], 1)

            def transposes(u):
                pe.wait_ge(S["scaled"], u + 1)
                if u >= 1:
                    pe.wait_ge(S["p_copied"], u)
                p = sc[:, u % 3, :]
                nc.tensor.transpose(bank[5][:, 0:P], p[:, 0:P], ident[:])
                nc.tensor.transpose(bank[5][:, P:2 * P], p[:, P:2 * P], ident[:])
                nc.tensor.transpose(bank[5][:, 2 * P:W], p[:, 2 * P:W], ident[:]).then_inc(S["p_tr"], 1)

            def values(u):
                g, b, h = unit(u)
                pe.wait_ge(S["p_copied"], u + 1)
                if u >= 1:
                    pe.wait_ge(S["o_copied"], u)
                nc.tensor.matmul(bank[6][:, 0:SEQ], vals[:, g % VALS, 2 * b, :], pt[:, u % 2, 0:SEQ],
                                 start=True, stop=False)
                nc.tensor.matmul(bank[6][:, P:SEQ], vals[:, g % VALS, 2 * b + 1, :], pt[:, u % 2, SEQ:W],
                                 start=False, stop=True).then_inc(S["pv"], 1)

            def output(g, b, t):
                if b == 0 and t == 0:
                    pe.wait_ge(S["wo_lo"], g + 1)
                nb = BATCHES * g + b
                if t == 0:
                    pe.wait_ge(S["o_copied"], G * (nb + 1))
                if 2 * nb + t >= 1:
                    pe.wait_ge(S["y_added"], 2 * nb + t)
                for h in range(G):
                    tok, cols = slice(t * P, (t + 1) * P), slice(h * C, (h + 1) * C)
                    ins = split_matmul(nc, bank[7][:], (o_hi[:, nb % 2, h, tok], o_lo[:, nb % 2, h, tok]),
                                       (wo_hi[:, cols], wo_lo[:, cols]), h == 0, h == G - 1)
                ins.then_inc(S["y_mm"], 1)

            pe.wait_ge(S["ready"], 2)
            for step in range(UNITS):
                project(0, step)
            for u in range(ALL + AHEAD + 3):
                if u < ALL:
                    scores(u)
                if u < ALL and u // UNITS + 1 < GROUPS:
                    project(u // UNITS + 1, u % UNITS)
                if 0 <= u - AHEAD < ALL:
                    transposes(u - AHEAD)
                v = u - AHEAD - 1
                if 0 <= v < ALL:
                    values(v)
                if output_of(v):
                    output(*output_of(v))

        @block.scalar
        def _(act):
            def project(g, step):
                b = g % 2
                if step < Q:
                    for t in (2 * step, 2 * step + 1):
                        act.wait_ge(S["kv_mm"], NT * g + t + 1)
                        if t == 0 and g:
                            act.wait_ge(S["k_tr"], 2 * g)
                        if t == 0 and g >= VALS:
                            act.wait_ge(S["pv"], UNITS * (g - VALS + 1))
                        nc.scalar.activation(keys[:, t, :], bank[t % 2][:, 0:HD], ACT.Copy).then_inc(
                            S["k_copied"], 1)
                        nc.scalar.activation(vals[:, g % VALS, t, :], bank[t % 2][:, HD:2 * HD],
                                             ACT.Copy).then_inc(S["kv_copied"], 1)
                        act.wait_ge(S["k_copied"], NT * g + t + 1)
                        if t or g:
                            act.wait_ge(S["kss"], NT * g + t)
                        nc.scalar.activation(k_sq[:], keys[:, t, :], ACT.Square,
                                             accum_out=kss[:, b, t:t + 1]).then_inc(S["kss"], 1)
                elif step < KTR:
                    i = step - Q
                    h, half = divmod(i, NH2)
                    act.wait_ge(S["q_mm"], G * NH2 * g + i + 1)
                    if g >= 2 and i == 0:
                        act.wait_ge(S["s_mm"], UNITS * (g - 1))
                    nc.scalar.activation(q_t[:, b, h, half * HALF:(half + 1) * HALF], bank[i % 2][:],
                                         ACT.Copy).then_inc(S["q_copied"], 1)
                    if i == 0:
                        act.wait_ge(S["kss"], NT * (g + 1))
                        nc.scalar.activation(kinv[:, b, :], kss[:, b, :], ACT.Sqrt, bias=eps[:],
                                             scale=1.0 / HD).then_inc(S["root"], 1)
                elif step < TAIL:
                    j = step - KTR
                    act.wait_ge(S["k_tr"], 2 * g + j + 1)
                    nc.scalar.activation(k_t[:, b, j * 512:(j + 1) * 512], bank[j][:], ACT.Copy,
                                         scale=kw[:]).then_inc(S["k_t"], 1)
                    if j == 1:
                        act.wait_ge(S["ssq"], G * NH2 * (g + 1))
                        nc.scalar.activation(ssq_t[:], bank[2][0:G * NH2, :], ACT.Copy).then_inc(S["ssq_t"], 1)
                elif step == TAIL:
                    act.wait_ge(S["ssq_tr"], g + 1)
                    nc.scalar.activation(qinv[:, b, :], bank[2][:, 0:NT * G], ACT.Sqrt, bias=eps[:],
                                         scale=1.0 / HD).then_inc(S["root"], 1)

            def exp(u):
                act.wait_ge(S["maxed"], u + 1)
                for i, (lo, hi) in enumerate(((0, P), (P, W))):
                    ins = nc.scalar.activation(sc[:, u % 3, lo:hi], sc[:, u % 3, lo:hi], ACT.Exp,
                                               bias=nmax[:, u % 3, i:i + 1],
                                               accum_out=den[:, u % 3, i:i + 1])
                ins.then_inc(S["exped"], 1)

            def copy_probs(u):
                act.wait_ge(S["p_tr"], u + 1)
                if u >= 2:
                    act.wait_ge(S["pv"], u - 1)
                nc.scalar.activation(pt[:, u % 2, :], bank[5][:, 0:W], ACT.Copy).then_inc(S["p_copied"], 1)

            def copy_out(u):
                nb = u // G
                act.wait_ge(S["pv"], u + 1)
                if nb >= 2:
                    act.wait_ge(S["y_mm"], 2 * (nb - 1))
                nc.scalar.activation(o_hi[:, nb % 2, u % G, :], bank[6][:, 0:SEQ], ACT.Copy).then_inc(S["o_hi"], 1)

            act.wait_ge(S["kw"], 1)
            for step in range(UNITS):
                project(0, step)
            for u in range(ALL + AHEAD + 2):
                if u < ALL:
                    exp(u)
                if AHEAD <= u < ALL + AHEAD:
                    copy_probs(u - AHEAD)
                if u < ALL and u // UNITS + 1 < GROUPS:
                    project(u // UNITS + 1, u % UNITS)
                if 0 <= u - AHEAD - 1 < ALL:
                    copy_out(u - AHEAD - 1)

        @block.vector
        def _(dve):
            nc.vector.memset(pick[:].bitcast(FP32), 0.0).then_inc(S["ready"], 1)
            dve.wait_ge(S["ready"], 1)
            nc.vector.memset(pick[:].rearrange("p a b -> p (a b)")[:, 0:(G * NH2) ** 2:G * NH2 + 1].bitcast(FP32),
                             1.0).then_inc(S["ready"], 1)
            nc.vector.memset(eps[:], EPS).then_inc(S["kw0"], 1)
            dve.wait_ge(S["small"], 32)
            nc.vector.tensor_scalar(nw[:, 0:1], nw[:, 0:1], 1.0 / math.sqrt(HD), None, ALU.mult).then_inc(
                S["kw0"], 1)
            dve.wait_ge(S["kw0"], 2)
            nc.vector.tensor_tensor(kw[:], nw[:, 0:1], nw[:, 1:2], ALU.mult).then_inc(S["kw"], 1)

            def split_qkv(g):
                dve.wait_ge(S["w"], 16 * max(2 * g, 1))
                if g:
                    dve.wait_ge(S["q_mm"], G * NH2 * g)
                    dve.wait_ge(S["kv_mm"], NT * g)
                nc.vector.tensor_copy(w_hi[:], stage[:]).then_inc(S["w_hi"], 1)

            def split_out(g):
                dve.wait_ge(S["w"], 16 * min(2 * g + 3, 2 * GROUPS))
                if g:
                    dve.wait_ge(S["y_mm"], NT * g)
                nc.vector.tensor_copy(wo_hi[:], stage[:, 0:WO]).then_inc(S["wo_hi"], 1)

            def project(g, step):
                b = g % 2
                if step == Q + 1:
                    dve.wait_ge(S["root"], 2 * g + 1)
                    nc.vector.reciprocal(kinv[:, b, :], kinv[:, b, :]).then_inc(S["inv"], 1)
                if step in (Q + 3, Q + 4):
                    dve.wait_ge(S["inv"], 2 * g + 1)
                    for t in range(4 * (step - Q - 3), 4 * (step - Q - 2)):
                        nc.vector.tensor_scalar(keys[:, t, :], keys[:, t, :], kinv[:, b, t:t + 1], None,
                                                ALU.mult).then_inc(S["k_scaled"], 1)
                if Q < step <= KTR:
                    n = G * NH2 * g + step - Q - 1
                    dve.wait_ge(S["sq"], n + 1)
                    if n >= 2:
                        dve.wait_ge(S["ssq"], n - 1)
                    nc.vector.tensor_copy(q_sq_hi[:, n % 2, :], q_sq[:]).then_inc(S["sq_hi"], 1)
                if step == SPLIT_QKV and g + 1 < GROUPS:
                    split_qkv(g + 1)
                if step == TAIL + 1:
                    dve.wait_ge(S["root"], 2 * g + 2)
                    nc.vector.reciprocal(qinv[:, b, :], qinv[:, b, :]).then_inc(S["inv"], 1)

            def bias_and_max(u):
                g, b, h = unit(u)
                s = sc[:, u % 3, :]
                dve.wait_ge(S["s_mm"], u + 1)
                if u % UNITS == 0:
                    dve.wait_ge(S["inv"], 2 * g + 2)
                dve.wait_ge(S["alibi"], G * g + h + 1)
                if u >= 3:
                    dve.wait_ge(S["p_tr"], u - 2)
                for i, (lo, hi) in enumerate(((0, P), (P, W))):
                    half, t4 = divmod(2 * b + i, HALF // P)
                    at = t4 * G * NH2 + h * NH2 + half
                    ins = nc.vector.scalar_tensor_tensor(
                        out=s[:, lo:hi], in0=bank[3 + u % 2][:, lo:hi], scalar=qinv[:, g % 2, at:at + 1],
                        in1=alibi[:, g % 2, h, lo:hi], op0=ALU.mult, op1=ALU.add)
                ins.then_inc(S["biased"], 1)
                dve.wait_ge(S["biased"], u + 1)
                for i, (lo, hi) in enumerate(((0, P), (P, W))):
                    ins = nc.vector.tensor_reduce(nmax[:, u % 3, i:i + 1], s[:, lo:hi], AX, ALU.max,
                                                  negate=True)
                ins.then_inc(S["maxed"], 1)

            def normalise(u):
                dve.wait_ge(S["exped"], u + 1)
                nc.vector.reciprocal(den[:, u % 3, :], den[:, u % 3, :]).then_inc(S["rden"], 1)
                dve.wait_ge(S["rden"], u + 1)
                for i, (lo, hi) in enumerate(((0, P), (P, W))):
                    p = sc[:, u % 3, lo:hi]
                    ins = nc.vector.tensor_scalar(p, p, den[:, u % 3, i:i + 1], None, ALU.mult)
                ins.then_inc(S["scaled"], 1)

            def copy_out(u):
                g, b, h = unit(u)
                nb = u // G
                dve.wait_ge(S["o_hi"], u + 1)
                if nb >= 2:
                    dve.wait_ge(S["y_mm"], 2 * (nb - 1))
                nc.vector.tensor_tensor(o_lo[:, nb % 2, h, :], bank[6][:, 0:SEQ],
                                        o_hi[:, nb % 2, h, :].bitcast(FP32), ALU.subtract).then_inc(
                    S["o_copied"], 1)

            def add_output(g, b, tile):
                t = 2 * b + tile
                dve.wait_ge(S["y_mm"], NT * g + t + 1)
                if g == 0:
                    nc.vector.tensor_copy(branch[:, t, :], bank[7][:]).then_inc(S["y_added"], 1)
                else:
                    dve.wait_ge(S["y_added"], NT * (g - 1) + t + 1)
                    nc.vector.tensor_tensor(branch[:, t, :], branch[:, t, :], bank[7][:],
                                            ALU.add).then_inc(S["y_added"], 1)

            split_qkv(0)
            for step in range(UNITS):
                project(0, step)
            for u in range(ALL + AHEAD + 5):
                if output_of(u - AHEAD - 3):
                    g, b, tile = output_of(u - AHEAD - 3)
                    if g == GROUPS - 1:
                        t = 2 * b + tile
                        branch_stats(chip, dve, t, S["y_added"], NT * g + t + 1)
                if output_of(u - AHEAD - 2):
                    add_output(*output_of(u - AHEAD - 2))
                if u < ALL:
                    g = u // UNITS
                    bias_and_max(u)
                    if u == 0 or (g and u % UNITS == SPLIT_OUT):
                        split_out(g)
                    if g + 1 < GROUPS:
                        project(g + 1, u % UNITS)
                if 1 <= u <= ALL:
                    normalise(u - 1)
                if 0 <= u - AHEAD - 1 < ALL:
                    copy_out(u - AHEAD - 1)


INNER = 1376


def int8_ffn_early(chip, scope):
    nc, d = chip.nc, chip.dram

    def sb(name, shape, dt=FP32):
        return scope.enter_context(nc.sbuf_tensor(f"ffn_{name}", shape, dt))

    gate_i = sb("gate_int", [P, 2, INNER], I32)
    up_i = sb("up_int", [P, INNER], I32)
    gate_w = sb("gate_w", [P, KC, INNER], FP32R)
    up_w = sb("up_w", [P, KC, INNER], FP32R)
    S = {n: chip.sem("ffn_" + n) for n in ("g0", "g1", "u", "g_cast", "u_cast")}

    def load(sp, kind, k):
        if kind == "gate":
            if k >= 2:
                sp.wait_ge(S["g_cast"], k - 1)
            sp.dma_start(gate_i[:, k % 2], d["gate1"][:, k, :]).then_inc(S[f"g{k % 2}"], 16)
        else:
            if k >= 1:
                sp.wait_ge(S["u_cast"], k)
            sp.dma_start(up_i[:], d["up1"][:, k, :]).then_inc(S["u"], 16)

    def sync(sp):
        for kind, k in (("gate", 0), ("up", 0), ("gate", 1), ("up", 1), ("gate", 2), ("up", 2), ("gate", 3)):
            load(sp, kind, k)

    def gpsimd(pool):
        for k in range(2):
            pool.wait_ge(S["u"], 16 * (k + 1))
            nc.gpsimd.tensor_copy(up_w[:, k, :], up_i[:]).then_inc(S["u_cast"], 1)

    def scalar(act, k):
        if k < 2:
            act.wait_ge(S[f"g{k}"], 16)
            nc.scalar.activation(gate_w[:, k, :], gate_i[:, k], ACT.Copy).then_inc(S["g_cast"], 1)

    return Early(sync, gpsimd, scalar, S, (load, gate_i, up_i, gate_w, up_w))


def int8_ffn(chip, early):
    nc, d, bank = chip.nc, chip.dram, chip.bank
    x_hi, x_lo, branch = chip.x_hi, chip.x_lo, chip.branch
    load, gate_i, up_i, gate_w, up_w = early.tensors
    IC = -(-INNER // P)
    rows = [min(P, INNER - i * P) for i in range(IC)]
    with ExitStack() as ctx:
        def sb(name, shape, dt=FP32):
            return ctx.enter_context(nc.sbuf_tensor(f"ffn_{name}", shape, dt))

        down_i = sb("down_int", [P, 2, C], I32)
        down_w = sb("down_w", [P, IC, C], FP32R)
        scales = sb("scales", [P, 2, IC])
        down_s = sb("down_scale", [P, C])
        gate = sb("gate", [P, 2, HALF])
        h = sb("hidden", [P, 2, HALF])
        h_hi = sb("hidden_hi", [P, IC, HALF], FP32R)
        h_lo = sb("hidden_lo", [P, IC, HALF], FP32R)
        S = {n: chip.layer_sem(ctx, "ffn_" + n) for n in (
            "d0", "d1", "small", "d_cast", "g_mm", "u_mm", "gated", "hidden", "h_hi", "h_lo", "y_mm", "y_copied")}
        S.update(early.sems)
        block = ctx.enter_context(nc.Block())


        @block.sync
        def _(sp):
            load(sp, "up", 3)
            sp.dma_start(scales[:], d["scales1"]).then_inc(S["small"], 16)
            sp.dma_start(down_s[:], d["down_scale1"]).then_inc(S["small"], 16)
            for i in range(IC):
                if i >= 2:
                    sp.wait_ge(S["d_cast"], i - 1)
                sp.dma_start(down_i[:, i % 2], d["down1"][:, i, :]).then_inc(S[f"d{i % 2}"], 16)

        @block.gpsimd
        def _(pool):
            for n in range(NH2 * IC):
                i = n % IC
                if n < IC:
                    pool.wait_ge(S[f"d{i % 2}"], 16 * (i // 2 + 1))
                    nc.gpsimd.tensor_copy(down_w[:, i, :], down_i[:, i % 2]).then_inc(S["d_cast"], 1)
                r = rows[i]
                pool.wait_ge(S["h_hi"], n + 1)
                if n >= IC:
                    pool.wait_ge(S["y_mm"], NT // 2)
                nc.gpsimd.tensor_tensor(h_lo[0:r, i, :], h[0:r, n % 2, :], h_hi[0:r, i, :].bitcast(FP32),
                                        ALU.subtract).then_inc(S["h_lo"], 1)

        @block.tensor
        def _(pe):
            for half in range(NH2):
                tok = slice(half * HALF, (half + 1) * HALF)
                for i in range(IC):
                    n = half * IC + i
                    cols = slice(i * P, i * P + rows[i])
                    for w, out, cast, done, freed in ((gate_w, bank[n % 2], "g_cast", "g_mm", "gated"),
                                                      (up_w, bank[2 + n % 2], "u_cast", "u_mm", "hidden")):
                        if n >= 2:
                            pe.wait_ge(S[freed], n - 1)
                        for k in range(KC):
                            if n == 0:
                                pe.wait_ge(S[cast], k + 1)
                            ins = split_matmul(nc, out[0:rows[i], :], (w[:, k, cols],),
                                               (x_hi[:, k, tok], x_lo[:, k, tok]), k == 0, k == KC - 1)
                        ins.then_inc(S[done], 1)
                pe.wait_ge(S["d_cast"], IC)
                for j in range(4):
                    t = 4 * half + j
                    if t >= 4:
                        pe.wait_ge(S["y_copied"], t - 3)
                    for i in range(IC):
                        if j == 0:
                            pe.wait_ge(S["h_lo"], half * IC + i + 1)
                        a = (slice(0, rows[i]), i, slice(j * P, (j + 1) * P))
                        ins = split_matmul(nc, bank[4 + j][:], (h_hi[a], h_lo[a]),
                                           (down_w[0:rows[i], i, :],), i == 0, i == IC - 1)
                    ins.then_inc(S["y_mm"], 1)

        @block.scalar
        def _(act):
            for k in (2, 3):
                act.wait_ge(S["u"], 16 * (k + 1))
                nc.scalar.activation(up_w[:, k, :], up_i[:], ACT.Copy).then_inc(S["u_cast"], 1)
            act.wait_ge(S["small"], 32)
            for n in range(NH2 * IC):
                i = n % IC
                r = rows[i]
                act.wait_ge(S["g_mm"], n + 1)
                if n >= 2:
                    act.wait_ge(S["hidden"], n - 1)
                nc.scalar.activation(gate[0:r, n % 2, :], bank[n % 2][0:r, :], ACT.Copy,
                                     scale=scales[0:r, 0, i:i + 1]).then_inc(S["gated"], 1)
                act.wait_ge(S["hidden"], n + 1)
                if n >= IC:
                    act.wait_ge(S["y_mm"], NT // 2)
                nc.scalar.activation(h_hi[0:r, i, :], h[0:r, n % 2, :], ACT.Copy).then_inc(S["h_hi"], 1)

        @block.vector
        def _(dve):
            for k in (2, 3):
                dve.wait_ge(S[f"g{k % 2}"], 32)
                nc.vector.tensor_copy(gate_w[:, k, :], gate_i[:, k % 2]).then_inc(S["g_cast"], 1)
            dve.wait_ge(S["small"], 32)
            for n in range(NH2 * IC):
                half, i = divmod(n, IC)
                r = rows[i]
                dve.wait_ge(S["u_mm"], n + 1)
                dve.wait_ge(S["gated"], n + 1)
                if n >= 2:
                    dve.wait_ge(S["h_lo"], n - 1)
                nc.vector.scalar_tensor_tensor(
                    out=h[0:r, n % 2, :], in0=bank[2 + n % 2][0:r, :], scalar=scales[0:r, 1, i:i + 1],
                    in1=gate[0:r, n % 2, :], op0=ALU.mult, op1=ALU.mult).then_inc(S["hidden"], 1)
                if i == IC - 1:
                    for j in range(4):
                        t = 4 * half + j
                        dve.wait_ge(S["y_mm"], t + 1)
                        nc.vector.tensor_tensor(branch[:, t, :], bank[4 + j][:], down_s[:], ALU.mult).then_inc(
                            S["y_copied"], 1)
                        branch_stats(chip, dve, t, S["y_copied"], t + 1)


def selective_scan(chip):
    nc, d, bank = chip.nc, chip.dram, chip.bank
    x_hi, x_lo, branch, ident = chip.x_hi, chip.x_lo, chip.branch, chip.ident
    STATES, RANK = 16, 16
    R = RANK + 2 * STATES
    UNITS = NH2 * STATES * KC
    RING = 3
    with ExitStack() as ctx:
        def sb(name, shape, dt=FP32):
            return ctx.enter_context(nc.sbuf_tensor(f"ssm_{name}", shape, dt))

        x_t = sb("x_t", [P, KC, TOKENS])
        xpw = sb("x_proj", [P, KC, R])
        xpw_hi = sb("x_proj_hi", [P, KC, R], FP32R)
        xpw_lo = sb("x_proj_lo", [P, KC, R], FP32R)
        dtw = sb("dt_proj", [RANK, C])
        dtb = sb("dt_bias", [P, KC])
        a_neg = sb("a", [P, KC, STATES])
        dskip = sb("d", [P, KC])
        sel = sb("row_select", [R, 2 * STATES, P])
        one = sb("one", [P, 1])
        xp = sb("xp", [R, TOKENS])
        dt = sb("dt", [P, KC, TOKENS])
        dtx = sb("dt_x", [P, KC, TOKENS])
        tmp = sb("softplus", [P, 2, 3, HALF])
        bc = sb("b_and_c", [P, RING, 2, HALF])
        da = sb("decay", [P, RING, HALF])
        dbx = sb("drive", [P, RING, HALF])
        hs = sb("state", [P, RING, HALF])
        hc = sb("read_out", [P, RING, HALF])
        S = {n: chip.layer_sem(ctx, "ssm_" + n) for n in (
            "w", "w2", "a", "xp_mm", "xp", "dt_mm", "pre", "e", "ln", "dt", "dtx", "bc_mm", "bc", "decay", "zero",
            "drive", "scan", "read", "y_mm", "y", "y_tr", "y_copied", "v", "one", "w_split", "x_whole")}
        block = ctx.enter_context(nc.Block())
        W1 = 16 * 5


        def unit(u):
            half, r = divmod(u, STATES * KC)
            return half, r // KC, r % KC

        def tok(half):
            return slice(half * HALF, (half + 1) * HALF)

        @block.sync
        def _(sp):
            sp.dma_start(xpw[:], d["x_proj2"]).then_inc(S["w"], 16)
            sp.dma_start(dtw[:], d["dt_proj2"]).then_inc(S["w2"], 16)
            sp.dma_start(dtb[:], d["dt_bias2"]).then_inc(S["w2"], 16)
            sp.dma_start(a_neg[:], d["a_log2"]).then_inc(S["w2"], 16)
            sp.dma_start(dskip[:], d["d2"]).then_inc(S["w2"], 16)
            sp.dma_start(sel[:], d["row_select2"]).then_inc(S["w2"], 16)

        @block.tensor
        def _(pe):
            pe.wait_ge(S["w_split"], 2)
            for half in range(NH2):
                for k in range(KC):
                    ins = split_matmul(nc, bank[half][0:R, :], (xpw_hi[:, k, :], xpw_lo[:, k, :]),
                                       (x_hi[:, k, tok(half)], x_lo[:, k, tok(half)]), k == 0, k == KC - 1)
                ins.then_inc(S["xp_mm"], 1)
            pe.wait_ge(S["w2"], W1)
            for i in range(NH2 * KC):
                half, c = divmod(i, KC)
                pe.wait_ge(S["xp"], half + 1)
                if i >= 4:
                    pe.wait_ge(S["pre"], 3 * (i - 3))
                nc.tensor.matmul(bank[4 + i % 4][:], dtw[:, c * P:(c + 1) * P], xp[0:RANK, tok(half)],
                                 start=True, stop=True).then_inc(S["dt_mm"], 1)

            def broadcast(j):
                half, n = divmod(j, STATES)
                if j < 2:
                    pe.wait_ge(S["pre"], 3 * NH2 * KC)
                else:
                    pe.wait_ge(S["bc"], j - 1)
                for i in range(2):
                    ins = nc.tensor.matmul(bank[4 + 2 * (j % 2) + i][:], sel[:, i * STATES + n, :],
                                           xp[:, tok(half)], start=True, stop=True)
                ins.then_inc(S["bc_mm"], 1)

            broadcast(0)
            broadcast(1)
            for u in range(UNITS):
                half, n, c = unit(u)
                if c == 0 and u // KC + 2 < NH2 * STATES:
                    broadcast(u // KC + 2)
                if half and n == 0:
                    pe.wait_ge(S["y"], c + 1)
                pe.wait_ge(S["read"], u + 1)
                nc.tensor.matmul(bank[c][:], ident[:], hc[:, u % RING, :], start=(n == 0),
                                 stop=(n == STATES - 1)).then_inc(S["y_mm"], 1)
            for t in range(NT):
                pe.wait_ge(S["y"], KC * (t // 4 + 1))
                if t >= 4:
                    pe.wait_ge(S["y_copied"], t - 3)
                for c in range(KC):
                    ins = nc.tensor.transpose(bank[4 + t % 4][:, c * P:(c + 1) * P], dt[:, c, t * P:(t + 1) * P],
                                              ident[:])
                ins.then_inc(S["y_tr"], 1)

        @block.scalar
        def _(act):
            for half in range(NH2):
                act.wait_ge(S["xp_mm"], half + 1)
                nc.scalar.activation(xp[:, tok(half)], bank[half][0:R, :], ACT.Copy).then_inc(S["xp"], 1)
            act.wait_ge(S["w2"], W1)
            act.wait_ge(S["one"], 1)
            nc.scalar.activation(a_neg[:], a_neg[:], ACT.Exp).then_inc(S["a"], 1)
            for i in range(NH2 * KC):
                act.wait_ge(S["pre"], 3 * i + 3)
                nc.scalar.activation(tmp[:, i % 2, 0, :], tmp[:, i % 2, 0, :], ACT.Exp).then_inc(S["e"], 1)
                act.wait_ge(S["e"], i + 1)
                half, c = divmod(i, KC)
                nc.scalar.activation(dt[:, c, tok(half)], tmp[:, i % 2, 0, :], ACT.Ln,
                                     bias=one[:]).then_inc(S["ln"], 1)
            act.wait_ge(S["dt"], NH2 * KC)
            act.wait_ge(S["a"], 2)
            for u in range(UNITS):
                half, n, c = unit(u)
                if c == 0:
                    j = u // KC
                    act.wait_ge(S["bc_mm"], j + 1)
                    if j >= RING:
                        act.wait_ge(S["drive"], KC * (j - RING + 1))
                        act.wait_ge(S["read"], KC * (j - RING + 1))
                    for i in range(2):
                        ins = nc.scalar.activation(bc[:, j % RING, i, :], bank[4 + 2 * (j % 2) + i][:], ACT.Copy)
                    ins.then_inc(S["bc"], 1)
                if u >= RING:
                    act.wait_ge(S["scan"], u - RING + 1)
                nc.scalar.activation(da[:, u % RING, :], dt[:, c, tok(half)], ACT.Exp,
                                     scale=a_neg[:, c, n:n + 1]).then_inc(S["decay"], 1)
            for t in range(NT):
                act.wait_ge(S["y_tr"], t + 1)
                nc.scalar.activation(branch[:, t, :], bank[4 + t % 4][:], ACT.Copy).then_inc(S["y_copied"], 1)

        @block.gpsimd
        def _(pool):
            for half in range(NH2):
                for c in range(KC):
                    nc.gpsimd.tensor_tensor(x_t[:, c, tok(half)], x_hi[:, c, tok(half)].bitcast(FP32),
                                            x_lo[:, c, tok(half)].bitcast(FP32), ALU.add).then_inc(
                        S["x_whole"], 1)
            for u in range(UNITS):
                half, n, c = unit(u)
                pool.wait_ge(S["scan"], u + 1)
                pool.wait_ge(S["bc"], u // KC + 1)
                if u >= RING:
                    pool.wait_ge(S["y_mm"], u - RING + 1)
                nc.gpsimd.tensor_tensor(hc[:, u % RING, :], hs[:, u % RING, :], bc[:, (u // KC) % RING, 1, :],
                                        ALU.mult).then_inc(S["read"], 1)

        @block.vector
        def _(dve):
            nc.vector.memset(one[:], 1.0).then_inc(S["one"], 1)
            dve.wait_ge(S["w"], 16)
            nc.vector.tensor_copy(xpw_hi[:], xpw[:]).then_inc(S["w_split"], 1)
            dve.wait_ge(S["w_split"], 1)
            nc.vector.tensor_tensor(xpw_lo[:], xpw[:], xpw_hi[:].bitcast(FP32), ALU.subtract).then_inc(
                S["w_split"], 1)
            dve.wait_ge(S["w2"], W1)

            def before_log(i):
                half, c = divmod(i, KC)
                dve.wait_ge(S["dt_mm"], i + 1)
                nc.vector.tensor_scalar(tmp[:, i % 2, 0, :], bank[4 + i % 4][:], dtb[:, c:c + 1], None,
                                        ALU.add).then_inc(S["pre"], 1)
                nc.vector.tensor_scalar(tmp[:, i % 2, 1, :], bank[4 + i % 4][:], dtb[:, c:c + 1], 0.0,
                                        ALU.add, ALU.max).then_inc(S["pre"], 1)
                dve.wait_ge(S["pre"], 3 * i + 2)
                nc.vector.scalar_tensor_tensor(out=tmp[:, i % 2, 0, :], in0=tmp[:, i % 2, 1, :], scalar=-2.0,
                                               in1=tmp[:, i % 2, 0, :], op0=ALU.mult,
                                               op1=ALU.add).then_inc(S["pre"], 1)

            def after_log(i):
                half, c = divmod(i, KC)
                e, m, w = (tmp[:, i % 2, j, :] for j in range(3))
                out = dt[:, c, tok(half)]
                dve.wait_ge(S["e"], i + 1)
                nc.vector.tensor_scalar(w, e, 1.0, -1.0, ALU.add, ALU.add).then_inc(S["v"], 1)
                dve.wait_ge(S["v"], 4 * i + 1)
                nc.vector.tensor_tensor(w, e, w, ALU.subtract).then_inc(S["v"], 1)
                dve.wait_ge(S["v"], 4 * i + 2)
                nc.vector.tensor_tensor(w, w, m, ALU.add).then_inc(S["v"], 1)
                dve.wait_ge(S["v"], 4 * i + 3)
                dve.wait_ge(S["ln"], i + 1)
                nc.vector.tensor_tensor(out, out, w, ALU.add).then_inc(S["dt"], 1)
                dve.wait_ge(S["dt"], i + 1)
                dve.wait_ge(S["x_whole"], i + 1)
                nc.vector.tensor_tensor(dtx[:, c, tok(half)], out, x_t[:, c, tok(half)], ALU.mult).then_inc(
                    S["v"], 1)

            for i in range(NH2 * KC + 1):
                if i < NH2 * KC:
                    before_log(i)
                if i >= 1:
                    after_log(i - 1)
            dve.wait_ge(S["a"], 1)
            nc.vector.tensor_scalar(a_neg[:], a_neg[:], -1.0, None, ALU.mult).then_inc(S["a"], 1)
            dve.wait_ge(S["v"], 4 * NH2 * KC)
            for u in range(UNITS + 1):
                if u < UNITS:
                    half, n, c = unit(u)
                    dve.wait_ge(S["bc"], u // KC + 1)
                    if u >= RING:
                        dve.wait_ge(S["scan"], u - RING + 1)
                    nc.vector.tensor_tensor(dbx[:, u % RING, :], dtx[:, c, tok(half)],
                                            bc[:, (u // KC) % RING, 0, :], ALU.mult).then_inc(S["drive"], 1)
                    dve.wait_ge(S["decay"], u + 1)
                    nc.vector.memset(da[:, u % RING, 0:HALF:SEQ], 0.0).then_inc(S["zero"], 1)
                if u >= 1:
                    v = u - 1
                    dve.wait_ge(S["zero"], v + 1)
                    dve.wait_ge(S["drive"], v + 1)
                    if v >= RING:
                        dve.wait_ge(S["read"], v - RING + 1)
                    nc.vector.tensor_tensor_scan(hs[:, v % RING, :], da[:, v % RING, :], dbx[:, v % RING, :],
                                                 0.0, ALU.mult, ALU.add).then_inc(S["scan"], 1)
                if u and u % (STATES * KC) == 0:
                    half = u // (STATES * KC) - 1
                    for c in range(KC):
                        dve.wait_ge(S["y_mm"], u - KC + c + 1)
                        nc.vector.scalar_tensor_tensor(
                            out=dt[:, c, tok(half)], in0=x_t[:, c, tok(half)], scalar=dskip[:, c:c + 1],
                            in1=bank[c][:], op0=ALU.mult, op1=ALU.add).then_inc(S["y"], 1)
            for t in range(NT):
                branch_stats(chip, dve, t, S["y_copied"], t + 1)


def table_linear_early(chip, scope):
    nc, d = chip.nc, chip.dram
    planes = scope.enter_context(nc.sbuf_tensor("lut_planes", [P, 4, KC * C // 32], I32))
    lut = scope.enter_context(nc.sbuf_tensor("lut_table", [P, KC, 16], FP32))
    bias = scope.enter_context(nc.sbuf_tensor("lut_bias", [P, C], FP32))
    loaded = chip.sem("lut_in")

    def sync(sp):
        sp.dma_start(planes[:], d["planes3"]).then_inc(loaded, 16)
        sp.dma_start(lut[:], d["lut3"]).then_inc(loaded, 16)
        sp.dma_start(bias[:], d["bias3"]).then_inc(loaded, 16)

    return Early(sync, no_part, no_part, {"in": loaded}, (planes, lut, bias))


def table_linear(chip, early):
    nc, d, bank = chip.nc, chip.dram, chip.bank
    x_hi, x_lo, branch, ident = chip.x_hi, chip.x_lo, chip.branch, chip.ident
    BITS, WORD = 4, 32
    WORDS = C // WORD
    CODES = 1 << BITS
    with ExitStack() as ctx:
        def sb(name, shape, dt=FP32):
            return ctx.enter_context(nc.sbuf_tensor(f"lut_{name}", shape, dt))

        planes, lut, bias = early.tensors
        bits = sb("bits", [P, BITS, KC * WORDS, WORD], I32)
        code = sb("code", [P, KC, C])
        w = sb("weights", [P, KC, C])
        pick = sb("pick", [P, 2, 2, C])
        w_hi = sb("weights_t_hi", [P, KC, C], FP32R)
        w_lo = sb("weights_t_lo", [P, KC, C], FP32R)
        S = {n: chip.layer_sem(ctx, "lut_" + n) for n in (
            "bits", "code", "dve_pick", "dve_w", "pool_pick", "pool_w", "w_tr", "w_hi", "w_lo", "y_mm", "y")}
        S.update(early.sems)
        block = ctx.enter_context(nc.Block())

        def look_up(eng, e, chunks, picked, written, slot):
            n = 0
            for o in chunks:
                for l in range(CODES):
                    if l == 0:
                        e.tensor_scalar(w[:, o, :], code[:, o, :], float(l), lut[:, o, l:l + 1], ALU.is_equal,
                                        ALU.mult).then_inc(written, 1)
                    else:
                        if n >= 2:
                            eng.wait_ge(written, written_before(n - 2))
                        e.tensor_scalar(pick[:, slot, n % 2, :], code[:, o, :], float(l), lut[:, o, l:l + 1],
                                        ALU.is_equal, ALU.mult).then_inc(picked, 1)
                        eng.wait_ge(picked, n + 1)
                        eng.wait_ge(written, written_before(n))
                        e.tensor_tensor(w[:, o, :], w[:, o, :], pick[:, slot, n % 2, :], ALU.add).then_inc(
                            written, 1)
                        n += 1

        def written_before(n):
            return n + n // (CODES - 1) + 1

        @block.gpsimd
        def _(pool):
            pool.wait_ge(S["code"], BITS - 1)
            look_up(pool, nc.gpsimd, (3,), S["pool_pick"], S["pool_w"], 1)

        @block.vector
        def _(dve):
            dve.wait_ge(S["in"], 48)
            for b in range(WORD):
                ins = nc.vector.tensor_scalar(bits[:, :, :, b], planes[:], b, 1, ALU.logical_shift_right,
                                              ALU.bitwise_and)
            ins.then_inc(S["bits"], 1)
            dve.wait_ge(S["bits"], 1)
            c2 = code[:].rearrange("p k c -> p (k c)")
            b2 = [bits[:, p].rearrange("p a b -> p (a b)") for p in range(BITS)]
            for p in range(BITS - 2, -1, -1):
                src = b2[BITS - 1] if p == BITS - 2 else c2
                if p < BITS - 2:
                    dve.wait_ge(S["code"], BITS - 2 - p)
                nc.vector.scalar_tensor_tensor(out=c2, in0=src, scalar=2.0, in1=b2[p], op0=ALU.mult,
                                               op1=ALU.add).then_inc(S["code"], 1)
            dve.wait_ge(S["code"], BITS - 1)
            look_up(dve, nc.vector, (0, 1, 2), S["dve_pick"], S["dve_w"], 0)
            for o in range(KC):
                dve.wait_ge(S["w_hi"], o + 1)
                nc.vector.tensor_tensor(w_lo[:, :, o * P:(o + 1) * P],
                                        bank[o][:].rearrange("p (k m) -> p k m", k=KC),
                                        w_hi[:, :, o * P:(o + 1) * P].bitcast(FP32), ALU.subtract).then_inc(
                    S["w_lo"], 1)
            for t in range(NT):
                dve.wait_ge(S["y_mm"], t + 1)
                nc.vector.tensor_tensor(branch[:, t, :], bank[4 + t % 4][:], bias[:], ALU.add).then_inc(
                    S["y"], 1)
                branch_stats(chip, dve, t, S["y"], t + 1)

        @block.tensor
        def _(pe):
            for o in range(KC):
                if o == 3:
                    pe.wait_ge(S["pool_w"], CODES)
                else:
                    pe.wait_ge(S["dve_w"], CODES * (o + 1))
                for i in range(KC):
                    ins = nc.tensor.transpose(bank[o][:, i * P:(i + 1) * P], w[:, o, i * P:(i + 1) * P],
                                              ident[:])
                ins.then_inc(S["w_tr"], 1)
            pe.wait_ge(S["w_lo"], KC)
            for t in range(NT):
                if t >= 4:
                    pe.wait_ge(S["y"], t - 3)
                for k in range(KC):
                    tok = slice(t * P, (t + 1) * P)
                    ins = split_matmul(nc, bank[4 + t % 4][:], (x_hi[:, k, tok], x_lo[:, k, tok]),
                                       (w_hi[:, k, :], w_lo[:, k, :]), k == 0, k == KC - 1)
                ins.then_inc(S["y_mm"], 1)

        @block.scalar
        def _(act):
            for o in range(KC):
                act.wait_ge(S["w_tr"], o + 1)
                nc.scalar.activation(w_hi[:, :, o * P:(o + 1) * P], bank[o][:].rearrange("p (k m) -> p k m", k=KC),
                                     ACT.Copy).then_inc(S["w_hi"], 1)


def head_mixer_early(chip, scope):
    nc, d = chip.nc, chip.dram

    def sb(name, shape, dt=FP32):
        return scope.enter_context(nc.sbuf_tensor(f"mix_{name}", shape, dt))

    w = sb("w_qkv", [P, KC, C])
    w_hi = sb("w_qkv_hi", [P, 3, KC, C], FP32R)
    w_lo = sb("w_qkv_lo", [P, 3, KC, C], FP32R)
    S = {n: chip.sem("mix_" + n) for n in ("w", "w_hi", "w_lo")}

    def sync(sp):
        for i in range(2):
            if i:
                sp.wait_ge(S["w_lo"], i)
            sp.dma_start(w[:], d["Wqkv4"][:, i]).then_inc(S["w"], 16)

    def gpsimd(pool):
        pool.wait_ge(S["w"], 16)
        nc.gpsimd.tensor_copy(w_hi[:, 0], w[:]).then_inc(S["w_hi"], 1)
        pool.wait_ge(S["w_hi"], 1)
        nc.gpsimd.tensor_tensor(w_lo[:, 0], w[:], w_hi[:, 0].bitcast(FP32), ALU.subtract).then_inc(S["w_lo"], 1)

    return Early(sync, gpsimd, no_part, S, (w, w_hi, w_lo))


def head_mixer(chip, early):
    nc, d, bank = chip.nc, chip.dram, chip.bank
    x_hi, x_lo, branch, ident = chip.x_hi, chip.x_lo, chip.branch, chip.ident
    H, D = 32, 16
    Q = 32
    PAIRS = Q // 2
    THRESHOLD = 4.0 * float(np.float32(0.001))
    with ExitStack() as ctx:
        def sb(name, shape, dt=FP32):
            return ctx.enter_context(nc.sbuf_tensor(f"mix_{name}", shape, dt))

        w, w_hi, w_lo = early.tensors
        wo = sb("w_out", [P, KC, C])
        bias = sb("bias", [Q + 1, 4, C])
        bias_r = sb("bias_hi_and_lo", [Q + 1, 4, C], FP32R)
        one = sb("ones", [Q + 1, P], FP32R)
        q_h = sb("q_heads", [P, 2, Q, D])
        k_h = sb("k_heads", [P, 2, PAIRS, 2, 2, D])
        v_h = sb("v_heads", [P, 2, Q, D])
        q_d = sb("q_channels", [P, 2, PAIRS, H])
        k_d = sb("k_channels", [P, 2, PAIRS, 2, H])
        top = sb("top", [P, 2, Q])
        ex = sb("exps", [P, 2, Q, H])
        den = sb("denominators", [P, 2, Q])
        pr = sb("probs_t", [P, 2, Q, H])
        o_h = sb("out_heads", [P, 2, Q, D])
        o = sb("out", [P, 2, H, D])
        o_t = sb("out_t", [P, 2, KC, P])
        S = {n: chip.layer_sem(ctx, "mix_" + n) for n in (
            "bias", "bias_hi", "bias_lo", "wo", "ready", "zeroed", "q_mm", "k_mm", "v_mm", "heads", "channels", "s_mm",
            "top", "shifted", "exped", "masked", "sum", "probs_t", "o_mm", "scaled", "o", "o_tr", "o_t", "y_mm", "y")}
        S.update(early.sems)
        block = ctx.enter_context(nc.Block())


        @block.sync
        def _(sp):
            for r in (0, Q):
                sp.dma_start(bias[r:r + 1], d["bias4"]).then_inc(S["bias"], 16)
            sp.wait_ge(S["w_lo"], 2)
            sp.dma_start(w[:], d["Wqkv4"][:, 2]).then_inc(S["w"], 16)
            sp.dma_start(wo[:], d["Wo4"]).then_inc(S["wo"], 16)

        @block.gpsimd
        def _(pool):
            nc.gpsimd.memset(one[:].bitcast(FP32), 1.0).then_inc(S["ready"], 1)
            nc.gpsimd.memset(k_h[:], 0.0).then_inc(S["ready"], 1)

        @block.tensor
        def _(pe):
            def project(t):
                for i, name in enumerate(("q_mm", "k_mm", "v_mm")):
                    if t == 0:
                        pe.wait_ge(S["w_lo"], i + 1)
                    else:
                        pe.wait_ge(S["heads"], 3 * (t - 1) + i + 1)
                    for k in range(KC):
                        tok = slice(t * P, (t + 1) * P)
                        split_matmul(nc, bank[i][:], (x_hi[:, k, tok], x_lo[:, k, tok]),
                                     (w_hi[:, i, k, :], w_lo[:, i, k, :]), k == 0, False)
                    if t == 0 and i == 0:
                        pe.wait_ge(S["bias_lo"], 1)
                    nc.tensor.matmul(bank[i][:], one[:], bias_r[:, i, :], start=False, stop=True).then_inc(
                        S[name], 1)

            def scores(t):
                pe.wait_ge(S["channels"], 2 * (t + 1))
                if t:
                    pe.wait_ge(S["masked"], t)
                for pair in range(PAIRS):
                    for j in range(4):
                        r = slice(Q * j, Q * (j + 1))
                        ins = nc.tensor.matmul(
                            bank[3 + pair // 8][r, (pair % 8) * 64:(pair % 8 + 1) * 64], q_d[r, t % 2, pair, :],
                            k_d[r, t % 2, pair].rearrange("p e h -> p (e h)"), start=True, stop=True)
                ins.then_inc(S["s_mm"], 1)

            def mix(t):
                pe.wait_ge(S["probs_t"], t + 1)
                if t:
                    pe.wait_ge(S["scaled"], t)
                for n in range(Q):
                    for j in range(4):
                        r = slice(Q * j, Q * (j + 1))
                        ins = nc.tensor.matmul(bank[5][r, n * D:(n + 1) * D], pr[r, t % 2, n, :],
                                               v_h[r, t % 2, n, :], start=True, stop=True)
                ins.then_inc(S["o_mm"], 1)

            def output(t):
                pe.wait_ge(S["o"], t + 1)
                if t:
                    pe.wait_ge(S["o_t"], t)
                for k in range(KC):
                    ins = nc.tensor.transpose(bank[6][:, k * P:(k + 1) * P],
                                              o[:, t % 2].rearrange("p h d -> p (h d)")[:, k * P:(k + 1) * P],
                                              ident[:])
                ins.then_inc(S["o_tr"], 1)

            def result(t):
                pe.wait_ge(S["o_t"], t + 1)
                if t:
                    pe.wait_ge(S["y"], t)
                for k in range(KC):
                    nc.tensor.matmul(bank[7][:], o_t[:, t % 2, k, :], wo[:, k, :], start=(k == 0), stop=False)
                nc.tensor.matmul(bank[7][:], one[:], bias_r[:, 3, :], start=False, stop=True).then_inc(
                    S["y_mm"], 1)

            pe.wait_ge(S["ready"], 2)
            project(0)
            pe.wait_ge(S["wo"], 16)
            for t in range(NT + 3):
                if t + 1 < NT:
                    project(t + 1)
                if t < NT:
                    scores(t)
                if 1 <= t <= NT:
                    mix(t - 1)
                if 2 <= t <= NT + 1:
                    output(t - 2)
                if t >= 3:
                    result(t - 3)

        @block.scalar
        def _(act):
            act.wait_ge(S["bias"], 32)
            act.wait_ge(S["zeroed"], 1)
            for r in (0, Q):
                nc.scalar.activation(bias_r[r:r + 1], bias[r:r + 1], ACT.Copy).then_inc(S["bias_hi"], 1)
            for i in (1, 2):
                act.wait_ge(S["w"], 16 * (i + 1))
                nc.scalar.activation(w_hi[:, i], w[:], ACT.Copy).then_inc(S["w_hi"], 1)
            for t in range(NT + 3):
                if t < NT:
                    act.wait_ge(S["shifted"], t + 1)
                    e = ex[:, t % 2].rearrange("p n h -> p (n h)")
                    nc.scalar.activation(e, e, ACT.Exp, scale=0.25).then_inc(S["exped"], 1)
                if 2 <= t <= NT + 1:
                    act.wait_ge(S["o_tr"], t - 1)
                    if t >= 4:
                        act.wait_ge(S["y_mm"], t - 3)
                    nc.scalar.activation(o_t[:, t % 2], bank[6][:].rearrange("p (k m) -> p k m", k=KC),
                                         ACT.Copy).then_inc(S["o_t"], 1)
                if t >= 3:
                    act.wait_ge(S["y_mm"], t - 2)
                    nc.scalar.activation(branch[:, t - 3, :], bank[7][:], ACT.Copy).then_inc(S["y"], 1)

        @block.vector
        def _(dve):
            def heads(t):
                if t >= 2:
                    dve.wait_ge(S["channels"], 2 * (t - 1))
                dve.wait_ge(S["q_mm"], t + 1)
                nc.vector.transpose(q_h[:, t % 2].rearrange("p n d -> p d n"),
                                    bank[0][:].rearrange("p (h d) -> p d h", d=D)).then_inc(S["heads"], 1)
                dve.wait_ge(S["k_mm"], t + 1)
                dve.wait_ge(S["ready"], 2)
                k_out = k_h[:, t % 2].rearrange("p n a b d -> p n (a b) d")[:, :, 0:4:3, :]
                nc.vector.transpose(k_out.rearrange("p n e d -> p d n e"),
                                    bank[1][:].rearrange("p (h d) -> p d h", d=D)).then_inc(S["heads"], 1)
                dve.wait_ge(S["v_mm"], t + 1)
                if t >= 2:
                    dve.wait_ge(S["o_mm"], t - 1)
                nc.vector.transpose(v_h[:, t % 2].rearrange("p n d -> p d n"),
                                    bank[2][:].rearrange("p (h d) -> p d h", d=D)).then_inc(S["heads"], 1)
                dve.wait_ge(S["heads"], 3 * t + 2)
                if t >= 2:
                    dve.wait_ge(S["s_mm"], t - 1)
                nc.vector.transpose(q_d[:, t % 2].rearrange("p n h -> p (n h)"),
                                    q_h[:, t % 2].rearrange("p n d -> p (n d)")).then_inc(S["channels"], 1)
                nc.vector.transpose(k_d[:, t % 2].rearrange("p n e h -> p (n e h)"),
                                    k_h[:, t % 2].rearrange("p n a b d -> p (n a b d)")).then_inc(
                    S["channels"], 1)

            def shift(t):
                dve.wait_ge(S["s_mm"], t + 1)
                if t >= 2:
                    dve.wait_ge(S["probs_t"], t - 1)
                for i in range(2):
                    s = bank[3 + i][:].rearrange("p (n h) -> p n h", h=H)
                    m = top[:, t % 2, i * PAIRS:(i + 1) * PAIRS]
                    nc.vector.tensor_reduce(m, s, AX, ALU.max).then_inc(S["top"], 1)
                for i in range(2):
                    s = bank[3 + i][:].rearrange("p (n h) -> p n h", h=H)
                    m = top[:, t % 2, i * PAIRS:(i + 1) * PAIRS]
                    dve.wait_ge(S["top"], 2 * t + i + 1)
                    ins = nc.vector.tensor_tensor(ex[:, t % 2, i * PAIRS:(i + 1) * PAIRS, :], s,
                                                  m.unsqueeze(2).to_broadcast([P, PAIRS, H]), ALU.subtract)
                ins.then_inc(S["shifted"], 1)

            def mask(t):
                dve.wait_ge(S["exped"], t + 1)
                for i in range(2):
                    e = ex[:, t % 2, i * PAIRS:(i + 1) * PAIRS, :].rearrange("p n h -> p (n h)")
                    ins = nc.vector.scalar_tensor_tensor(out=e, in0=bank[3 + i][:], scalar=THRESHOLD, in1=e,
                                                         op0=ALU.is_gt, op1=ALU.mult)
                ins.then_inc(S["masked"], 1)
                dve.wait_ge(S["masked"], t + 1)
                nc.vector.tensor_reduce(den[:, t % 2, :], ex[:, t % 2], AX, ALU.add).then_inc(S["sum"], 1)
                dve.wait_ge(S["sum"], 2 * t + 1)
                nc.vector.reciprocal(den[:, t % 2, :], den[:, t % 2, :]).then_inc(S["sum"], 1)
                if t >= 2:
                    dve.wait_ge(S["o_mm"], t - 1)
                nc.vector.transpose(pr[:, t % 2].rearrange("p n h -> p (n h)"),
                                    ex[:, t % 2].rearrange("p n h -> p (n h)")).then_inc(S["probs_t"], 1)

            def normalise(t):
                dve.wait_ge(S["o_mm"], t + 1)
                dve.wait_ge(S["sum"], 2 * t + 2)
                if t >= 2:
                    dve.wait_ge(S["o"], t - 1)
                nc.vector.tensor_tensor(o_h[:, t % 2], bank[5][:].rearrange("p (n d) -> p n d", d=D),
                                        den[:, t % 2, :].unsqueeze(2).to_broadcast([P, Q, D]),
                                        ALU.mult).then_inc(S["scaled"], 1)
                dve.wait_ge(S["scaled"], t + 1)
                if t >= 2:
                    dve.wait_ge(S["o_tr"], t - 1)
                nc.vector.transpose(o[:, t % 2].rearrange("p h d -> p d h"),
                                    o_h[:, t % 2].rearrange("p n d -> p d n")).then_inc(S["o"], 1)

            nc.vector.memset(bias_r[:].bitcast(FP32), 0.0).then_inc(S["zeroed"], 1)
            dve.wait_ge(S["bias_hi"], 2)
            nc.vector.tensor_tensor(bias_r[Q:Q + 1], bias[Q:Q + 1], bias_r[Q:Q + 1].bitcast(FP32),
                                    ALU.subtract).then_inc(S["bias_lo"], 1)
            for i in (1, 2):
                dve.wait_ge(S["w_hi"], i + 1)
                nc.vector.tensor_tensor(w_lo[:, i], w[:], w_hi[:, i].bitcast(FP32), ALU.subtract).then_inc(
                    S["w_lo"], 1)
            heads(0)
            for t in range(NT + 1):
                if t + 1 < NT:
                    heads(t + 1)
                if t < NT:
                    shift(t)
                if t >= 1:
                    normalise(t - 1)
                if t < NT:
                    mask(t)
            for t in range(NT):
                branch_stats(chip, dve, t, S["y"], t + 1)


def routed_lora_early(chip, scope):
    nc, d = chip.nc, chip.dram
    N = 32 + 4

    def sb(name, shape, dt=FP32):
        return scope.enter_context(nc.sbuf_tensor(f"lora_{name}", shape, dt))

    small_w = sb("a_and_router", [P, KC, N])
    small_hi = sb("a_and_router_hi", [P, KC, N], FP32R)
    small_lo = sb("a_and_router_lo", [P, KC, N], FP32R)
    w = sb("w", [P, KC, C])
    w_hi = sb("w_hi", [P, KC, C], FP32R)
    w_lo = sb("w_lo", [P, KC, C], FP32R)
    S = {n: chip.sem("lora_" + n) for n in ("in", "w", "split", "w_hi", "w_lo")}

    def sync(sp):
        sp.dma_start(small_w[:], d["small5"]).then_inc(S["in"], 16)
        sp.dma_start(w[:], d["W5"]).then_inc(S["w"], 16)

    def gpsimd(pool):
        pool.wait_ge(S["in"], 16)
        nc.gpsimd.tensor_copy(small_hi[:], small_w[:]).then_inc(S["split"], 1)
        pool.wait_ge(S["split"], 1)
        nc.gpsimd.tensor_tensor(small_lo[:], small_w[:], small_hi[:].bitcast(FP32), ALU.subtract).then_inc(
            S["split"], 1)
        pool.wait_ge(S["w"], 16)
        nc.gpsimd.tensor_copy(w_hi[:], w[:]).then_inc(S["w_hi"], 1)
        pool.wait_ge(S["w_hi"], 1)
        nc.gpsimd.tensor_tensor(w_lo[:], w[:], w_hi[:].bitcast(FP32), ALU.subtract).then_inc(S["w_lo"], 1)

    return Early(sync, gpsimd, no_part, S, (small_hi, small_lo, w_hi, w_lo))


def routed_lora(chip, early):
    nc, d, bank = chip.nc, chip.dram, chip.bank
    x_hi, x_lo, branch, ident = chip.x_hi, chip.x_lo, chip.branch, chip.ident
    E, R = 4, 8
    ER = E * R
    SCALE = 16.0 / 8.0
    with ExitStack() as ctx:
        def sb(name, shape, dt=FP32):
            return ctx.enter_context(nc.sbuf_tensor(f"lora_{name}", shape, dt))

        small_hi, small_lo, w_hi, w_lo = early.tensors
        ra_t = sb("ranks_and_logits_t", [ER + E, TOKENS])
        bm = sb("b", [ER, C])
        bias = sb("bias", [P, C])
        ra = sb("ranks_and_logits", [P, NT, ER + E])
        top = sb("top", [P, NT])
        g = sb("gates", [P, NT, E])
        den = sb("den", [P, NT])
        mixed_t = sb("mixed_t", [ER, TOKENS])
        S = {n: chip.layer_sem(ctx, "lora_" + n) for n in (
            "bm", "ra_mm", "ra_t", "ra_tr", "ra", "v", "exped", "mixed", "m_tr", "m_t", "y_mm", "y")}
        S.update(early.sems)
        block = ctx.enter_context(nc.Block())

        @block.sync
        def _(sp):
            sp.dma_start(bm[:], d["Bm5"]).then_inc(S["bm"], 16)
            sp.dma_start(bias[:], d["bias5"]).then_inc(S["bm"], 16)

        @block.tensor
        def _(pe):
            pe.wait_ge(S["split"], 2)
            for half in range(NH2):
                tok = slice(half * HALF, (half + 1) * HALF)
                for k in range(KC):
                    ins = split_matmul(nc, bank[2 + half][0:ER + E, :], (small_hi[:, k, :], small_lo[:, k, :]),
                                       (x_hi[:, k, tok], x_lo[:, k, tok]), k == 0, k == KC - 1)
                ins.then_inc(S["ra_mm"], 1)
            pe.wait_ge(S["ra_t"], 2)
            for t in range(NT):
                ins = nc.tensor.transpose(bank[0][:, t * (ER + E):(t + 1) * (ER + E)],
                                          ra_t[:, t * P:(t + 1) * P], ident[0:ER + E, 0:ER + E])
            ins.then_inc(S["ra_tr"], 1)
            pe.wait_ge(S["w_lo"], 1)
            pe.wait_ge(S["bm"], 32)

            def base(t):
                if t >= 4:
                    pe.wait_ge(S["y"], t - 3)
                for k in range(KC):
                    tok = slice(t * P, (t + 1) * P)
                    split_matmul(nc, bank[4 + t % 4][:], (x_hi[:, k, tok], x_lo[:, k, tok]),
                                 (w_hi[:, k, :], w_lo[:, k, :]), k == 0, False)

            def update(t):
                nc.tensor.matmul(bank[4 + t % 4][:], mixed_t[:, t * P:(t + 1) * P], bm[:], start=False,
                                 stop=True).then_inc(S["y_mm"], 1)

            for t in range(4):
                base(t)
            pe.wait_ge(S["mixed"], 1)
            for t in range(NT):
                ins = nc.tensor.transpose(bank[1 + t // 4][0:ER, (t % 4) * P:(t % 4 + 1) * P], ra[:, t, 0:ER],
                                          ident[:])
            ins.then_inc(S["m_tr"], 1)
            pe.wait_ge(S["m_t"], 2)
            for t in range(4):
                update(t)
            for t in range(4, NT):
                base(t)
                update(t)

        @block.scalar
        def _(act):
            for half in range(NH2):
                act.wait_ge(S["ra_mm"], half + 1)
                nc.scalar.activation(ra_t[:, half * HALF:(half + 1) * HALF], bank[2 + half][0:ER + E, :],
                                     ACT.Copy).then_inc(S["ra_t"], 1)
            act.wait_ge(S["ra_tr"], 1)
            nc.scalar.activation(ra[:].rearrange("p t n -> p (t n)"), bank[0][:, 0:NT * (ER + E)],
                                 ACT.Copy).then_inc(S["ra"], 1)
            act.wait_ge(S["v"], 2)
            nc.scalar.activation(g[:], g[:], ACT.Exp).then_inc(S["exped"], 1)
            act.wait_ge(S["m_tr"], 1)
            for i in range(2):
                nc.scalar.activation(mixed_t[:, i * HALF:(i + 1) * HALF], bank[1 + i][0:ER, :],
                                     ACT.Copy).then_inc(S["m_t"], 1)

        @block.vector
        def _(dve):
            logits = ra[:, :, ER:ER + E]
            dve.wait_ge(S["ra"], 1)
            nc.vector.tensor_reduce(top[:], logits, AX, ALU.max).then_inc(S["v"], 1)
            dve.wait_ge(S["v"], 1)
            nc.vector.tensor_tensor(g[:], logits, top[:].unsqueeze(2).to_broadcast([P, NT, E]),
                                    ALU.subtract).then_inc(S["v"], 1)
            dve.wait_ge(S["exped"], 1)
            nc.vector.tensor_reduce(den[:], g[:], AX, ALU.add).then_inc(S["v"], 1)
            dve.wait_ge(S["v"], 3)
            nc.vector.reciprocal(den[:], den[:]).then_inc(S["v"], 1)
            dve.wait_ge(S["v"], 4)
            nc.vector.tensor_tensor(g[:], g[:], den[:].unsqueeze(2).to_broadcast([P, NT, E]),
                                    ALU.mult).then_inc(S["v"], 1)
            dve.wait_ge(S["v"], 5)
            nc.vector.tensor_scalar(g[:], g[:], SCALE, None, ALU.mult).then_inc(S["v"], 1)
            dve.wait_ge(S["v"], 6)
            for e in range(E):
                r = ra[:, :, e * R:(e + 1) * R]
                ins = nc.vector.tensor_tensor(r, r, g[:, :, e:e + 1].to_broadcast([P, NT, R]), ALU.mult)
            ins.then_inc(S["mixed"], 1)
            dve.wait_ge(S["bm"], 32)
            for t in range(NT):
                dve.wait_ge(S["y_mm"], t + 1)
                nc.vector.tensor_tensor(branch[:, t, :], bank[4 + t % 4][:], bias[:], ALU.add).then_inc(
                    S["y"], 1)
                branch_stats(chip, dve, t, S["y"], t + 1)


def latent_attention_early(chip, scope):
    nc, d = chip.nc, chip.dram
    H, QL, L = 32, 192, 64
    wq1_hi = scope.enter_context(nc.sbuf_tensor("mla_w_query_1_hi", [P, H, 2 * L], FP32R))
    wq1_lo = scope.enter_context(nc.sbuf_tensor("mla_w_query_1_lo", [P, H, 2 * L], FP32R))
    wq2 = scope.enter_context(nc.sbuf_tensor("mla_w_query_2", [P, H, 2 * L], FP32R))
    wvo = scope.enter_context(nc.sbuf_tensor("mla_w_value_out", [P, H // 2, C], FP32))
    factors = scope.enter_context(ExitStack())
    up_t = factors.enter_context(nc.sbuf_tensor("mla_w_q_up_t", [P, H, QL], FP32))
    uk = factors.enter_context(nc.sbuf_tensor("mla_w_uk", [P, H, L], FP32))
    S = {n: chip.sem("mlw_" + n) for n in ("up0", "up1")}

    def sync(sp):
        for i in range(2):
            h = slice(i * H // 2, (i + 1) * H // 2)
            sp.dma_start(up_t[:, h], d["w_q_up_nope_t6"][:, h]).then_inc(S[f"up{i}"], 16)
            sp.dma_start(uk[:, h], d["w_uk6"][:, h]).then_inc(S[f"up{i}"], 16)

    return Early(sync, no_part, no_part, S, (wq1_hi, wq1_lo, wq2, wvo, factors, up_t, uk))


def latent_attention(chip, early):
    nc, d, bank = chip.nc, chip.dram, chip.bank
    x_hi, x_lo, branch, ident = chip.x_hi, chip.x_lo, chip.branch, chip.ident
    H, QL, L, DN, DR = 32, 192, 64, 128, 64
    QL2 = QL - P
    SCALE = 1.0 / math.sqrt(DN + DR)
    W = P + SEQ
    PAIRS = H // 2
    RING = 4
    BEHIND = 3
    with ExitStack() as keep:
        wq1_hi, wq1_lo, wq2, wvo, factors, up_t, uk = early.tensors

        with ExitStack() as ctx:
            def sb(name, shape, dt=FP32):
                return ctx.enter_context(nc.sbuf_tensor(f"mla_{name}", shape, dt))

            uv = sb("w_uv", [P, H, L])
            HS = 4
            wout = sb("w_out", [P, 2, HS, C])
            S = {n: chip.layer_sem(keep, "mlw_" + n) for n in (
                "uv", "rope", "rope_hi", "rope_lo", "out0", "out1", "a_mm", "b_mm", "a_hi", "a_lo",
                "b_hi", "b_lo", "vo_mm", "vo")}
            S.update(early.sems)
            block = ctx.enter_context(nc.Block())

            def by_head(ap):
                return ap.rearrange("p (h l) -> p h l", l=L)

            @block.sync
            def _(sp):
                sp.dma_start(uv[:], d["w_uv6"]).then_inc(S["uv"], 16)
                for c in range(H // HS):
                    if c == 2:
                        sp.wait_ge(S["a_mm"], H // 8)
                        sp.wait_ge(S["b_mm"], H // 8)
                        sp.dma_start(uk[:], d["w_q_up_rope_low6"]).then_inc(S["rope"], 16)
                    if c == 4:
                        sp.wait_ge(S["rope_lo"], 1)
                        sp.dma_start(uk[0:QL2], d["w_q_up_rope_high6"]).then_inc(S["rope"], 16)
                        sp.dma_start(uk[QL2:P], d["w_q_up_rope_high6"]).then_inc(S["rope"], 16)
                    if c >= 2:
                        sp.wait_ge(S["vo_mm"], HS * (c - 1) // 2)
                    sp.dma_start(wout[:, c % 2], d["w_out6"][:, c * HS:(c + 1) * HS]).then_inc(
                        S[f"out{c % 2}"], 16)

            @block.tensor
            def _(pe):
                for i in range(H // 8):
                    if i % 2 == 0:
                        pe.wait_ge(S[f"up{i // 2}"], 32)
                    if i >= 2:
                        pe.wait_ge(S["a_lo"], i - 1)
                    for h in range(8 * i, 8 * i + 8):
                        ins = nc.tensor.matmul(bank[i % 2][:, (h % 8) * L:(h % 8 + 1) * L], up_t[:, h, 0:P],
                                               uk[:, h, :], start=True, stop=True)
                    ins.then_inc(S["a_mm"], 1)
                    if i >= 2:
                        pe.wait_ge(S["b_lo"], i - 1)
                    for h in range(8 * i, 8 * i + 8):
                        for r in range(2):
                            ins = nc.tensor.matmul(
                                bank[2 + i % 2][r * QL2:(r + 1) * QL2, (h % 8) * L:(h % 8 + 1) * L],
                                up_t[:, h, P:QL], uk[:, h, :], start=True, stop=True)
                    ins.then_inc(S["b_mm"], 1)
                pe.wait_ge(S["uv"], 16)
                for j in range(PAIRS):
                    c = j // (HS // 2)
                    if j % (HS // 2) == 0:
                        pe.wait_ge(S[f"out{c % 2}"], 16 * (c // 2 + 1))
                    if j >= 2:
                        pe.wait_ge(S["vo"], j - 1)
                    for e in range(2):
                        h = 2 * j + e
                        ins = nc.tensor.matmul(bank[4 + j % 2][L * e:L * (e + 1), :], uv[:, h, :],
                                               wout[:, c % 2, h % HS, :], start=True, stop=True)
                    ins.then_inc(S["vo_mm"], 1)

            @block.scalar
            def _(act):
                for i in range(H // 8):
                    act.wait_ge(S["a_mm"], i + 1)
                    nc.scalar.activation(wq1_hi[:, 8 * i:8 * i + 8, 0:L], by_head(bank[i % 2][:]),
                                         ACT.Copy).then_inc(S["a_hi"], 1)
                    act.wait_ge(S["b_mm"], i + 1)
                    nc.scalar.activation(wq2[:, 8 * i:8 * i + 8, 0:L], by_head(bank[2 + i % 2][:]),
                                         ACT.Copy).then_inc(S["b_hi"], 1)

            @block.vector
            def _(dve):
                for i in range(H // 8):
                    heads = slice(8 * i, 8 * i + 8)
                    dve.wait_ge(S["a_hi"], i + 1)
                    nc.vector.tensor_tensor(wq1_lo[:, heads, 0:L], by_head(bank[i % 2][:]),
                                            wq1_hi[:, heads, 0:L].bitcast(FP32), ALU.subtract).then_inc(
                        S["a_lo"], 1)
                    dve.wait_ge(S["b_hi"], i + 1)
                    nc.vector.tensor_tensor(wq2[QL2:P, heads, 0:L], by_head(bank[2 + i % 2][QL2:P, :]),
                                            wq2[QL2:P, heads, 0:L].bitcast(FP32), ALU.subtract).then_inc(
                        S["b_lo"], 1)
                for j in range(PAIRS):
                    dve.wait_ge(S["vo_mm"], j + 1)
                    nc.vector.tensor_copy(wvo[:, j, :], bank[4 + j % 2][:]).then_inc(S["vo"], 1)

            @block.gpsimd
            def _(pool):
                pool.wait_ge(S["rope"], 16)
                nc.gpsimd.tensor_copy(wq1_hi[:, :, L:2 * L], uk[:]).then_inc(S["rope_hi"], 1)
                pool.wait_ge(S["rope_hi"], 1)
                nc.gpsimd.tensor_tensor(wq1_lo[:, :, L:2 * L], uk[:], wq1_hi[:, :, L:2 * L].bitcast(FP32),
                                        ALU.subtract).then_inc(S["rope_lo"], 1)
                pool.wait_ge(S["rope"], 48)
                nc.gpsimd.tensor_copy(wq2[:, :, L:2 * L], uk[:]).then_inc(S["rope_hi"], 1)
                pool.wait_ge(S["rope_hi"], 2)
                nc.gpsimd.tensor_tensor(wq2[QL2:P, :, L:2 * L], uk[QL2:P],
                                        wq2[QL2:P, :, L:2 * L].bitcast(FP32), ALU.subtract).then_inc(
                    S["rope_lo"], 1)

        factors.close()

        with ExitStack() as ctx:
            def sb(name, shape, dt=FP32):
                return ctx.enter_context(nc.sbuf_tensor(f"mla_{name}", shape, dt))

            wd = sb("w_down", [P, KC, 2 * P + L + DR])
            wd_hi = sb("w_down_hi", [P, KC, 2 * P + L + DR], FP32R)
            wd_lo = sb("w_down_lo", [P, KC, 2 * P + L + DR], FP32R)
            cos = sb("cos", [P, SEQ])
            sin = sb("sin", [P, SEQ])
            mask = sb("causal", [P, W])
            cq1_hi = sb("query_latent_1_hi", [P, TOKENS], FP32R)
            cq1_lo = sb("query_latent_1_lo", [P, TOKENS], FP32R)
            cq2_hi = sb("query_latent_2_hi", [P, TOKENS], FP32R)
            cq2_lo = sb("query_latent_2_lo", [QL2, TOKENS], FP32R)
            ckv = sb("latent", [P, NT, L])
            k_t = sb("keys_t", [P, TOKENS])
            q_t = sb("queries_t", [P, 3, SEQ])
            rot = sb("rotated", [P, 2, SEQ])
            sc = sb("scores", [P, RING, W])
            nmax = sb("neg_max", [P, RING, 2])
            den = sb("denominators", [P, RING, 2])
            pt = sb("probs_t", [P, 2, W])
            o_t = sb("out_t", [P, 2, SEQ])
            UNITS = BATCHES * H
            S = {n: chip.layer_sem(keep, "mla_" + n) for n in (
                "wd", "wd_split", "tab", "c_mm", "c_hi", "c_lo", "kv_mm", "kv", "q_mm", "rot",
                "q_rot", "q_add", "s_mm",
                "biased", "maxed", "exped", "rden", "scaled", "scaled_1st", "p_tr",
                "p_copied", "pv", "o_copied", "y_mm", "y")}
            block = ctx.enter_context(nc.Block())

            KU = BATCHES

            @block.sync
            def _(sp):
                sp.dma_start(wd[:], d["w_down6"]).then_inc(S["wd"], 16)
                sp.dma_start(cos[L:P, :], d["cos6"]).then_inc(S["tab"], 16)
                sp.dma_start(sin[L:P, :], d["sin6"]).then_inc(S["tab"], 16)
                sp.dma_start(mask[:], d["causal6"]).then_inc(S["tab"], 16)

            def rope_target(i):
                if i < KU:
                    return k_t[:, i * SEQ:(i + 1) * SEQ]
                return q_t[:, (i - KU) % 3, :]

            @block.tensor
            def _(pe):
                pe.wait_ge(S["wd_split"], 2)
                for i in range(2 * NH2):
                    half, part = divmod(i, 2)
                    if i >= 2:
                        pe.wait_ge(S["c_lo"], i - 1)
                    for k in range(KC):
                        tok, cols = slice(half * HALF, (half + 1) * HALF), slice(part * P, (part + 1) * P)
                        ins = split_matmul(nc, bank[5 + i % 2][:], (wd_hi[:, k, cols], wd_lo[:, k, cols]),
                                           (x_hi[:, k, tok], x_lo[:, k, tok]), k == 0, k == KC - 1)
                    ins.then_inc(S["c_mm"], 1)

                def project(i):
                    if i >= 2:
                        pe.wait_ge(S["q_rot"], i - 1)
                    b = bank[i % 2][:, 0:SEQ]
                    if i < KU:
                        for k in range(KC):
                            tok = slice(i * SEQ, (i + 1) * SEQ)
                            ins = split_matmul(nc, b, (wd_hi[:, k, 2 * P:], wd_lo[:, k, 2 * P:]),
                                               (x_hi[:, k, tok], x_lo[:, k, tok]), k == 0, k == KC - 1)
                    else:
                        bt, h = divmod(i - KU, H)
                        tok = slice(bt * SEQ, (bt + 1) * SEQ)
                        if i == KU:
                            pe.wait_ge(S["c_lo"], 2 * NH2)
                        split_matmul(nc, b, (wq1_hi[:, h, :], wq1_lo[:, h, :]),
                                     (cq1_hi[:, tok], cq1_lo[:, tok]), True, False)
                        nc.tensor.matmul(b, wq2[:, h, :], cq2_hi[:, tok], start=False, stop=False)
                        ins = nc.tensor.matmul(b, wq2[0:QL2, h, :], cq2_lo[:, tok], start=False, stop=True)
                    ins.then_inc(S["q_mm"], 1)

                def scores(u):
                    bt = u // H
                    pe.wait_ge(S["q_add"], KU + u + 1)
                    pe.wait_ge(S["q_rot"], KU + u + 1)
                    if u >= 2:
                        pe.wait_ge(S["biased"], u - 1)
                    q, k = q_t[:, u % 3, :], k_t[:, bt * SEQ:(bt + 1) * SEQ]
                    nc.tensor.matmul(bank[2 + u % 2][:, 0:P], q[:, 0:P], k[:, 0:P], start=True, stop=True)
                    nc.tensor.matmul(bank[2 + u % 2][:, P:W], q[:, P:SEQ], k, start=True, stop=True).then_inc(
                        S["s_mm"], 1)

                def transposes(u):
                    pe.wait_ge(S["scaled_1st"], u + 1)
                    pe.wait_ge(S["scaled"], u + 1)
                    if u >= 1:
                        pe.wait_ge(S["p_copied"], u)
                    p = sc[:, u % RING, :]
                    nc.tensor.transpose(bank[4][:, 0:P], p[:, 0:P], ident[:])
                    nc.tensor.transpose(bank[4][:, P:2 * P], p[:, P:2 * P], ident[:])
                    nc.tensor.transpose(bank[4][:, 2 * P:W], p[:, 2 * P:W], ident[:]).then_inc(S["p_tr"], 1)

                def values(u):
                    bt, h = divmod(u, H)
                    pe.wait_ge(S["p_copied"], u + 1)
                    if u >= 1:
                        pe.wait_ge(S["o_copied"], u)
                    r = slice(L * (h % 2), L * (h % 2 + 1))
                    o = bank[5]
                    nc.tensor.matmul(o[r, 0:SEQ], ckv[:, 2 * bt, :], pt[:, u % 2, 0:SEQ], start=True, stop=False)
                    nc.tensor.matmul(o[r, P:SEQ], ckv[:, 2 * bt + 1, :], pt[:, u % 2, SEQ:W], start=False,
                                     stop=True).then_inc(S["pv"], 1)

                def result(j, t):
                    if t == 0:
                        pe.wait_ge(S["o_copied"], 2 * (j + 1))
                    bt, pair = divmod(j, PAIRS)
                    if pair == 0 and bt:
                        pe.wait_ge(S["y"], 2 * (bt - 1) + t + 1)
                    nc.tensor.matmul(bank[6 + t][:], o_t[:, j % 2, t * P:(t + 1) * P], wvo[:, pair, :],
                                     start=(pair == 0), stop=(pair == PAIRS - 1)).then_inc(S["y_mm"], 1)

                for i in range(KU + 2):
                    project(i)
                pe.wait_ge(S["q_rot"], KU)
                for t in range(NT):
                    ins = nc.tensor.transpose(bank[7][:, t * L:(t + 1) * L], k_t[0:L, t * P:(t + 1) * P],
                                              ident[0:L, 0:L])
                ins.then_inc(S["kv_mm"], 1)
                pe.wait_ge(S["kv"], 1)
                for u in range(UNITS + BEHIND + 3):
                    if u < UNITS:
                        scores(u)
                        if u + 2 < UNITS:
                            project(KU + u + 2)
                    if 0 <= u - BEHIND < UNITS:
                        transposes(u - BEHIND)
                    v = u - BEHIND - 1
                    if 0 <= v < UNITS:
                        values(v)
                    if v >= 2:
                        result(v // 2 - 1, v % 2)

            @block.scalar
            def _(act):
                for i in range(2 * NH2):
                    half, part = divmod(i, 2)
                    out = (cq2_hi if part else cq1_hi)[:, half * HALF:(half + 1) * HALF]
                    act.wait_ge(S["c_mm"], i + 1)
                    nc.scalar.activation(out, bank[5 + i % 2][:], ACT.Copy).then_inc(S["c_hi"], 1)

                def latent(i):
                    act.wait_ge(S["rot"], i + 1)
                    if i >= KU + 3:
                        act.wait_ge(S["s_mm"], i - KU - 2)
                    nc.scalar.activation(rope_target(i)[0:L, :], bank[i % 2][0:L, 0:SEQ], ACT.Copy).then_inc(
                        S["q_rot"], 1)

                def exp(u):
                    act.wait_ge(S["maxed"], u + 1)
                    for i, (lo, hi) in enumerate(((0, P), (P, W))):
                        ins = nc.scalar.activation(sc[:, u % RING, lo:hi], sc[:, u % RING, lo:hi], ACT.Exp,
                                                   bias=nmax[:, u % RING, i:i + 1],
                                                   accum_out=den[:, u % RING, i:i + 1])
                    ins.then_inc(S["exped"], 1)

                def copy_probs(u):
                    act.wait_ge(S["p_tr"], u + 1)
                    if u >= 2:
                        act.wait_ge(S["pv"], u - 1)
                    nc.scalar.activation(pt[:, u % 2, :], bank[4][:, 0:W], ACT.Copy).then_inc(S["p_copied"], 1)

                def copy_out(u):
                    bt, h = divmod(u, H)
                    r = slice(L * (h % 2), L * (h % 2 + 1))
                    act.wait_ge(S["pv"], u + 1)
                    if u // 2 >= 2:
                        act.wait_ge(S["y_mm"], 2 * (u // 2 - 1))
                    nc.scalar.activation(o_t[r, u // 2 % 2, :], bank[5][r, 0:SEQ],
                                         ACT.Copy).then_inc(S["o_copied"], 1)

                for i in range(KU + 2):
                    latent(i)
                act.wait_ge(S["kv_mm"], 1)
                nc.scalar.activation(ckv[:].rearrange("p t l -> p (t l)"), bank[7][:], ACT.Copy).then_inc(
                    S["kv"], 1)
                for u in range(UNITS + BEHIND + 1):
                    if 0 <= u - BEHIND < UNITS:
                        copy_probs(u - BEHIND)
                    if u < UNITS:
                        exp(u)
                    if u + 2 < UNITS:
                        latent(KU + u + 2)
                    if u >= BEHIND + 1:
                        copy_out(u - BEHIND - 1)

            @block.gpsimd
            def _(pool):
                def rotate(i):
                    pool.wait_ge(S["rot"], i + 1)
                    if i >= KU + 4:
                        pool.wait_ge(S["scaled"], i - KU - 3)
                    out = rope_target(i)[L:P, :]
                    nc.gpsimd.tensor_tensor(out, out, rot[L:P, i % 2, :], ALU.add).then_inc(S["q_add"], 1)

                def normalise(u):
                    pool.wait_ge(S["rden"], u + 1)
                    pool.wait_ge(S["q_add"], min(KU + u + 4, KU + UNITS))
                    p = sc[:, u % RING, P:W]
                    nc.gpsimd.tensor_scalar(p, p, den[:, u % RING, 1:2], None, ALU.mult).then_inc(
                        S["scaled"], 1)

                for i in range(KU + 2):
                    rotate(i)
                for u in range(UNITS + 1):
                    if u + 2 < UNITS:
                        rotate(KU + u + 2)
                    if u >= 1:
                        normalise(u - 1)

            @block.vector
            def _(dve):
                dve.wait_ge(S["wd"], 16)
                nc.vector.tensor_copy(wd_hi[:], wd[:]).then_inc(S["wd_split"], 1)
                dve.wait_ge(S["wd_split"], 1)
                nc.vector.tensor_tensor(wd_lo[:], wd[:], wd_hi[:].bitcast(FP32), ALU.subtract).then_inc(
                    S["wd_split"], 1)
                for i in range(2 * NH2):
                    half, part = divmod(i, 2)
                    rows, tok = QL2 if part else P, slice(half * HALF, (half + 1) * HALF)
                    dve.wait_ge(S["c_hi"], i + 1)
                    nc.vector.tensor_tensor((cq2_lo if part else cq1_lo)[:, tok], bank[5 + i % 2][0:rows, :],
                                            (cq2_hi if part else cq1_hi)[0:rows, tok].bitcast(FP32),
                                            ALU.subtract).then_inc(S["c_lo"], 1)
                dve.wait_ge(S["tab"], 48)

                def rotate(i):
                    b = bank[i % 2]
                    out = rope_target(i)
                    dve.wait_ge(S["q_mm"], i + 1)
                    if i >= KU + 3:
                        dve.wait_ge(S["s_mm"], i - KU - 2)
                    if i >= 2:
                        dve.wait_ge(S["q_add"], i - 1)
                    nc.vector.tensor_tensor(out[L:P, :], b[L:P, 0:SEQ], cos[L:P, :], ALU.mult)
                    nc.vector.tensor_tensor(rot[64:96, i % 2, :], b[96:128, 0:SEQ], sin[64:96, :], ALU.mult)
                    nc.vector.tensor_tensor(rot[96:128, i % 2, :], b[64:96, 0:SEQ], sin[96:128, :],
                                            ALU.mult).then_inc(S["rot"], 1)

                def bias_and_max(u):
                    s = sc[:, u % RING, :]
                    dve.wait_ge(S["s_mm"], u + 1)
                    if u >= RING:
                        dve.wait_ge(S["p_tr"], u - RING + 1)
                    nc.vector.scalar_tensor_tensor(out=s, in0=bank[2 + u % 2][:, 0:W], scalar=SCALE, in1=mask[:],
                                                   op0=ALU.mult, op1=ALU.add).then_inc(S["biased"], 1)
                    dve.wait_ge(S["biased"], u + 1)
                    for i, (lo, hi) in enumerate(((0, P), (P, W))):
                        ins = nc.vector.tensor_reduce(nmax[:, u % RING, i:i + 1], s[:, lo:hi], AX, ALU.max,
                                                      negate=True)
                    ins.then_inc(S["maxed"], 1)

                def normalise(u):
                    dve.wait_ge(S["exped"], u + 1)
                    nc.vector.reciprocal(den[:, u % RING, :], den[:, u % RING, :]).then_inc(S["rden"], 1)
                    dve.wait_ge(S["rden"], u + 1)
                    p = sc[:, u % RING, 0:P]
                    nc.vector.tensor_scalar(p, p, den[:, u % RING, 0:1], None, ALU.mult).then_inc(
                        S["scaled_1st"], 1)

                def copy_result(n):
                    if n:
                        branch_stats(chip, dve, n - 1, S["y"], n)
                    bt, t = divmod(n, 2)
                    dve.wait_ge(S["y_mm"], 2 * PAIRS * (bt + 1) + t - 1)
                    nc.vector.tensor_copy(branch[:, n, :], bank[6 + t][:]).then_inc(S["y"], 1)

                for i in range(KU + 2):
                    rotate(i)
                for u in range(UNITS + 1):
                    if u > H and (u - BEHIND - 2) % H < 2:
                        copy_result(2 * (u // H - 1) + (u - BEHIND - 2) % H)
                    if u < UNITS:
                        bias_and_max(u)
                        if u + 2 < UNITS:
                            rotate(KU + u + 2)
                    if u >= 1:
                        normalise(u - 1)
                copy_result(NT - 2)
                copy_result(NT - 1)
                branch_stats(chip, dve, NT - 1, S["y"], NT)


def moe_ffn(chip):
    nc, d, bank = chip.nc, chip.dram, chip.bank
    x_hi, x_lo, branch, ident = chip.x_hi, chip.x_lo, chip.branch, chip.ident
    E, SC = 16, 4
    U = E + SC
    UNITS = NH2 * U
    GU = KC * 2 * P
    WN = GU + C
    STAGE, RING, HR = 2, 5, 4
    LAG = 3
    with ExitStack() as ctx:
        def sb(name, shape, dt=FP32):
            return ctx.enter_context(nc.sbuf_tensor(f"moe_{name}", shape, dt))

        gw = sb("gate_w", [P, KC, E])
        gw_hi = sb("gate_w_hi", [P, KC, E], FP32R)
        gw_lo = sb("gate_w_lo", [P, KC, E], FP32R)
        stage = sb("weights", [P, STAGE, WN])
        w_hi = sb("w_hi", [P, RING, WN], FP32R)
        w_lo = sb("w_lo", [P, RING, WN], FP32R)
        sel_in = sb("row_select_in", [E, E, P])
        sel = sb("row_select", [E, E, P], FP32R)
        iota = sb("iota", [P, NT, E])
        lg_t = sb("logits_t", [E, TOKENS])
        p = sb("probs", [P, NT, E])
        r1 = sb("rank1", [P, NT, E])
        r2 = sb("rank2", [P, NT, E])
        t1 = sb("top1", [P, NT])
        t2 = sb("top2", [P, NT])
        ix = sb("index", [P, NT])
        comb_hi = sb("combine_t_hi", [E, TOKENS], FP32R)
        comb_lo = sb("combine_t_lo", [E, TOKENS], FP32R)
        act_s = sb("silu", [P, 2, HALF])
        mul = sb("product", [P, 2, HALF])
        h = sb("hidden", [P, 2, HALF])
        h_hi = sb("hidden_hi", [P, HR, HALF], FP32R)
        h_lo = sb("hidden_lo", [P, HR, HALF], FP32R)
        S = {n: chip.layer_sem(ctx, "moe_" + n) for n in (
            "in", "in2", "gw", "sel", "w0", "w1", "w_hi", "w_lo", "l_mm", "lg_t", "l_tr", "v", "exped", "comb", "c_tr",
            "c_hi", "c_lo", "g_mm", "u_mm", "b_mm", "silu", "prod", "hidden", "h_hi", "h_lo", "down", "y_mm", "y")}
        block = ctx.enter_context(nc.Block())


        def tok(n):
            return slice(n // U * HALF, (n // U + 1) * HALF)

        @block.sync
        def _(sp):
            sp.dma_start(gw[:], d["gate_w7"]).then_inc(S["in"], 16)
            for n in range(UNITS):
                if n >= STAGE:
                    sp.wait_ge(S["w_lo"], n - STAGE + 1)
                sp.dma_start(stage[:, n % STAGE], d["w7"][n % U]).then_inc(S[f"w{n % STAGE}"], 16)
                if n == 1:
                    sp.dma_start(iota[:], d["iota7"]).then_inc(S["in2"], 16)
                    sp.dma_start(sel_in[:], d["expert_select7"]).then_inc(S["in2"], 16)

        @block.gpsimd
        def _(pool):
            def weights_low(n):
                pool.wait_ge(S["w_hi"], n + 1)
                nc.gpsimd.tensor_tensor(w_lo[:, n % RING], stage[:, n % STAGE], w_hi[:, n % RING].bitcast(FP32),
                                        ALU.subtract).then_inc(S["w_lo"], 1)

            weights_low(0)
            weights_low(1)
            for n in range(UNITS):
                if n + 2 < UNITS:
                    weights_low(n + 2)
                pool.wait_ge(S["h_hi"], n + 1)
                nc.gpsimd.tensor_tensor(h_lo[:, n % HR, :], h[:, n % 2, :], h_hi[:, n % HR, :].bitcast(FP32),
                                        ALU.subtract).then_inc(S["h_lo"], 1)

        @block.tensor
        def _(pe):
            pe.wait_ge(S["gw"], 2)
            for half in range(NH2):
                t = slice(half * HALF, (half + 1) * HALF)
                for k in range(KC):
                    ins = split_matmul(nc, bank[4 + half][0:E, :], (gw_hi[:, k, :], gw_lo[:, k, :]),
                                       (x_hi[:, k, t], x_lo[:, k, t]), k == 0, k == KC - 1)
                ins.then_inc(S["l_mm"], 1)
            pe.wait_ge(S["lg_t"], NH2)
            for t in range(NT):
                ins = nc.tensor.transpose(bank[6][:, t * E:(t + 1) * E], lg_t[:, t * P:(t + 1) * P],
                                          ident[0:E, 0:E])
            ins.then_inc(S["l_tr"], 1)

            def gate_up(n):
                pe.wait_ge(S["w_lo"], n + 1)
                if n >= 2:
                    pe.wait_ge(S["hidden"], n - 1)
                for j, name in enumerate(("g_mm", "u_mm")):
                    for k in range(KC):
                        at = k * 2 * P + j * P
                        ins = split_matmul(nc, bank[2 * (n % 2) + j][:],
                                           (w_hi[:, n % RING, at:at + P], w_lo[:, n % RING, at:at + P]),
                                           (x_hi[:, k, tok(n)], x_lo[:, k, tok(n)]), k == 0, k == KC - 1)
                    ins.then_inc(S[name], 1)

            def token_weights(n):
                pe.wait_ge(S["silu"], n + 1)
                pe.wait_ge(S["sel"], 1)
                pe.wait_ge(S["c_lo"], NH2)
                split_matmul(nc, bank[2 * (n % 2)][:], (sel[:, n % U - SC, :],),
                             (comb_hi[:, tok(n)], comb_lo[:, tok(n)]), True, True).then_inc(S["b_mm"], 1)

            def down(n):
                pe.wait_ge(S["h_lo"], n + 1)
                for j in range(4):
                    if n % U == 0 and n:
                        pe.wait_ge(S["y"], j + 1)
                    a = (slice(0, P), n % HR, slice(j * P, (j + 1) * P))
                    ins = split_matmul(nc, bank[4 + j][:], (h_hi[a], h_lo[a]),
                                       (w_hi[:, n % RING, GU:], w_lo[:, n % RING, GU:]), n % U == 0,
                                       n % U == U - 1)
                    if n % U == U - 1:
                        ins.then_inc(S["y_mm"], 1)
                if n % U < U - 1:
                    ins.then_inc(S["down"], 1)
                else:
                    pe.wait_ge(S["y_mm"], 4 * (n // U + 1))
                    pe.sem_inc(S["down"], 1)

            for n in range(UNITS + LAG):
                if n < UNITS:
                    gate_up(n)
                if n == LAG - 1:
                    pe.wait_ge(S["comb"], 1)
                    for t in range(NT):
                        ins = nc.tensor.transpose(bank[4 + t // 4][0:E, (t % 4) * P:(t % 4 + 1) * P],
                                                  p[:, t, :], ident[:])
                    ins.then_inc(S["c_tr"], 1)
                if 1 <= n <= UNITS and (n - 1) % U >= SC:
                    token_weights(n - 1)
                if n >= LAG:
                    if n == LAG:
                        pe.wait_ge(S["c_lo"], NH2)
                    down(n - LAG)

        @block.scalar
        def _(act):
            for half in range(NH2):
                act.wait_ge(S["l_mm"], half + 1)
                nc.scalar.activation(lg_t[:, half * HALF:(half + 1) * HALF], bank[4 + half][0:E, :],
                                     ACT.Copy).then_inc(S["lg_t"], 1)
            act.wait_ge(S["v"], 2)
            nc.scalar.activation(p[:], p[:], ACT.Exp).then_inc(S["exped"], 1)

            def silu(n):
                act.wait_ge(S["g_mm"], n + 1)
                if n >= 2:
                    act.wait_ge(S["prod"], n - 1)
                nc.scalar.activation(act_s[:, n % 2, :], bank[2 * (n % 2)][:], ACT.Silu).then_inc(S["silu"], 1)

            for n in range(UNITS + 1):
                if n < UNITS:
                    silu(n)
                if n == LAG - 1:
                    act.wait_ge(S["c_tr"], 1)
                    for i in range(NH2):
                        nc.scalar.activation(comb_hi[:, i * HALF:(i + 1) * HALF], bank[4 + i][0:E, :],
                                             ACT.Copy).then_inc(S["c_hi"], 1)
                if n >= 1:
                    m = n - 1
                    act.wait_ge(S["hidden"], m + 1)
                    if m >= HR:
                        act.wait_ge(S["down"], m - HR + 1)
                    nc.scalar.activation(h_hi[:, m % HR, :], h[:, m % 2, :], ACT.Copy).then_inc(S["h_hi"], 1)
                if n == U + LAG - 1 or n == UNITS:
                    half = n // U - 1
                    for j in range(4):
                        act.wait_ge(S["y_mm"], 4 * half + j + 1)
                        nc.scalar.activation(branch[:, 4 * half + j, :], bank[4 + j][:], ACT.Copy).then_inc(
                            S["y"], 1)

        @block.vector
        def _(dve):
            v = [0]

            def chain(ins):
                v[0] += 1
                ins.then_inc(S["v"], 1)
                dve.wait_ge(S["v"], v[0])

            def wide(x):
                return x[:].unsqueeze(2).to_broadcast([P, NT, E])

            def weights_high(n):
                dve.wait_ge(S[f"w{n % STAGE}"], 16 * (n // STAGE + 1))
                if n >= RING:
                    dve.wait_ge(S["down"], n - RING + 1)
                nc.vector.tensor_copy(w_hi[:, n % RING], stage[:, n % STAGE]).then_inc(S["w_hi"], 1)

            tt, red = nc.vector.tensor_tensor, nc.vector.tensor_reduce
            dve.wait_ge(S["in"], 16)
            nc.vector.tensor_copy(gw_hi[:], gw[:]).then_inc(S["gw"], 1)
            dve.wait_ge(S["gw"], 1)
            tt(gw_lo[:], gw[:], gw_hi[:].bitcast(FP32), ALU.subtract).then_inc(S["gw"], 1)
            weights_high(0)
            weights_high(1)
            logits = bank[6][:, 0:NT * E].rearrange("p (t e) -> p t e", e=E)
            dve.wait_ge(S["l_tr"], 1)
            chain(red(t1[:], logits, AX, ALU.max))
            chain(tt(p[:], logits, wide(t1), ALU.subtract))
            dve.wait_ge(S["exped"], 1)
            chain(red(t1[:], p[:], AX, ALU.add))
            chain(nc.vector.reciprocal(t1[:], t1[:]))
            chain(tt(p[:], p[:], wide(t1), ALU.mult))
            dve.wait_ge(S["in2"], 32)
            for top, rank in ((t1, r1), (t2, r2)):
                chain(red(top[:], p[:], AX, ALU.max))
                chain(tt(rank[:], p[:], wide(top), ALU.is_equal))
                chain(nc.vector.scalar_tensor_tensor(out=rank[:], in0=rank[:], scalar=-100.0, in1=iota[:],
                                                     op0=ALU.mult, op1=ALU.add))
                chain(red(ix[:], rank[:], AX, ALU.min))
                chain(tt(rank[:], rank[:], wide(ix), ALU.is_equal))
                if top is t1:
                    chain(nc.vector.scalar_tensor_tensor(out=p[:], in0=rank[:], scalar=-4.0, in1=p[:],
                                                         op0=ALU.mult, op1=ALU.add))
            chain(tt(ix[:], t1[:], t2[:], ALU.add))
            chain(nc.vector.reciprocal(ix[:], ix[:]))
            chain(tt(t1[:], t1[:], ix[:], ALU.mult))
            chain(tt(t2[:], t2[:], ix[:], ALU.mult))
            chain(tt(r1[:], r1[:], wide(t1), ALU.mult))
            chain(tt(r2[:], r2[:], wide(t2), ALU.mult))
            tt(p[:], r1[:], r2[:], ALU.add).then_inc(S["comb"], 1)
            nc.vector.tensor_copy(sel[:], sel_in[:]).then_inc(S["sel"], 1)
            routed = 0
            for n in range(UNITS):
                if n + 2 < UNITS:
                    weights_high(n + 2)
                if n == LAG - 1:
                    for i in range(NH2):
                        t = slice(i * HALF, (i + 1) * HALF)
                        dve.wait_ge(S["c_hi"], i + 1)
                        tt(comb_lo[:, t], bank[4 + i][0:E, :], comb_hi[:, t].bitcast(FP32),
                           ALU.subtract).then_inc(S["c_lo"], 1)
                dve.wait_ge(S["silu"], n + 1)
                dve.wait_ge(S["u_mm"], n + 1)
                if n >= 2:
                    dve.wait_ge(S["h_lo"], n - 1)
                if n % U < SC:
                    tt(h[:, n % 2, :], act_s[:, n % 2, :], bank[2 * (n % 2) + 1][:], ALU.mult).then_inc(
                        S["hidden"], 1)
                    dve.wait_ge(S["hidden"], n + 1)
                    dve.sem_inc(S["prod"], 1)
                else:
                    tt(mul[:, n % 2, :], act_s[:, n % 2, :], bank[2 * (n % 2) + 1][:], ALU.mult).then_inc(
                        S["prod"], 1)
                    dve.wait_ge(S["prod"], n + 1)
                    dve.wait_ge(S["b_mm"], routed + 1)
                    tt(h[:, n % 2, :], mul[:, n % 2, :], bank[2 * (n % 2)][:], ALU.mult).then_inc(
                        S["hidden"], 1)
                    routed += 1
            for t in range(NT):
                branch_stats(chip, dve, t, S["y"], t + 1)


LAYER_BUILDERS = [(gqa_attention, None), (int8_ffn, int8_ffn_early), (selective_scan, None),
                  (table_linear, table_linear_early), (head_mixer, head_mixer_early), (routed_lora, routed_lora_early),
                  (latent_attention, latent_attention_early), (moe_ffn, None)]
LAST_LAYERS = 8


def sandwich(nc, dram):
    with ExitStack() as ctx:
        chip = Chip(nc, ctx, dram)
        for n, (layer, begin) in enumerate(LAYER_BUILDERS[:LAST_LAYERS]):
            if n == 1:
                chip.place_stream()
            with ExitStack() as scope:
                if begin:
                    early = begin(chip, scope)
                    add_and_norm(chip, early)
                    layer(chip, early)
                else:
                    add_and_norm(chip)
                    layer(chip)
        if LAST_LAYERS == 1:
            chip.place_stream()
        add_and_norm(chip)


def _chunks(w):
    k, n = w.shape
    return np.ascontiguousarray(w.reshape(k // P, P, n).transpose(1, 0, 2))


def _layout(a):
    out = {}
    out["x"] = a["L0_attn_x"].reshape(NT, P, C)
    out["ident"] = np.eye(P, dtype=np.float32)
    wq, wk, wv, wo = (_chunks(a["L0_attn_W" + n].T) for n in "qkvo")
    q0 = wq.reshape(P, KC, 8, 512).transpose(2, 0, 1, 3).reshape(8, P, -1)
    kv0 = np.concatenate([wk.reshape(P, KC, 8, P), wv.reshape(P, KC, 8, P)], -1)
    out["Wqkv0"] = np.concatenate([q0, kv0.transpose(2, 0, 1, 3).reshape(8, P, -1)], -1)
    out["Wo0"] = wo.reshape(P, 8, 4 * C).transpose(1, 0, 2)
    out["qk_norm_w"] = np.stack([a["L0_attn_q_norm_w"], a["L0_attn_k_norm_w"]], 1)
    i, j = np.arange(P)[:, None], np.arange(SEQ)[None]
    rel = np.concatenate([j[:, :P] - i, j - i - P], 1).astype(np.float32)
    out["alibi_rel"] = np.where(rel > 0, np.float32(-1e33), rel)
    def pad_rows(w, n):
        return np.concatenate([w, np.zeros((n - w.shape[0],) + w.shape[1:], w.dtype)])
    out["gate1"] = _chunks(a["L0_ffn_gate_wq"].T)
    out["up1"] = _chunks(a["L0_ffn_up_wq"].T)
    out["down1"] = _chunks(pad_rows(a["L0_ffn_down_wq"].T, 11 * P))
    out["scales1"] = np.stack([pad_rows(a[f"L0_ffn_{n}_scale"], 11 * P).reshape(11, P).T
                               for n in ("gate", "up")], 1)
    out["down_scale1"] = np.broadcast_to(a["L0_ffn_down_scale"], (P, C))
    out["x_proj2"] = _chunks(a["L1_attn_x_proj_w"].T)
    out["dt_proj2"] = a["L1_attn_dt_proj_w"].T
    out["dt_bias2"] = a["L1_attn_dt_proj_b"].reshape(KC, P).T
    out["a_log2"] = _chunks(a["L1_attn_A_log"])
    out["d2"] = a["L1_attn_D"].reshape(KC, P).T
    row = np.zeros((48, 32, P), np.float32)
    row[np.arange(16, 48), np.arange(32)] = 1
    out["row_select2"] = row
    q = a["L1_ffn_qweight"][:4]
    out["planes3"] = q.reshape(4, KC, P, 16).transpose(2, 0, 1, 3).reshape(P, 4, KC * 16)
    out["lut3"] = _chunks(a["L1_ffn_lut4"])
    out["bias3"] = np.broadcast_to(a["L1_ffn_bias"], (P, C))
    out["Wqkv4"] = np.stack([_chunks(a[f"L2_attn_W{n}"].T) for n in "qkv"], 1)
    out["Wo4"] = _chunks(a["L2_attn_Wo"].T)
    out["bias4"] = np.stack([a[f"L2_attn_b{n}"] for n in "qkvo"])[None]
    lora_a = a["L2_ffn_A"].reshape(32, C)
    out["small5"] = _chunks(np.concatenate([lora_a, a["L2_ffn_Wr"]]).T)
    out["W5"] = _chunks(a["L2_ffn_W"].T)
    out["Bm5"] = a["L2_ffn_Bm"].transpose(0, 2, 1).reshape(32, C)
    out["bias5"] = np.broadcast_to(a["L2_ffn_b"], (P, C))
    out["w_q_up_nope_t6"] = a["L3_attn_w_q_up_nope"].reshape(192, 32, P).transpose(2, 1, 0)
    out["w_uk6"] = a["L3_attn_w_uk"].reshape(32, P, 64).transpose(1, 0, 2)
    out["w_uv6"] = a["L3_attn_w_uv"].reshape(32, P, 64).transpose(1, 0, 2)
    out["w_out6"] = a["L3_attn_w_out"].reshape(32, P, C).transpose(1, 0, 2)
    rope = a["L3_attn_w_q_up_rope"].reshape(192, 32, 64)
    out["w_q_up_rope_low6"], out["w_q_up_rope_high6"] = rope[:P], rope[P:]
    out["w_down6"] = _chunks(np.concatenate(
        [a["L3_attn_w_q_down"], a["L3_attn_w_q_down"][:, P:], a["L3_attn_w_kv_down"], a["L3_attn_w_k_rope"]], 1))
    f32 = np.float32
    freqs = f32(1) / np.power(f32(10000.0), np.arange(0, 64, 2, dtype=f32) / f32(64))
    ramp = np.clip((f32(2 * np.pi) / freqs / f32(4096.0) - f32(1)) / f32(31.0), f32(0), f32(1))
    inv = (freqs / (f32(1) - ramp + ramp * f32(40.0))).astype(f32)
    ang = inv[:, None] * np.arange(SEQ, dtype=f32)[None]
    out["cos6"] = np.concatenate([np.cos(ang)] * 2).astype(f32)
    out["sin6"] = np.concatenate([-np.sin(ang), np.sin(ang)]).astype(f32)
    out["causal6"] = np.where(rel > 0, f32(-1e30), f32(0))
    out["gate_w7"] = _chunks(a["L3_ffn_gate_w"].T)
    gu = a["L3_ffn_w_gate_up"].transpose(0, 2, 1).reshape(16, KC, P, 256)
    sg = a["L3_ffn_shared_w_gate_up"].T.reshape(KC, P, 2, 4, P).transpose(3, 0, 1, 2, 4).reshape(4, KC, P, 256)
    gu = np.concatenate([sg, gu]).transpose(0, 2, 1, 3).reshape(20, P, -1)
    down = np.concatenate([a["L3_ffn_shared_w_down"].T.reshape(4, P, C), a["L3_ffn_w_down"].transpose(0, 2, 1)])
    out["w7"] = np.concatenate([gu, down], 2)
    row = np.zeros((16, 16, P), np.float32)
    row[np.arange(16), np.arange(16)] = 1
    out["expert_select7"] = row
    out["iota7"] = np.broadcast_to(np.arange(16, dtype=np.float32), (P, NT, 16))
    return {k: np.ascontiguousarray(v) for k, v in out.items()}


def kernel(**inputs):
    import concourse.bacc as bacc
    from concourse.bass_utils import run_bass_kernel_spmd

    nc = bacc.Bacc("TRN2", target_bir_lowering=False, num_devices=1)
    arrays = _layout({k: np.asarray(v) for k, v in inputs.items()})
    dram = {k: nc.dram_tensor("in_" + k, v.shape, mybir.dt.from_np(v.dtype), kind="ExternalInput").ap()
            for k, v in arrays.items()}
    dram["out"] = nc.dram_tensor("out_x", (NT, P, C), FP32, kind="ExternalOutput").ap()
    sandwich(nc, dram)
    r = run_bass_kernel_spmd(nc, [{"in_" + k: v for k, v in arrays.items()}], core_ids=[0])
    return r.results[0]["out_x"].reshape(BATCHES, SEQ, C)
```
